# Optimizing a Trainium2 kernel written in Bass

```python
import numpy as np
import jax
import jax.numpy as jnp

def _softmax(x, axis=-1):
    return jax.nn.softmax(x, axis=axis)

def _gelu(x):
    return jax.nn.gelu(x, approximate=True)

def _silu(x):
    return jax.nn.silu(x)

def _sigmoid(x):
    return jax.nn.sigmoid(x)

def _layernorm(x, axis=-1, eps=1e-05):
    m = jnp.mean(x, axis=axis, keepdims=True)
    v = jnp.var(x, axis=axis, keepdims=True)
    return (x - m) / jnp.sqrt(v + eps)

def _scatter_add(tgt, idx, src, axis=0):
    return tgt.at[idx].add(src)

def _segment_sum(src, seg, n):
    return jax.ops.segment_sum(src, seg, n)
kernel_name = 'mk_sandwich_d1_jaxref_r4_ef8eb2'

def setup_inputs(seed: int=0):
    np.random.seed(seed)
    _w = jnp.asarray

    def _L0_attn_setup():
        import jax, jax.numpy as jnp
        import numpy as np
        D_MODEL = 256
        D_STATE = 16
        D_CONV = 4
        EXPAND = 2
        D_INNER = EXPAND * D_MODEL
        DT_RANK = D_MODEL // 16
        BATCH, SEQ = (8, 512)
        EPS = 1e-12

        def _layernorm(x, g, b):
            m = x.mean(-1, keepdims=True)
            v = ((x - m) ** 2).mean(-1, keepdims=True)
            return (x - m) / jnp.sqrt(v + EPS) * g + b

        def _l2norm(x, axis):
            n = jnp.sqrt((x * x).sum(axis, keepdims=True))
            return x / jnp.maximum(n, EPS)

        def _mamba(x, in_proj_w, conv_w, conv_b, x_proj_w, dt_proj_w, dt_proj_b, A_log, D_skip, out_proj_w):
            B, L, _ = x.shape
            xz = x @ in_proj_w.T
            u, res = jnp.split(xz, 2, axis=-1)
            xp = jnp.pad(u, ((0, 0), (D_CONV - 1, 0), (0, 0)))
            conv = conv_b + sum((xp[:, k:k + L, :] * conv_w[:, k] for k in range(D_CONV)))
            u = jax.nn.silu(conv)
            x_dbl = u @ x_proj_w.T
            dt, Bm, C = jnp.split(x_dbl, [DT_RANK, DT_RANK + D_STATE], axis=-1)
            delta = jax.nn.softplus(dt @ dt_proj_w.T + dt_proj_b)
            A = -jnp.exp(A_log)

            def step(h, t):
                delta_t, B_t, C_t, u_t = t
                dA = jnp.exp(delta_t[..., None] * A)
                h = dA * h + delta_t[..., None] * B_t[:, None, :] * u_t[..., None]
                y = jnp.einsum('bdn,bn->bd', h, C_t)
                return (h, y)
            xs = (jnp.swapaxes(delta, 0, 1), jnp.swapaxes(Bm, 0, 1), jnp.swapaxes(C, 0, 1), jnp.swapaxes(u, 0, 1))
            h0 = jnp.zeros((B, D_INNER, D_STATE), x.dtype)
            _, ys = jax.lax.scan(step, h0, xs)
            y = jnp.swapaxes(ys, 0, 1) + u * D_skip
            y = y * jax.nn.silu(res)
            return y @ out_proj_w.T

        def _forward(input_tensor, in_proj_w, conv_w, conv_b, x_proj_w, dt_proj_w, dt_proj_b, A_log, D_skip, out_proj_w, ln0_g, ln0_b, q_w, q_b, k_w, k_b, w_g, proj_w, proj_b, fl_w, fl_b, lni_g, lni_b, ln1_g, ln1_b, d1_w, d1_b, d2_w, d2_b, ln2_g, ln2_b):
            m = _mamba(input_tensor, in_proj_w, conv_w, conv_b, x_proj_w, dt_proj_w, dt_proj_b, A_log, D_skip, out_proj_w)
            h = _layernorm(m + input_tensor, ln0_g, ln0_b)
            q = jax.nn.gelu(_l2norm(h @ q_w.T + q_b, -1), approximate=False)
            k = _l2norm(h @ k_w.T + k_b, -1)
            qw = q @ w_g * D_MODEL ** (-0.5)
            Aw = _l2norm(qw, 1)
            G = (Aw * q).sum(1)
            hs = G[:, None, :] * k @ proj_w.T + proj_b
            hs = hs * _layernorm(h, lni_g, lni_b) @ fl_w.T + fl_b
            h2 = _layernorm(hs + h, ln1_g, ln1_b)
            f = jax.nn.gelu(h2 @ d1_w.T + d1_b, approximate=False) @ d2_w.T + d2_b
            return _layernorm(f + h2, ln2_g, ln2_b)
        key = jax.random.key(seed)
        ks = iter(jax.random.split(key, 40))

        def p(shape, scale=0.02):
            return jax.random.normal(next(ks), shape, jnp.float32) * scale
        inp = {}
        inp['input_tensor'] = jax.random.normal(next(ks), (BATCH, SEQ, D_MODEL), jnp.float32)
        inp['in_proj_w'] = p((2 * D_INNER, D_MODEL))
        inp['conv_w'] = p((D_INNER, D_CONV), 0.1)
        inp['conv_b'] = jnp.zeros((D_INNER,), jnp.float32)
        inp['x_proj_w'] = p((DT_RANK + 2 * D_STATE, D_INNER))
        inp['dt_proj_w'] = p((D_INNER, DT_RANK), 0.1)
        inp['dt_proj_b'] = jnp.full((D_INNER,), -2.0, jnp.float32)
        inp['A_log'] = jnp.broadcast_to(jnp.log(jnp.arange(1, D_STATE + 1, dtype=jnp.float32)), (D_INNER, D_STATE)).copy()
        inp['D_skip'] = jnp.ones((D_INNER,), jnp.float32)
        inp['out_proj_w'] = p((D_MODEL, D_INNER))
        inp['ln0_g'] = jnp.ones((D_MODEL,), jnp.float32)
        inp['ln0_b'] = jnp.zeros((D_MODEL,), jnp.float32)
        inp['q_w'] = p((D_MODEL, D_MODEL))
        inp['q_b'] = jnp.zeros((D_MODEL,), jnp.float32)
        inp['k_w'] = p((D_MODEL, D_MODEL))
        inp['k_b'] = jnp.zeros((D_MODEL,), jnp.float32)
        inp['w_g'] = p((D_MODEL, 1), 1.0)
        inp['proj_w'] = p((D_MODEL, D_MODEL))
        inp['proj_b'] = jnp.zeros((D_MODEL,), jnp.float32)
        inp['fl_w'] = p((D_MODEL, D_MODEL))
        inp['fl_b'] = jnp.zeros((D_MODEL,), jnp.float32)
        inp['lni_g'] = jnp.ones((D_MODEL,), jnp.float32)
        inp['lni_b'] = jnp.zeros((D_MODEL,), jnp.float32)
        inp['ln1_g'] = jnp.ones((D_MODEL,), jnp.float32)
        inp['ln1_b'] = jnp.zeros((D_MODEL,), jnp.float32)
        inp['d1_w'] = p((4 * D_MODEL, D_MODEL))
        inp['d1_b'] = jnp.zeros((4 * D_MODEL,), jnp.float32)
        inp['d2_w'] = p((D_MODEL, 4 * D_MODEL))
        inp['d2_b'] = jnp.zeros((D_MODEL,), jnp.float32)
        inp['ln2_g'] = jnp.ones((D_MODEL,), jnp.float32)
        inp['ln2_b'] = jnp.zeros((D_MODEL,), jnp.float32)
        return inp
    _L0_attn_in = _L0_attn_setup()

    def _L0_ffn_setup():
        import jax, jax.numpy as jnp
        import numpy as np
        import math
        B, S, H = (8, 1024, 256)
        E, I, K = (8, 512, 2)
        CAP_FACTOR = 1.0

        def _router(x, expert_embeddings):
            dot = jnp.einsum('bsh,eh->bse', x, expert_embeddings)
            n = dot.shape[0] * dot.shape[1]
            dot2 = dot.reshape(n, E)
            vals, idx = jax.lax.top_k(dot2, K)
            rows = jnp.arange(n)[:, None]
            masked = jnp.full_like(dot2, -jnp.inf).at[rows, idx].set(vals)
            return jax.nn.softmax(masked, axis=-1)
        key = jax.random.key(seed)
        k1, k2, k3, k4 = jax.random.split(key, 4)

        def kaiming(k, shape):
            bound = math.sqrt(3.0 / shape[-1])
            return jax.random.uniform(k, shape, jnp.float32, -bound, bound)
        x = jax.random.normal(k1, (B, S, H), jnp.float32)
        expert_embeddings = kaiming(k2, (E, H))
        first_linear = kaiming(k3, (E, I, H))
        second_linear = kaiming(k4, (E, H, I))
        return {'x': x, 'expert_embeddings': expert_embeddings, 'first_linear': first_linear, 'second_linear': second_linear}
    _L0_ffn_in = _L0_ffn_setup()
    _d = {'L0_attn_input_tensor': _L0_attn_in['input_tensor'], 'L0_attn_in_proj_w': _L0_attn_in['in_proj_w'], 'L0_attn_conv_w': _L0_attn_in['conv_w'], 'L0_attn_conv_b': _L0_attn_in['conv_b'], 'L0_attn_x_proj_w': _L0_attn_in['x_proj_w'], 'L0_attn_dt_proj_w': _L0_attn_in['dt_proj_w'], 'L0_attn_dt_proj_b': _L0_attn_in['dt_proj_b'], 'L0_attn_A_log': _L0_attn_in['A_log'], 'L0_attn_D_skip': _L0_attn_in['D_skip'], 'L0_attn_out_proj_w': _L0_attn_in['out_proj_w'], 'L0_attn_ln0_g': _L0_attn_in['ln0_g'], 'L0_attn_ln0_b': _L0_attn_in['ln0_b'], 'L0_attn_q_w': _L0_attn_in['q_w'], 'L0_attn_q_b': _L0_attn_in['q_b'], 'L0_attn_k_w': _L0_attn_in['k_w'], 'L0_attn_k_b': _L0_attn_in['k_b'], 'L0_attn_w_g': _L0_attn_in['w_g'], 'L0_attn_proj_w': _L0_attn_in['proj_w'], 'L0_attn_proj_b': _L0_attn_in['proj_b'], 'L0_attn_fl_w': _L0_attn_in['fl_w'], 'L0_attn_fl_b': _L0_attn_in['fl_b'], 'L0_attn_lni_g': _L0_attn_in['lni_g'], 'L0_attn_lni_b': _L0_attn_in['lni_b'], 'L0_attn_ln1_g': _L0_attn_in['ln1_g'], 'L0_attn_ln1_b': _L0_attn_in['ln1_b'], 'L0_attn_d1_w': _L0_attn_in['d1_w'], 'L0_attn_d1_b': _L0_attn_in['d1_b'], 'L0_attn_d2_w': _L0_attn_in['d2_w'], 'L0_attn_d2_b': _L0_attn_in['d2_b'], 'L0_attn_ln2_g': _L0_attn_in['ln2_g'], 'L0_attn_ln2_b': _L0_attn_in['ln2_b'], 'L0_ffn_expert_embeddings': _L0_ffn_in['expert_embeddings'], 'L0_ffn_first_linear': _L0_ffn_in['first_linear'], 'L0_ffn_second_linear': _L0_ffn_in['second_linear']}
    _x0 = _d['L0_attn_input_tensor']
    _d['L0_attn_input_tensor'] = jax.random.normal(jax.random.fold_in(jax.random.key(seed), 1), (32, 512, 256), dtype=_x0.dtype)
    del _x0
    return _d

def reference(L0_attn_input_tensor, L0_attn_in_proj_w, L0_attn_conv_w, L0_attn_conv_b, L0_attn_x_proj_w, L0_attn_dt_proj_w, L0_attn_dt_proj_b, L0_attn_A_log, L0_attn_D_skip, L0_attn_out_proj_w, L0_attn_ln0_g, L0_attn_ln0_b, L0_attn_q_w, L0_attn_q_b, L0_attn_k_w, L0_attn_k_b, L0_attn_w_g, L0_attn_proj_w, L0_attn_proj_b, L0_attn_fl_w, L0_attn_fl_b, L0_attn_lni_g, L0_attn_lni_b, L0_attn_ln1_g, L0_attn_ln1_b, L0_attn_d1_w, L0_attn_d1_b, L0_attn_d2_w, L0_attn_d2_b, L0_attn_ln2_g, L0_attn_ln2_b, L0_ffn_expert_embeddings, L0_ffn_first_linear, L0_ffn_second_linear):

    def _L0_attn_ref(input_tensor, in_proj_w, conv_w, conv_b, x_proj_w, dt_proj_w, dt_proj_b, A_log, D_skip, out_proj_w, ln0_g, ln0_b, q_w, q_b, k_w, k_b, w_g, proj_w, proj_b, fl_w, fl_b, lni_g, lni_b, ln1_g, ln1_b, d1_w, d1_b, d2_w, d2_b, ln2_g, ln2_b):
        import jax, jax.numpy as jnp
        import numpy as np
        D_MODEL = 256
        D_STATE = 16
        D_CONV = 4
        EXPAND = 2
        D_INNER = EXPAND * D_MODEL
        DT_RANK = D_MODEL // 16
        BATCH, SEQ = (8, 512)
        EPS = 1e-12

        def _layernorm(x, g, b):
            m = x.mean(-1, keepdims=True)
            v = ((x - m) ** 2).mean(-1, keepdims=True)
            return (x - m) / jnp.sqrt(v + EPS) * g + b

        def _l2norm(x, axis):
            n = jnp.sqrt((x * x).sum(axis, keepdims=True))
            return x / jnp.maximum(n, EPS)

        def _mamba(x, in_proj_w, conv_w, conv_b, x_proj_w, dt_proj_w, dt_proj_b, A_log, D_skip, out_proj_w):
            B, L, _ = x.shape
            xz = x @ in_proj_w.T
            u, res = jnp.split(xz, 2, axis=-1)
            xp = jnp.pad(u, ((0, 0), (D_CONV - 1, 0), (0, 0)))
            conv = conv_b + sum((xp[:, k:k + L, :] * conv_w[:, k] for k in range(D_CONV)))
            u = jax.nn.silu(conv)
            x_dbl = u @ x_proj_w.T
            dt, Bm, C = jnp.split(x_dbl, [DT_RANK, DT_RANK + D_STATE], axis=-1)
            delta = jax.nn.softplus(dt @ dt_proj_w.T + dt_proj_b)
            A = -jnp.exp(A_log)

            def step(h, t):
                delta_t, B_t, C_t, u_t = t
                dA = jnp.exp(delta_t[..., None] * A)
                h = dA * h + delta_t[..., None] * B_t[:, None, :] * u_t[..., None]
                y = jnp.einsum('bdn,bn->bd', h, C_t)
                return (h, y)
            xs = (jnp.swapaxes(delta, 0, 1), jnp.swapaxes(Bm, 0, 1), jnp.swapaxes(C, 0, 1), jnp.swapaxes(u, 0, 1))
            h0 = jnp.zeros((B, D_INNER, D_STATE), x.dtype)
            _, ys = jax.lax.scan(step, h0, xs)
            y = jnp.swapaxes(ys, 0, 1) + u * D_skip
            y = y * jax.nn.silu(res)
            return y @ out_proj_w.T

        def _forward(input_tensor, in_proj_w, conv_w, conv_b, x_proj_w, dt_proj_w, dt_proj_b, A_log, D_skip, out_proj_w, ln0_g, ln0_b, q_w, q_b, k_w, k_b, w_g, proj_w, proj_b, fl_w, fl_b, lni_g, lni_b, ln1_g, ln1_b, d1_w, d1_b, d2_w, d2_b, ln2_g, ln2_b):
            m = _mamba(input_tensor, in_proj_w, conv_w, conv_b, x_proj_w, dt_proj_w, dt_proj_b, A_log, D_skip, out_proj_w)
            h = _layernorm(m + input_tensor, ln0_g, ln0_b)
            q = jax.nn.gelu(_l2norm(h @ q_w.T + q_b, -1), approximate=False)
            k = _l2norm(h @ k_w.T + k_b, -1)
            qw = q @ w_g * D_MODEL ** (-0.5)
            Aw = _l2norm(qw, 1)
            G = (Aw * q).sum(1)
            hs = G[:, None, :] * k @ proj_w.T + proj_b
            hs = hs * _layernorm(h, lni_g, lni_b) @ fl_w.T + fl_b
            h2 = _layernorm(hs + h, ln1_g, ln1_b)
            f = jax.nn.gelu(h2 @ d1_w.T + d1_b, approximate=False) @ d2_w.T + d2_b
            return _layernorm(f + h2, ln2_g, ln2_b)
        return _forward(input_tensor, in_proj_w, conv_w, conv_b, x_proj_w, dt_proj_w, dt_proj_b, A_log, D_skip, out_proj_w, ln0_g, ln0_b, q_w, q_b, k_w, k_b, w_g, proj_w, proj_b, fl_w, fl_b, lni_g, lni_b, ln1_g, ln1_b, d1_w, d1_b, d2_w, d2_b, ln2_g, ln2_b)

    def _L0_ffn_ref(x, expert_embeddings, first_linear, second_linear):
        import jax, jax.numpy as jnp
        import numpy as np
        import math
        B, S, H = (8, 1024, 256)
        E, I, K = (8, 512, 2)
        CAP_FACTOR = 1.0

        def _router(x, expert_embeddings):
            dot = jnp.einsum('bsh,eh->bse', x, expert_embeddings)
            n = dot.shape[0] * dot.shape[1]
            dot2 = dot.reshape(n, E)
            vals, idx = jax.lax.top_k(dot2, K)
            rows = jnp.arange(n)[:, None]
            masked = jnp.full_like(dot2, -jnp.inf).at[rows, idx].set(vals)
            return jax.nn.softmax(masked, axis=-1)
        batch, seq, hidden = x.shape
        n_tokens = batch * seq
        expert_capacity = math.ceil(n_tokens / E * CAP_FACTOR)
        weights = _router(x, expert_embeddings)
        ones = (weights > 0).astype(weights.dtype)
        cap_ones = jnp.where(jnp.cumsum(ones, axis=0) <= expert_capacity, ones, 0.0)
        caw = weights * cap_ones
        vals, idx = jax.lax.top_k(caw.T, expert_capacity)
        index = idx.reshape(-1)
        x_flat = x.reshape(n_tokens, hidden)
        tokens = x_flat[index].reshape(E, expert_capacity, hidden)
        inter = jax.nn.relu(jnp.einsum('ech,eih->eci', tokens, first_linear))
        out = jnp.einsum('eci,ehi->ech', inter, second_linear)
        out = out * vals[:, :, None]
        final = jnp.zeros((n_tokens, hidden), x.dtype).at[index].add(out.reshape(-1, hidden))
        return final.reshape(x.shape)
    x = L0_attn_input_tensor
    x = x + _layernorm(_L0_attn_ref(_layernorm(x, axis=-1), L0_attn_in_proj_w, L0_attn_conv_w, L0_attn_conv_b, L0_attn_x_proj_w, L0_attn_dt_proj_w, L0_attn_dt_proj_b, L0_attn_A_log, L0_attn_D_skip, L0_attn_out_proj_w, L0_attn_ln0_g, L0_attn_ln0_b, L0_attn_q_w, L0_attn_q_b, L0_attn_k_w, L0_attn_k_b, L0_attn_w_g, L0_attn_proj_w, L0_attn_proj_b, L0_attn_fl_w, L0_attn_fl_b, L0_attn_lni_g, L0_attn_lni_b, L0_attn_ln1_g, L0_attn_ln1_b, L0_attn_d1_w, L0_attn_d1_b, L0_attn_d2_w, L0_attn_d2_b, L0_attn_ln2_g, L0_attn_ln2_b), axis=-1)
    x = x + _layernorm(_L0_ffn_ref(_layernorm(x, axis=-1), L0_ffn_expert_embeddings, L0_ffn_first_linear, L0_ffn_second_linear), axis=-1)
    return x

_drawn_inputs = setup_inputs


def setup_inputs(seed=0):
    import zlib

    import numpy as np

    out = dict(_drawn_inputs(seed))
    spreads = {'L0_attn_conv_b': (0.0, 0.408),
     'L0_attn_dt_proj_b': (-2.0, 0.6),
     'L0_attn_D_skip': (1.0, 0.6),
     'L0_attn_ln0_g': (1.0, 0.2),
     'L0_attn_ln0_b': (0.0, 0.1),
     'L0_attn_q_b': (0.0, 0.778),
     'L0_attn_k_b': (0.0, 2.0),
     'L0_attn_proj_b': (0.0, 0.1),
     'L0_attn_fl_b': (0.0, 0.1),
     'L0_attn_lni_g': (1.0, 0.6),
     'L0_attn_lni_b': (0.0, 0.529),
     'L0_attn_ln1_g': (1.0, 0.2),
     'L0_attn_ln1_b': (0.0, 0.1),
     'L0_attn_d1_b': (0.0, 0.1),
     'L0_attn_d2_b': (0.0, 0.1),
     'L0_attn_ln2_g': (1.0, 0.2),
     'L0_attn_ln2_b': (0.0, 0.1)}
    factors = {'L0_attn_in_proj_w': 3.411,
     'L0_attn_conv_w': 5.204,
     'L0_attn_x_proj_w': 8.0,
     'L0_attn_dt_proj_w': 8.0,
     'L0_attn_A_log': 8.0,
     'L0_attn_out_proj_w': 3.446,
     'L0_attn_q_w': 8.0,
     'L0_attn_k_w': 7.738,
     'L0_attn_w_g': 6.149,
     'L0_attn_proj_w': 7.5}
    for name, (base, spread) in spreads.items():
        noise = np.random.default_rng([zlib.crc32(name.encode()), seed]).standard_normal(out[name].shape)
        drawn = base * np.exp(spread * noise) if base else spread * noise
        out[name] = jnp.asarray(drawn.astype(out[name].dtype))
    for name, factor in factors.items():
        out[name] = (out[name] * factor).astype(out[name].dtype)
    return out
```

```python
from contextlib import ExitStack

import concourse.bass as bass
from concourse import mybir

ALU = mybir.AluOpType
ACT = mybir.ActivationFunctionType
F32 = mybir.dt.float32
BF16 = mybir.dt.bfloat16
U32 = mybir.dt.uint32
AX_X = mybir.AxisListType.X

P = 128
LEAD = 2
LN_EPS = 1e-5
EPS = 1e-12
LOG_SHIFT = 20
LN2 = 0.6931471805599453


class Steps:

    def __init__(self, sem, names):
        self.sem, self.names, self.next = sem, list(names), 0

    def did(self, name):
        assert self.names[self.next % len(self.names)] == name, (name, self.names[self.next % len(self.names)])
        self.next += 1
        return self.sem

    def value(self, index, n):
        return (n + LEAD) * len(self.names) + index + 1

    def at(self, name, n):
        return self.sem, self.value(self.names.index(name), n)

    def credit(self, engine):
        engine.sem_inc(self.sem, LEAD * len(self.names))


def advance(stage):
    if stage is not None:
        next(stage, None)


def build(nc, t):
    S, L, D = t["x"].shape
    DI = t["conv_w"].shape[0]
    NS = t["A_log"].shape[1]
    R = t["dt_w"].shape[0]
    FF = t["d1_w"].shape[1]
    NE, _, EI = t["e1_w"].shape
    TT = L // P
    KD, KI, KF, KE = D // P, DI // P, FF // P, EI // P
    NX = R + 2 * NS
    NTOK = S * L
    CAP = -(-NTOK // NE)
    NSLOT = NE * CAP
    BLK = min(512, CAP)
    TB = BLK // P
    QB = CAP // BLK
    FAR = float(1 << 20)
    assert S % 2 == 0 and L == 512 and CAP % BLK == 0 and NSLOT % (16 * P) == 0 and S >= 4

    NP2 = NS // 2
    NU = NP2 * KI
    RING = 4

    x_v = t["x"].rearrange("s (t p) d -> s p t d", p=P)
    out_v = t["out"].rearrange("s (t p) d -> s p t d", p=P)
    bc_dram = [nc.dram_tensor(f"bc_rows{i}", (2 * NS, L), F32, kind="Internal").ap() for i in range(2)]
    x1_dram = nc.dram_tensor("x1_rows", (S, L, D), F32, kind="Internal").ap()
    x1_v = x1_dram.rearrange("s (t p) d -> s p t d", p=P)
    xe_dram = nc.dram_tensor("expert_in", (NSLOT, D), F32, kind="Internal").ap()
    ye_dram = nc.dram_tensor("expert_out", (NSLOT, D), F32, kind="Internal").ap()
    xe_zero_v = xe_dram.rearrange("(a p r) d -> a p (r d)", p=P, r=16)
    xe_v = xe_dram.rearrange("(n t p) d -> n p t d", t=TB, p=P)
    ye_v = ye_dram.rearrange("(n t p) d -> n p t d", t=TB, p=P)

    with ExitStack() as whole:
        def sem(name):
            return whole.enter_context(nc.semaphore(name))

        idx_all = whole.enter_context(nc.sbuf_tensor("idx_all", [P, S * TT, 2], U32))
        w_all = whole.enter_context(nc.sbuf_tensor("w_all", [P, S * TT, 2], F32))
        ident = whole.enter_context(nc.sbuf_tensor("ident", [P, P], F32))
        ones = whole.enter_context(nc.sbuf_tensor("ones", [P, P], F32))
        eps5 = whole.enter_context(nc.sbuf_tensor("eps5", [P, 1], F32))
        eps12 = whole.enter_context(nc.sbuf_tensor("eps12", [P, 1], F32))
        shift = whole.enter_context(nc.sbuf_tensor("shift", [P, 1], F32))
        bank = [whole.enter_context(nc.psum_tensor(f"bank{i}", [P, 512], F32)) for i in range(8)]

        attention_phase(nc, t, dict(locals()), sem)
        expert_phase(nc, t, dict(locals()), sem)
        combine_phase(nc, t, dict(locals()), sem)


def attention_phase(nc, t, env, sem):
    S, L, D, DI, NS, R, NE, TT = (env[k] for k in ("S", "L", "D", "DI", "NS", "R", "NE", "TT"))
    KD, KI, KF, NX, CAP, NSLOT, FAR = (env[k] for k in ("KD", "KI", "KF", "NX", "CAP", "NSLOT", "FAR"))
    NP2, NU, RING = env["NP2"], env["NU"], env["RING"]
    x_v, x1_v, xe_dram, bc_dram, xe_zero_v = (env[k] for k in ("x_v", "x1_v", "xe_dram", "bc_dram", "xe_zero_v"))
    idx_all, w_all, ident, ones, eps5, eps12, shift, bank = (
        env[k] for k in ("idx_all", "w_all", "ident", "ones", "eps5", "eps12", "shift", "bank"))
    Y, RB, PB = bank[0:4], bank[4:6], bank[6:8]

    with ExitStack() as ctx:
        def sb(name, shape, dt=F32):
            return ctx.enter_context(nc.sbuf_tensor(name, shape, dt))

        in_w = sb("in_w", [P, KD, 2 * DI])
        xp_w = sb("xp_w", [P, KI, NX])
        dt_w = sb("dt_w", [R, DI])
        out_w = sb("out_w", [P, KI, D])
        q_w = sb("q_w", [P, KD, D])
        k_w = sb("k_w", [P, KD, D])
        pr_w = sb("pr_w", [P, KD, D])
        fl_w = sb("fl_w", [P, KD, D])
        d1_w = sb("d1_w", [P, KD, KF * P])
        d2_w = sb("d2_w", [P, KF, D])
        emb = sb("emb", [P, KD, NE])
        conv_w = sb("conv_w", [P, KI, 4])
        conv_b = sb("conv_b", [P, KI])
        dt_b = sb("dt_b", [P, KI])
        a_neg = sb("a_neg", [P, KI, NS])
        d_skip = sb("d_skip", [P, KI])
        k_b = sb("k_b", [P, KD])
        g0f = sb("g0f", [P, KD])
        b0f = sb("b0f", [P, KD])
        g1f = sb("g1f", [P, KD])
        b1f = sb("b1f", [P, KD])
        d1_b = sb("d1_b", [P, KF])
        rows = {n: sb(f"row_{n}", [P, D]) for n in
                ("q_b", "pr_b", "fl_b", "ln0_g", "ln0_b", "lni_g", "lni_b", "ln1_g", "ln2_g", "ln2_b", "w_g")}
        d2_row = sb("d2_row", [P, D])
        tri = sb("tri", [P, P], BF16)
        ones_bf = sb("ones_bf", [P, P], BF16)
        iota8 = sb("iota8", [P, NE])
        slot0 = sb("slot0", [P, NE])
        xin = [sb(f"xin{i}", [P, TT, D]) for i in range(2)]
        u = [sb(f"u{i}", [P, KI, L]) for i in range(2)]
        g = [sb(f"g{i}", [P, KI, L]) for i in range(2)]
        delta = [sb(f"delta{i}", [P, KI, L]) for i in range(2)]
        du = [sb(f"du{i}", [P, KI, L]) for i in range(2)]
        xT = [d[:, 0:KD, :] for d in du]
        xd = sb("xd", [NX, L])
        rest = sb("rest", [P, L])
        bc = [sb(f"bc{i}", [P, 2, 2, L]) for i in range(2)]
        dA = [sb(f"dA{i}", [P, 2, L]) for i in range(2)]
        st = [sb(f"st{i}", [P, 2, L]) for i in range(RING)]
        stat_pre = sb("stat_pre", [P, TT, 6])
        mv_pre = sb("mv_pre", [P, TT, 2])
        r_pre = sb("r_pre", [P, TT])
        F = sb("F", [P, KD, L])
        gT = sb("gT", [P, KF, L])
        h = sb("h", [P, TT, D])
        tb = sb("tb", [P, TT, D])
        s = sb("s", [P, TT, D])
        gT_flat = gT[:, :, :].rearrange("p a b -> p (a b)")
        part = TT * D
        q = gT_flat[:, 0:part].rearrange("p (t d) -> p t d", t=TT)
        li = gT_flat[:, part:2 * part].rearrange("p (t d) -> p t d", t=TT)
        kT = gT_flat[:, 2 * part:3 * part].rearrange("p (k l) -> p k l", k=KD)
        ksq = gT_flat[:, 3 * part:4 * part].rearrange("p (k l) -> p k l", k=KD)
        proj_g = sb("proj_g", [P, KD, D])
        junk_act = li
        junk_dve = gT_flat[:, 3 * part:4 * part].rearrange("p (t d) -> p t d", t=TT)
        stat = sb("stat", [P, TT, 6])
        mv = sb("mv", [P, TT, 2])
        r = sb("r", [P, TT])
        ssq = sb("ssq", [P, TT])
        rq = sb("rq", [P, TT])
        ssk = sb("ssk", [P, TT])
        rk = sb("rk", [P, TT])
        qw = sb("qw", [P, TT])
        qw2 = sb("qw2", [P, TT])
        ssg = sb("ssg", [P, 1])
        rg = sb("rg", [P, 1])
        gcol = sb("gcol", [P, KD])
        dots = sb("dots", [P, TT, NE])
        top = sb("top", [P, TT, 8])
        top_i = sb("top_i", [P, TT, 8], U32)
        top_f = sb("top_f", [P, TT, 2])
        dv = sb("dv", [P, TT])
        e2 = sb("e2", [P, TT])
        den = sb("den", [P, TT])
        wts = sb("wts", [P, TT, 2])
        pos2 = sb("pos2", [P, TT])
        oh = [sb(f"oh{i}", [P, TT, NE]) for i in range(2)]
        asg = sb("asg", [P, TT, NE], BF16)
        cum = sb("cum", [P, TT, NE])
        keep = sb("keep", [P, TT, NE])
        pick = [sb(f"pick{i}", [P, TT, NE]) for i in range(2)]
        slot_f = sb("slot_f", [P, TT, 2])
        idx = sb("idx", [P, TT, 2], U32)
        run = sb("run", [P, NE])

        weights_in = sem("weights_in")
        consts = sem("consts")
        setup_dve = sem("setup_dve")
        setup_act = sem("setup_act")
        x_loaded = sem("x_loaded")
        xd_stored = sem("xd_stored")
        bc_loaded = [sem(f"bc_loaded{i}") for i in range(2)]
        xr_loaded = sem("xr_loaded")
        x1_stored = sem("x1_stored")
        scattered = sem("scattered")
        carried_pool = sem("carried_pool")
        carried_sp = sem("carried_sp")
        carried_dve = sem("carried_dve")
        zero_tile = sem("zero_tile")
        zeroed = sem("zeroed")

        def ln_names(n):
            return [f"{n}_stats", f"{n}_aggr"]

        pre_dve = Steps(sem("pre_dve"), ["x_stats", "x_aggr", "x_normed"]
                        + [f"conv{c}_{j}" for c in range(KI) for j in range(3)]
                        + ["xd"] + [f"z{c}" for c in range(KI)] + [f"w{c}" for c in range(KI)] + ["delta"])
        pre_act = Steps(sem("pre_act"), ["x_ln", "x_r", "xT"] + [f"tap{c}" for c in range(KI)] + ["u"]
                        + [f"g{c}" for c in range(KI)] + ["z_abs", "sp_exp"] + [f"sp_ln{c}" for c in range(KI)])
        pre_pe = Steps(sem("pre_pe"), ["xT"] + [f"u{c}" for c in range(KI)] + [f"g{c}" for c in range(KI)]
                       + ["xd"] + [f"dt{c}" for c in range(KI)])
        pre_pool = Steps(sem("pre_pool"), [f"{n}{c}" for c in range(KI) for n in ("rest", "log1p")] + ["du"])
        scan_exp = Steps(sem("scan_exp"), range(NU))
        scan_in = Steps(sem("scan_in"), range(NU))
        scan_h = Steps(sem("scan_h"), range(NU))
        scan_hc = Steps(sem("scan_hc"), range(NU))
        scan_sum = Steps(sem("scan_sum"), range(NU))
        post_pe = Steps(sem("post_pe"), ["m", "hT", "q", "k", "ssk", "G", "hs", "tT", "fl", "sT"]
                        + [f"d1_{j}" for j in range(KF)] + ["d2_0", "d2_1", "nT", "dots", "cum"])
        post_act = Steps(sem("post_act"), ["h_ln", "h_r", "hT", "q_sq", "kT", "k_sq", "q_ln", "q_r", "k_ln", "k_r",
                                           "q_gelu", "hi_ln", "hi_r", "G_ln", "G_r", "tT", "s_ln", "s_r", "sT"]
                         + [f"gelu{j}" for j in range(KF)]
                         + ["f_ln", "f_r", "o_ln", "o_r", "n_ln", "n_r", "nT", "e2"])
        post_dve = Steps(sem("post_dve"), [f"y_{a}{c}" for a in "ab" for c in (0, 1)]
                         + [f"y_{a}{c}" for a in "ab" for c in (2, 3)]
                         + ["h_sum", "h_stats", "h_aggr", "h_normed", "q_sum", "ssq", "ssk"]
                         + ["hi_stats", "hi_aggr", "qw", "qw2", "ssg_sum", "ssg", "li", "G", "proj_g", "t",
                            "s_sum", "s_stats", "s_aggr", "s_normed", "f_sum0", "f_sum1", "f_stats", "f_aggr",
                            "f_normed", "o_stats", "o_aggr", "o_normed", "n_stats", "n_aggr", "n_normed",
                            "dots", "top", "top_i", "dv", "top_f", "den", "w1", "w2", "pos2", "oh0", "oh1",
                            "oh1_pos", "asg", "cum", "keep", "run", "slotv", "slotk", "pick0", "pick1",
                            "slot0", "slot1", "idx", "idx_all", "w_all"])
        post_pool = Steps(sem("post_pool"), ["h_g", "h_b", "li_g", "li_b", "h_fl", "t_li", "s_g", "s_b",
                                             "f_g", "f_b", "x1", "sent"])

        DMA_IN = [(in_w[:, :, :], t["in_w"].rearrange("(k p) n -> p k n", p=P)),
                  (xp_w[:, :, :], t["xp_w"].rearrange("(k p) n -> p k n", p=P)),
                  (dt_w[:, :], t["dt_w"]),
                  (out_w[:, :, :], t["out_w"].rearrange("(k p) n -> p k n", p=P)),
                  (q_w[:, :, :], t["q_w"].rearrange("(k p) n -> p k n", p=P)),
                  (k_w[:, :, :], t["k_w"].rearrange("(k p) n -> p k n", p=P)),
                  (pr_w[:, :, :], t["pr_w"].rearrange("(k p) n -> p k n", p=P)),
                  (fl_w[:, :, :], t["fl_w"].rearrange("(k p) n -> p k n", p=P)),
                  (d1_w[:, :, :], t["d1_w"].rearrange("(k p) n -> p k n", p=P)),
                  (d2_w[:, :, :], t["d2_w"].rearrange("(k p) n -> p k n", p=P)),
                  (emb[:, :, :], t["emb"].rearrange("(k p) n -> p k n", p=P)),
                  (conv_w[:, :, :], t["conv_w"].rearrange("(k p) n -> p k n", p=P)),
                  (a_neg[:, :, :], t["A_log"].rearrange("(k p) n -> p k n", p=P))]
        DMA_IN += [(dst[:, :], t[name].rearrange("(k p) -> p k", p=P)) for dst, name in
                   ((conv_b, "conv_b"), (dt_b, "dt_b"), (d_skip, "D_skip"), (k_b, "k_b"), (g0f, "ln0_g"),
                    (b0f, "ln0_b"), (g1f, "ln1_g"), (b1f, "ln1_b"), (d1_b, "d1_b"))]
        DMA_IN += [(rows[n][:, :], t[n].partition_broadcast(P)) for n in rows]
        DMA_IN += [(d2_row[:, :], t["d2_b"].partition_broadcast(P)), (s[:, 0, :], t["ln1_b"].partition_broadcast(P))]

        def run_stages(unit, post, pre, b):
            for k in range(NU):
                unit(k)
                advance(post)
                if k >= 2 and (k % 2 == 0 or k > 20):
                    advance(pre)
            for stage in (post, pre):
                if stage is not None:
                    for _ in stage:
                        pass

        def all_sequences(engine, pre, scan, post):
            for _ in pre(0, 0):
                pass
            scan(0, 0, None, pre(1, 1))
            with engine.Fori(0, (S - 2) // 2) as i:
                for half in range(2):
                    b = 2 * i + (1 + half)
                    par = (1 + half) % 2
                    scan(b, par, post(b - 1, 1 - par), pre(b + 1, 1 - par))
            scan(S - 1, 1, post(S - 2, 0), None)
            for _ in post(S - 1, 1):
                pass

        block = ctx.enter_context(nc.Block())

        @block.sync
        def _(sp):
            sp.sem_inc(x1_stored, 16)
            for dst, src in DMA_IN:
                with nc.allow_non_contiguous_dma(reason="small per-channel vectors, once"):
                    sp.dma_start(dst, src).then_inc(weights_in, 16)
            sp.wait_ge(zero_tile, 1)
            for a in range(xe_zero_v.shape[0]):
                sp.dma_start(xe_zero_v[a], gT_flat).then_inc(zeroed, 16)

            def pre(b, par):
                sp.wait_ge(*pre_pe.at("xT", b - 2))
                sp.wait_ge(*post_dve.at("h_sum", b - 2))
                sp.sem_inc(carried_sp, 1)
                sp.dma_start(xin[par][:, :, :], x_v[b]).then_inc(x_loaded, 16)
                for _ in range(9):
                    yield
                sp.wait_ge(*pre_dve.at("xd", b))
                sp.dma_start(bc_dram[par], xd[R:NX, :]).then_inc(xd_stored, 16)

            def load_bc(b, par, pair):
                sp.wait_ge(*scan_hc.at(NU - 1, b - 1) if pair < 2 else scan_hc.at((pair - 2) * KI + KI - 1, b))
                src = bc_dram[par].rearrange("(s n) l -> s n l", s=2)[:, 2 * pair:2 * pair + 2, :]
                sp.dma_start(bc[pair % 2][:, :, :, :], src.partition_broadcast(P)).then_inc(bc_loaded[pair % 2], 16)

            def scan(b, par, post_stage, pre_stage):
                sp.wait_ge(xd_stored, 16 * (b + 1))
                sp.sem_inc(carried_sp, 1)
                load_bc(b, par, 0)
                load_bc(b, par, 1)

                def unit(k):
                    if k % KI == 0 and k // KI >= 1 and k // KI + 1 < NP2:
                        load_bc(b, par, k // KI + 1)
                run_stages(unit, post_stage, pre_stage, b)

            def post(b, par):
                for _ in range(13):
                    yield
                sp.wait_ge(*post_dve.at("s_sum", b))
                sp.sem_inc(carried_sp, 1)
                sp.dma_start(h[:, :, :], x_v[b]).then_inc(xr_loaded, 16)
                for _ in range(9):
                    yield
                sp.wait_ge(*post_pool.at("x1", b))
                sp.sem_inc(carried_sp, 1)
                sp.dma_start(x1_v[b], h[:, :, :]).then_inc(x1_stored, 16)

            all_sequences(sp, pre, scan, post)
            sp.wait_ge(x1_stored, 16 * (S + 1))
            sp.wait_ge(*post_pool.at("sent", S - 1))

        @block.gpsimd
        def _(pool):
            pool.memset(ident[:, :], 0.0).then_inc(consts, 1)
            pool.memset(ones[:, :], 1.0).then_inc(consts, 1)
            pool.memset(ones_bf[:, :], 1.0).then_inc(consts, 1)
            pool.memset(tri[:, :], 1.0).then_inc(consts, 1)
            pool.memset(eps5[:, :], LN_EPS).then_inc(consts, 1)
            pool.memset(eps12[:, :], EPS).then_inc(consts, 1)
            pool.memset(shift[:, :], 0.5 * LOG_SHIFT * LN2).then_inc(consts, 1)
            pool.memset(run[:, :], 0.0).then_inc(consts, 1)
            for i in range(2):
                pool.memset(dA[i][:, :, 0:1], 0.0).then_inc(consts, 1)
            pool.iota(iota8[:, :], pattern=[[1, NE]], base=0, channel_multiplier=0,
                      allow_small_or_imprecise_dtypes=True).then_inc(consts, 1)
            pool.iota(slot0[:, :], pattern=[[CAP, NE]], base=-1 - int(FAR), channel_multiplier=0,
                      allow_small_or_imprecise_dtypes=True).then_inc(consts, 1)
            pool.wait_ge(consts, 12)
            pool.affine_select(out=ident[:, :], in_=ident[:, :], compare_op=ALU.not_equal, fill=1.0, base=0,
                               pattern=[[-1, P]], channel_multiplier=1).then_inc(consts, 1)
            pool.affine_select(out=tri[:, :], in_=tri[:, :], compare_op=ALU.is_ge, fill=0.0, base=0,
                               pattern=[[1, P]], channel_multiplier=-1).then_inc(consts, 1)
            for steps in (pre_pool, scan_hc, post_pool):
                steps.credit(pool)
            pool.wait_ge(weights_in, 16 * len(DMA_IN))
            pool.wait_ge(setup_dve, 2)

            def pre(b, par):
                for _ in range(12):
                    yield
                for c in range(KI):
                    pool.wait_ge(*pre_dve.at(f"w{c}", b))
                    pool.tensor_tensor(rest[:, :], du[par][:, c, :], rest[:, :], ALU.subtract)\
                        .then_inc(pre_pool.did(f"rest{c}"), 1)
                    pool.wait_ge(*pre_act.at(f"sp_ln{c}", b))
                    pool.wait_ge(*pre_pool.at(f"rest{c}", b))
                    pool.tensor_tensor(du[par][:, c, :], du[par][:, c, :], rest[:, :], ALU.add)\
                        .then_inc(pre_pool.did(f"log1p{c}"), 1)
                    yield
                pool.wait_ge(*pre_dve.at("delta", b))
                pool.tensor_tensor(du[par][:, :, :], delta[par][:, :, :], u[par][:, :, :], ALU.mult)\
                    .then_inc(pre_pool.did("du"), 1)

            def scan(b, par, post_stage, pre_stage):
                def unit(k):
                    pair = k // KI
                    tile = st[k % RING]
                    pool.wait_ge(*scan_h.at(k, b))
                    pool.tensor_tensor(tile[:, :, :], tile[:, :, :], bc[pair % 2][:, 1, :, :], ALU.mult)\
                        .then_inc(scan_hc.did(k), 1)
                run_stages(unit, post_stage, pre_stage, b)

            def times(name, dst, row):
                pool.tensor_tensor(dst[:, :, :], dst[:, :, :], row[:, :].unsqueeze(1).to_broadcast([P, TT, D]),
                                   ALU.mult).then_inc(post_pool.did(name), 1)

            def plus(name, dst, row):
                pool.tensor_tensor(dst[:, :, :], dst[:, :, :], row[:, :].unsqueeze(1).to_broadcast([P, TT, D]),
                                   ALU.add).then_inc(post_pool.did(name), 1)

            def post(b, par):
                yield
                yield
                yield
                pool.wait_ge(*post_pe.at("hT", b))
                times("h_g", h, rows["ln0_g"])
                pool.wait_ge(*post_pool.at("h_g", b))
                plus("h_b", h, rows["ln0_b"])
                for _ in range(5):
                    yield
                pool.wait_ge(*post_dve.at("li", b))
                times("li_g", li, rows["lni_g"])
                pool.wait_ge(*post_pool.at("li_g", b))
                plus("li_b", li, rows["lni_b"])
                yield
                plus("h_fl", h, rows["fl_b"])
                pool.wait_ge(*post_dve.at("t", b))
                pool.wait_ge(*post_pool.at("li_b", b))
                pool.tensor_tensor(tb[:, :, :], tb[:, :, :], li, ALU.mult).then_inc(post_pool.did("t_li"), 1)
                yield
                yield
                yield
                pool.wait_ge(*post_pe.at("sT", b))
                times("s_g", s, rows["ln1_g"])
                pool.wait_ge(*post_pool.at("s_g", b))
                plus("s_b", s, d2_row)
                for _ in range(7):
                    yield
                pool.wait_ge(*post_dve.at("f_normed", b))
                times("f_g", s, rows["ln2_g"])
                pool.wait_ge(*post_pool.at("f_g", b))
                plus("f_b", s, rows["ln2_b"])
                yield
                yield
                yield
                pool.wait_ge(*post_dve.at("o_normed", b))
                pool.wait_ge(xr_loaded, 16 * (b + 1))
                pool.tensor_tensor(h[:, :, :], h[:, :, :], s[:, :, :], ALU.add).then_inc(post_pool.did("x1"), 1)
                for _ in range(5):
                    yield
                pool.wait_ge(*post_dve.at("idx", b))
                pool.sem_inc(carried_pool, 1)
                pool.wait_ge(zeroed, 16 * xe_zero_v.shape[0])
                for tile in range(TT):
                    for choice in range(2):
                        pool.indirect_dma_start(
                            out=xe_dram, out_offset=bass.IndirectOffsetOnAxis(ap=idx[:, tile, choice:choice + 1], axis=0),
                            in_=tb[:, tile, :], in_offset=None, bounds_check=NSLOT - 1, oob_is_err=False)\
                            .then_inc(scattered, 16)
                yield
                yield
                pool.wait_ge(scattered, 16 * 2 * TT * (b + 1))
                pool.sem_inc(post_pool.did("sent"), 1)

            all_sequences(pool, pre, scan, post)

        @block.scalar
        def _(act):
            for steps in (pre_act, scan_exp, post_act):
                steps.credit(act)
            act.wait_ge(consts, 14)
            act.wait_ge(weights_in, 16 * len(DMA_IN))
            act.activation(a_neg[:, :, :], a_neg[:, :, :], ACT.Exp).then_inc(setup_act, 1)
            act.wait_ge(setup_dve, 2)

            def rsqrt(steps, name, out, var, eps, b):
                act.activation(out[:, :], var, ACT.Ln, bias=eps[:, 0:1]).then_inc(steps.did(f"{name}_ln"), 1)
                act.wait_ge(*steps.at(f"{name}_ln", b))
                act.activation(out[:, :], out[:, :], ACT.Exp, scale=-0.5).then_inc(steps.did(f"{name}_r"), 1)

            def rnorm(name, out, ss, b):
                act.activation(out[:, :], ss[:, :], ACT.Ln, scale=float(1 << LOG_SHIFT))\
                    .then_inc(post_act.did(f"{name}_ln"), 1)
                act.wait_ge(*post_act.at(f"{name}_ln", b))
                act.activation(out[:, :], out[:, :], ACT.Exp, scale=-0.5, bias=shift[:, 0:1])\
                    .then_inc(post_act.did(f"{name}_r"), 1)

            def pre(b, par):
                act.wait_ge(*pre_dve.at("x_aggr", b))
                rsqrt(pre_act, "x", r_pre, mv_pre[:, :, 1], eps5, b)
                yield
                act.wait_ge(*pre_pe.at("xT", b))
                act.copy(xT[par][:, 0, :], RB[0][:, :])
                act.copy(xT[par][:, 1, :], RB[1][:, :]).then_inc(pre_act.did("xT"), 1)
                yield
                for c in range(KI):
                    act.wait_ge(*pre_pe.at(f"u{c}", b))
                    if c == 0:
                        act.wait_ge(*post_pe.at("m", b - 2))
                    act.activation(u[par][:, c, :], RB[c % 2][:, :], ACT.Identity, bias=conv_b[:, c:c + 1],
                                   scale=conv_w[:, c, 3:4]).then_inc(pre_act.did(f"tap{c}"), 1)
                    yield
                act.wait_ge(*pre_dve.at("conv3_2", b))
                act.activation(u[par][:, :, :], u[par][:, :, :], ACT.Silu).then_inc(pre_act.did("u"), 1)
                for c in range(KI):
                    act.wait_ge(*pre_pe.at(f"g{c}", b))
                    act.activation(g[par][:, c, :], RB[c % 2][:, :], ACT.Silu).then_inc(pre_act.did(f"g{c}"), 1)
                    if c % 2 == 1:
                        yield
                for _ in range(3):
                    yield
                act.wait_ge(*pre_dve.at("z3", b))
                act.activation(du[par][:, :, :], delta[par][:, :, :], ACT.Abs).then_inc(pre_act.did("z_abs"), 1)
                act.wait_ge(*pre_act.at("z_abs", b))
                act.activation(du[par][:, :, :], du[par][:, :, :], ACT.Exp, scale=-1.0)\
                    .then_inc(pre_act.did("sp_exp"), 1)
                yield
                for c in range(KI):
                    act.wait_ge(*pre_pool.at(f"rest{c}", b))
                    act.activation(du[par][:, c, :], du[par][:, c, :], ACT.Ln, bias=ones[:, 0:1])\
                        .then_inc(pre_act.did(f"sp_ln{c}"), 1)
                    yield

            def scan(b, par, post_stage, pre_stage):
                def decay(k):
                    pair, c = k // KI, k % KI
                    if k == 0:
                        act.wait_ge(*pre_dve.at("delta", b))
                    act.wait_ge(*scan_h.at(NU - 2 + k, b - 1) if k < 2 else scan_h.at(k - 2, b))
                    for j in range(2):
                        last = act.activation(dA[k % 2][:, j, 1:L], delta[par][:, c, 1:L], ACT.Exp,
                                              scale=a_neg[:, c, 2 * pair + j:2 * pair + j + 1])
                    last.then_inc(scan_exp.did(k), 1)

                def unit(k):
                    if k == 0:
                        decay(0)
                    if k + 1 < NU:
                        decay(k + 1)
                run_stages(unit, post_stage, pre_stage, b)

            def post(b, par):
                yield
                yield
                act.wait_ge(*post_dve.at("h_aggr", b))
                rsqrt(post_act, "h", r, mv[:, :, 1], eps12, b)
                yield
                act.wait_ge(*post_pe.at("hT", b))
                for c in range(KD):
                    last = act.activation(F[:, c, :], PB[c][:, :], ACT.Identity, bias=b0f[:, c:c + 1],
                                          scale=g0f[:, c:c + 1])
                last.then_inc(post_act.did("hT"), 1)
                yield
                act.wait_ge(*post_dve.at("q_sum", b))
                for tile in range(TT):
                    last = act.activation(junk_act[:, tile, :], q[:, tile, :], ACT.Square, accum_out=ssq[:, tile:tile + 1])
                last.then_inc(post_act.did("q_sq"), 1)
                yield
                act.wait_ge(*post_pe.at("k", b))
                for c in range(KD):
                    last = act.activation(kT[:, c, :], PB[c][:, :], ACT.Identity, bias=k_b[:, c:c + 1])
                last.then_inc(post_act.did("kT"), 1)
                act.wait_ge(*post_act.at("kT", b))
                act.activation(ksq, kT, ACT.Square).then_inc(post_act.did("k_sq"), 1)
                act.wait_ge(*post_dve.at("ssq", b))
                rnorm("q", rq, ssq, b)
                yield
                act.wait_ge(*post_dve.at("ssk", b))
                rnorm("k", rk, ssk, b)
                for tile in range(TT):
                    if tile == 0:
                        act.wait_ge(*post_act.at("q_r", b))
                    last = act.activation(q[:, tile, :], q[:, tile, :], ACT.Gelu, scale=rq[:, tile:tile + 1])
                last.then_inc(post_act.did("q_gelu"), 1)
                yield
                act.wait_ge(*post_dve.at("hi_aggr", b))
                rsqrt(post_act, "hi", r, mv[:, :, 1], eps12, b)
                act.wait_ge(*post_dve.at("ssg", b))
                rnorm("G", rg, ssg, b)
                yield
                yield
                yield
                act.wait_ge(*post_pe.at("tT", b))
                act.copy(F[:, 0, :], PB[0][:, :])
                act.copy(F[:, 1, :], PB[1][:, :]).then_inc(post_act.did("tT"), 1)
                yield
                act.wait_ge(*post_dve.at("s_aggr", b))
                rsqrt(post_act, "s", r, mv[:, :, 1], eps12, b)
                yield
                act.wait_ge(*post_pe.at("sT", b))
                for c in range(KD):
                    last = act.activation(F[:, c, :], PB[c][:, :], ACT.Identity, bias=b1f[:, c:c + 1],
                                          scale=g1f[:, c:c + 1])
                last.then_inc(post_act.did("sT"), 1)
                yield
                for j in range(KF):
                    act.wait_ge(*post_pe.at(f"d1_{j}", b))
                    act.activation(gT[:, j, :], PB[j % 2][:, :], ACT.Gelu, bias=d1_b[:, j:j + 1])\
                        .then_inc(post_act.did(f"gelu{j}"), 1)
                    if j % 2 == 1:
                        yield
                yield
                act.wait_ge(*post_dve.at("f_aggr", b))
                rsqrt(post_act, "f", r, mv[:, :, 1], eps12, b)
                yield
                yield
                yield
                act.wait_ge(*post_dve.at("o_aggr", b))
                rsqrt(post_act, "o", r, mv[:, :, 1], eps5, b)
                yield
                yield
                act.wait_ge(*post_dve.at("n_aggr", b))
                rsqrt(post_act, "n", r, mv[:, :, 1], eps5, b)
                yield
                act.wait_ge(*post_pe.at("nT", b))
                act.copy(F[:, 0, :], PB[0][:, :])
                act.copy(F[:, 1, :], PB[1][:, :]).then_inc(post_act.did("nT"), 1)
                yield
                act.wait_ge(*post_dve.at("dv", b))
                act.activation(e2[:, :], dv[:, :], ACT.Exp).then_inc(post_act.did("e2"), 1)

            all_sequences(act, pre, scan, post)

        @block.tensor
        def _(pe):
            for steps in (pre_pe, scan_sum, post_pe):
                steps.credit(pe)
            pe.wait_ge(consts, 14)
            pe.wait_ge(weights_in, 16 * len(DMA_IN))

            def turn(src, banks):
                for c in range(KD):
                    for tile in range(TT):
                        last = pe.transpose(banks[c][:, tile * P:(tile + 1) * P], src[:, tile, c * P:(c + 1) * P],
                                            ident[:, :])
                return last

            def token_major(srcT, w, K, tiles=range(TT)):
                for tile in tiles:
                    for c in range(K):
                        last = pe.matmul(PB[tile // 2][:, (tile % 2) * D:(tile % 2 + 1) * D],
                                         srcT[:, c, tile * P:(tile + 1) * P], w[:, c, :], start=c == 0, stop=c == K - 1)
                return last

            def pre(b, par):
                yield
                pe.wait_ge(*pre_dve.at("x_normed", b))
                turn(xin[par], RB).then_inc(pre_pe.did("xT"), 1)
                yield
                for m in range(2 * KI):
                    name = f"u{m}" if m < KI else f"g{m - KI}"
                    if m == 0:
                        pe.wait_ge(*pre_act.at("xT", b))
                    elif 2 <= m < KI + 2:
                        pe.wait_ge(*pre_dve.at(f"conv{m - 2}_2", b))
                    elif m >= KI + 2:
                        pe.wait_ge(*pre_act.at(f"g{m - KI - 2}", b))
                    for c in range(KD):
                        last = pe.matmul(RB[m % 2][:, :], in_w[:, c, m * P:(m + 1) * P], xT[par][:, c, :],
                                         start=c == 0, stop=c == KD - 1)
                    last.then_inc(pre_pe.did(name), 1)
                    if m < KI or m % 2 == 1:
                        yield
                pe.wait_ge(*pre_act.at("g2", b))
                for c in range(KI):
                    last = pe.matmul(RB[0][0:NX, :], xp_w[:, c, :], u[par][:, c, :], start=c == 0, stop=c == KI - 1)
                last.then_inc(pre_pe.did("xd"), 1)
                yield
                for c in range(KI):
                    if c == 0:
                        pe.wait_ge(*pre_act.at("g3", b))
                        pe.wait_ge(*pre_dve.at("xd", b))
                    elif c >= 2:
                        pe.wait_ge(*pre_dve.at(f"z{c - 2}", b))
                    pe.matmul(RB[(c + 1) % 2][:, :], dt_w[:, c * P:(c + 1) * P], xd[0:R, :], start=True, stop=True)\
                        .then_inc(pre_pe.did(f"dt{c}"), 1)
                    if c % 2 == 1:
                        yield

            def scan(b, par, post_stage, pre_stage):
                def add_states(k):
                    pair, c = k // KI, k % KI
                    if pair == 0:
                        pe.wait_ge(*post_dve.at(f"y_a{c}", b - 1))
                    pe.wait_ge(*scan_hc.at(k, b))
                    for j in range(2):
                        last = pe.matmul(Y[c][:, :], ident[:, :], st[k % RING][:, j, :],
                                         start=pair == 0 and j == 0, stop=pair == NP2 - 1 and j == 1)
                    last.then_inc(scan_sum.did(k), 1)

                def unit(k):
                    if k >= 1:
                        add_states(k - 1)
                run_stages(unit, post_stage, pre_stage, b)
                add_states(NU - 1)

            def post(b, par):
                yield
                yield
                pe.wait_ge(*post_dve.at("y_b3", b))
                token_major(u[par], out_w, KI).then_inc(post_pe.did("m"), 1)
                yield
                pe.wait_ge(*post_dve.at("h_normed", b))
                turn(h, PB).then_inc(post_pe.did("hT"), 1)
                pe.wait_ge(*post_act.at("hT", b))
                token_major(F, q_w, KD).then_inc(post_pe.did("q"), 1)
                yield
                pe.wait_ge(*post_dve.at("q_sum", b))
                for m in range(KD):
                    for c in range(KD):
                        last = pe.matmul(PB[m][:, :], k_w[:, c, m * P:(m + 1) * P], F[:, c, :],
                                         start=c == 0, stop=c == KD - 1)
                last.then_inc(post_pe.did("k"), 1)
                yield
                pe.wait_ge(*post_act.at("k_sq", b))
                for tile in range(TT):
                    for c in range(KD):
                        last = pe.matmul(PB[0][:, tile:tile + 1], ksq[:, c, tile * P:(tile + 1) * P], ones[:, 0:1],
                                         start=c == 0, stop=c == KD - 1)
                last.then_inc(post_pe.did("ssk"), 1)
                yield
                yield
                pe.wait_ge(*post_dve.at("qw2", b))
                for c in range(KD):
                    for tile in range(TT):
                        pe.matmul(PB[1][:, c:c + 1], q[:, tile, c * P:(c + 1) * P], qw[:, tile:tile + 1],
                                  start=tile == 0, stop=tile == TT - 1)
                pe.matmul(PB[1][:, 8:8 + TT], ones[:, :], qw2[:, :], start=True, stop=True)\
                    .then_inc(post_pe.did("G"), 1)
                yield
                pe.wait_ge(*post_dve.at("proj_g", b))
                token_major(kT, proj_g, KD).then_inc(post_pe.did("hs"), 1)
                yield
                yield
                pe.wait_ge(*post_pool.at("t_li", b))
                turn(tb, PB).then_inc(post_pe.did("tT"), 1)
                yield
                pe.wait_ge(*post_act.at("tT", b))
                token_major(F, fl_w, KD).then_inc(post_pe.did("fl"), 1)
                yield
                pe.wait_ge(*post_dve.at("s_normed", b))
                turn(s, PB).then_inc(post_pe.did("sT"), 1)
                yield
                for j in range(KF):
                    if j == 0:
                        pe.wait_ge(*post_act.at("sT", b))
                    elif j >= 2:
                        pe.wait_ge(*post_act.at(f"gelu{j - 2}", b))
                    for c in range(KD):
                        last = pe.matmul(PB[j % 2][:, :], d1_w[:, c, j * P:(j + 1) * P], F[:, c, :],
                                         start=c == 0, stop=c == KD - 1)
                    last.then_inc(post_pe.did(f"d1_{j}"), 1)
                    if j % 2 == 1:
                        yield
                pe.wait_ge(*post_act.at(f"gelu{KF - 1}", b))
                token_major(gT, d2_w, KF, (0, 1)).then_inc(post_pe.did("d2_0"), 1)
                yield
                token_major(gT, d2_w, KF, (2, 3)).then_inc(post_pe.did("d2_1"), 1)
                for _ in range(6):
                    yield
                pe.wait_ge(*post_dve.at("n_normed", b))
                turn(tb, PB).then_inc(post_pe.did("nT"), 1)
                pe.wait_ge(*post_act.at("nT", b))
                for tile in range(TT):
                    for c in range(KD):
                        last = pe.matmul(PB[0][:, tile * NE:(tile + 1) * NE], F[:, c, tile * P:(tile + 1) * P],
                                         emb[:, c, :], start=c == 0, stop=c == KD - 1)
                last.then_inc(post_pe.did("dots"), 1)
                yield
                yield
                pe.wait_ge(*post_dve.at("asg", b))
                for tile in range(TT):
                    dst = PB[1][:, tile * NE:(tile + 1) * NE]
                    for before in range(tile):
                        pe.matmul(dst, ones_bf[:, :], asg[:, before, :], start=before == 0, stop=False)
                    pe.matmul(dst, tri[:, :], asg[:, tile, :], start=tile == 0, stop=True)
                for tile in range(TT):
                    last = pe.matmul(PB[1][:, TT * NE:(TT + 1) * NE], ones_bf[:, :], asg[:, tile, :],
                                     start=tile == 0, stop=tile == TT - 1)
                last.then_inc(post_pe.did("cum"), 1)

            all_sequences(pe, pre, scan, post)

        @block.vector
        def _(dve):
            dve.memset(gT_flat, 0.0).then_inc(zero_tile, 1)
            for steps in (pre_dve, scan_in, scan_h, post_dve):
                steps.credit(dve)
            dve.wait_ge(consts, 14)
            dve.wait_ge(weights_in, 16 * len(DMA_IN))
            dve.tensor_tensor(d2_row[:, :], d2_row[:, :], s[:, 0, :], ALU.add).then_inc(setup_dve, 1)
            dve.wait_ge(setup_act, 1)
            dve.tensor_scalar(a_neg[:, :, :], a_neg[:, :, :], -1.0, None, ALU.mult).then_inc(setup_dve, 1)

            def stats(steps, name, src, stat_t, mv_t, b):
                for tile in range(TT):
                    last = dve.bn_stats(stat_t[:, tile, :], src[:, tile, :])
                last.then_inc(steps.did(f"{name}_stats"), 1)
                dve.wait_ge(*steps.at(f"{name}_stats", b))
                dve.sem_inc(carried_dve, 1)
                for tile in range(TT):
                    last = dve.bn_aggr(mv_t[:, tile, :], stat_t[:, tile, :])
                last.then_inc(steps.did(f"{name}_aggr"), 1)

            def normalise(dst, src, mv_t, r_t):
                for tile in range(TT):
                    last = dve.tensor_scalar(dst[:, tile, :], src[:, tile, :], mv_t[:, tile, 0:1],
                                             r_t[:, tile:tile + 1], ALU.subtract, ALU.mult)
                return last

            def pre(b, par):
                dve.wait_ge(x_loaded, 16 * (b + 1))
                stats(pre_dve, "x", xin[par], stat_pre, mv_pre, b)
                yield
                dve.wait_ge(*pre_act.at("x_r", b))
                normalise(xin[par], xin[par], mv_pre, r_pre).then_inc(pre_dve.did("x_normed"), 1)
                yield
                for c in range(KI):
                    for j in range(3):
                        if j == 0:
                            dve.wait_ge(*pre_act.at(f"tap{c}", b))
                        else:
                            dve.wait_ge(*pre_dve.at(f"conv{c}_{j - 1}", b))
                        late = u[par][:, c, j + 1:L]
                        dve.scalar_tensor_tensor(late, RB[c % 2][:, 0:L - 1 - j], conv_w[:, c, 2 - j:3 - j], late,
                                                 ALU.mult, ALU.add).then_inc(pre_dve.did(f"conv{c}_{j}"), 1)
                    yield
                yield
                yield
                dve.wait_ge(*pre_pe.at("xd", b))
                dve.wait_ge(xd_stored, 16 * b)
                dve.tensor_copy(xd[:, :], RB[0][0:NX, :]).then_inc(pre_dve.did("xd"), 1)
                yield
                for c in range(KI):
                    dve.wait_ge(*pre_pe.at(f"dt{c}", b))
                    dve.tensor_scalar(delta[par][:, c, :], RB[(c + 1) % 2][:, :], dt_b[:, c:c + 1], None, ALU.add)\
                        .then_inc(pre_dve.did(f"z{c}"), 1)
                    if c % 2 == 1:
                        yield
                yield
                for c in range(KI):
                    if c == 0:
                        dve.wait_ge(*pre_act.at("sp_exp", b))
                    else:
                        dve.wait_ge(*pre_pool.at(f"log1p{c - 1}", b))
                    dve.tensor_scalar(rest[:, :], du[par][:, c, :], 1.0, 1.0, ALU.add, ALU.subtract)\
                        .then_inc(pre_dve.did(f"w{c}"), 1)
                    yield
                dve.wait_ge(*pre_pool.at("log1p3", b))
                dve.scalar_tensor_tensor(delta[par][:, :, :], delta[par][:, :, :], 0.0, du[par][:, :, :],
                                         ALU.max, ALU.add).then_inc(pre_dve.did("delta"), 1)

            def scan(b, par, post_stage, pre_stage):
                def drive(k):
                    pair, c = k // KI, k % KI
                    if k == 0:
                        dve.wait_ge(*pre_pool.at("du", b))
                    if c == 0:
                        dve.wait_ge(bc_loaded[pair % 2], 16 * (NP2 // 2) * b + 16 * (pair // 2 + 1))
                    dve.wait_ge(*scan_sum.at(NU - RING + k, b - 1) if k < RING else scan_sum.at(k - RING, b))
                    dve.tensor_tensor(st[k % RING][:, :, :],
                                      du[par][:, c, :].unsqueeze(1).to_broadcast([P, 2, L]),
                                      bc[pair % 2][:, 0, :, :], ALU.mult).then_inc(scan_in.did(k), 1)

                def unit(k):
                    if k == 0:
                        drive(0)
                    if k + 1 < NU:
                        drive(k + 1)
                    dve.wait_ge(*scan_exp.at(k, b))
                    dve.wait_ge(*scan_in.at(k, b))
                    flat = st[k % RING][:, :, :].rearrange("p a l -> p (a l)")
                    dve.tensor_tensor_scan(flat, dA[k % 2][:, :, :].rearrange("p a l -> p (a l)"), flat, 0.0,
                                           ALU.mult, ALU.add).then_inc(scan_h.did(k), 1)
                run_stages(unit, post_stage, pre_stage, b)

            def own(name, b):
                return post_dve.at(name, b)

            def post(b, par):
                for c0 in (0, 2):
                    for c in (c0, c0 + 1):
                        dve.wait_ge(*scan_sum.at(NU - KI + c, b))
                        dve.scalar_tensor_tensor(u[par][:, c, :], u[par][:, c, :], d_skip[:, c:c + 1], Y[c][:, :],
                                                 ALU.mult, ALU.add).then_inc(post_dve.did(f"y_a{c}"), 1)
                    for c in (c0, c0 + 1):
                        dve.wait_ge(*own(f"y_a{c}", b))
                        dve.tensor_tensor(u[par][:, c, :], u[par][:, c, :], g[par][:, c, :], ALU.mult)\
                            .then_inc(post_dve.did(f"y_b{c}"), 1)
                    yield
                dve.wait_ge(*post_pe.at("m", b))
                dve.wait_ge(x1_stored, 16 * (b + 1))
                for i in range(2):
                    last = dve.tensor_tensor(h[:, 2 * i:2 * i + 2, :], PB[i][:, :].rearrange("p (a d) -> p a d", a=2),
                                             xin[par][:, 2 * i:2 * i + 2, :], ALU.add)
                last.then_inc(post_dve.did("h_sum"), 1)
                dve.wait_ge(*own("h_sum", b))
                stats(post_dve, "h", h, stat, mv, b)
                yield
                dve.wait_ge(*post_act.at("h_r", b))
                normalise(h, h, mv, r).then_inc(post_dve.did("h_normed"), 1)
                yield
                dve.wait_ge(*post_pe.at("q", b))
                for i in range(2):
                    last = dve.tensor_tensor(q[:, 2 * i:2 * i + 2, :], PB[i][:, :].rearrange("p (a d) -> p a d", a=2),
                                             rows["q_b"][:, :].unsqueeze(1).to_broadcast([P, 2, D]), ALU.add)
                last.then_inc(post_dve.did("q_sum"), 1)
                yield
                dve.wait_ge(*post_act.at("q_sq", b))
                dve.tensor_scalar(ssq[:, :], ssq[:, :], EPS * EPS, None, ALU.max).then_inc(post_dve.did("ssq"), 1)
                yield
                dve.wait_ge(*post_pe.at("ssk", b))
                dve.tensor_scalar(ssk[:, :], PB[0][:, 0:TT], EPS * EPS, None, ALU.max)\
                    .then_inc(post_dve.did("ssk"), 1)
                dve.wait_ge(*post_pool.at("h_b", b))
                stats(post_dve, "hi", h, stat, mv, b)
                yield
                dve.wait_ge(*post_act.at("q_gelu", b))
                for tile in range(TT):
                    last = dve.tensor_tensor_reduce(out=junk_dve[:, tile, :], in0=q[:, tile, :], in1=rows["w_g"][:, :],
                                                    scale=D ** -0.5, scalar=0.0, op0=ALU.mult, op1=ALU.add,
                                                    accum_out=qw[:, tile:tile + 1])
                last.then_inc(post_dve.did("qw"), 1)
                dve.wait_ge(*own("qw", b))
                dve.tensor_tensor(qw2[:, :], qw[:, :], qw[:, :], ALU.mult).then_inc(post_dve.did("qw2"), 1)
                dve.wait_ge(*post_pe.at("G", b))
                dve.tensor_reduce(ssg[:, :], PB[1][:, 8:8 + TT], AX_X, ALU.add).then_inc(post_dve.did("ssg_sum"), 1)
                dve.wait_ge(*own("ssg_sum", b))
                dve.tensor_scalar(ssg[:, :], ssg[:, :], EPS * EPS, None, ALU.max).then_inc(post_dve.did("ssg"), 1)
                yield
                dve.wait_ge(*post_act.at("hi_r", b))
                normalise(li, h, mv, r).then_inc(post_dve.did("li"), 1)
                dve.wait_ge(*post_act.at("G_r", b))
                dve.tensor_scalar(gcol[:, :], PB[1][:, 0:KD], rg[:, 0:1], None, ALU.mult)\
                    .then_inc(post_dve.did("G"), 1)
                dve.wait_ge(*own("G", b))
                for c in range(KD):
                    last = dve.tensor_scalar(proj_g[:, c, :], pr_w[:, c, :], gcol[:, c:c + 1], None, ALU.mult)
                last.then_inc(post_dve.did("proj_g"), 1)
                yield
                dve.wait_ge(*post_pe.at("hs", b))
                dve.wait_ge(*post_pool.at("sent", b - 1))
                for tile in range(TT):
                    last = dve.scalar_tensor_tensor(tb[:, tile, :], PB[tile // 2][:, (tile % 2) * D:(tile % 2 + 1) * D],
                                                    rk[:, tile:tile + 1], rows["pr_b"][:, :], ALU.mult, ALU.add)
                last.then_inc(post_dve.did("t"), 1)
                yield
                yield
                dve.wait_ge(*post_pe.at("fl", b))
                dve.wait_ge(*post_pool.at("h_fl", b))
                for i in range(2):
                    last = dve.tensor_tensor(s[:, 2 * i:2 * i + 2, :], PB[i][:, :].rearrange("p (a d) -> p a d", a=2),
                                             h[:, 2 * i:2 * i + 2, :], ALU.add)
                last.then_inc(post_dve.did("s_sum"), 1)
                dve.wait_ge(*own("s_sum", b))
                stats(post_dve, "s", s, stat, mv, b)
                yield
                dve.wait_ge(*post_act.at("s_r", b))
                normalise(s, s, mv, r).then_inc(post_dve.did("s_normed"), 1)
                for _ in range(6):
                    yield
                for i in range(2):
                    dve.wait_ge(*post_pe.at(f"d2_{i}", b))
                    if i == 0:
                        dve.wait_ge(*post_pool.at("s_b", b))
                    part_s = s[:, 2 * i:2 * i + 2, :]
                    dve.tensor_tensor(part_s, PB[i][:, :].rearrange("p (a d) -> p a d", a=2), part_s, ALU.add)\
                        .then_inc(post_dve.did(f"f_sum{i}"), 1)
                dve.wait_ge(*own("f_sum1", b))
                stats(post_dve, "f", s, stat, mv, b)
                yield
                dve.wait_ge(*post_act.at("f_r", b))
                normalise(s, s, mv, r).then_inc(post_dve.did("f_normed"), 1)
                yield
                yield
                dve.wait_ge(*post_pool.at("f_b", b))
                stats(post_dve, "o", s, stat, mv, b)
                yield
                dve.wait_ge(*post_act.at("o_r", b))
                normalise(s, s, mv, r).then_inc(post_dve.did("o_normed"), 1)
                yield
                dve.wait_ge(*post_pool.at("x1", b))
                stats(post_dve, "n", h, stat, mv, b)
                yield
                dve.wait_ge(*post_act.at("n_r", b))
                normalise(tb, h, mv, r).then_inc(post_dve.did("n_normed"), 1)
                yield
                dve.wait_ge(*post_pe.at("dots", b))
                dve.tensor_copy(dots[:, :, :], PB[0][:, 0:TT * NE].rearrange("p (t e) -> p t e", t=TT))\
                    .then_inc(post_dve.did("dots"), 1)
                dve.wait_ge(*own("dots", b))
                dve.sem_inc(carried_dve, 1)
                for tile in range(TT):
                    last = dve.max(top[:, tile, :], dots[:, tile, :])
                last.then_inc(post_dve.did("top"), 1)
                dve.wait_ge(*own("top", b))
                dve.sem_inc(carried_dve, 1)
                for tile in range(TT):
                    last = dve.max_index(top_i[:, tile, :], top[:, tile, :], dots[:, tile, :])
                last.then_inc(post_dve.did("top_i"), 1)
                dve.tensor_tensor(dv[:, :], top[:, :, 1], top[:, :, 0], ALU.subtract).then_inc(post_dve.did("dv"), 1)
                dve.wait_ge(*own("top_i", b))
                dve.tensor_copy(top_f[:, :, :], top_i[:, :, 0:2]).then_inc(post_dve.did("top_f"), 1)
                yield
                dve.wait_ge(*post_act.at("e2", b))
                dve.tensor_scalar(den[:, :], e2[:, :], 1.0, None, ALU.add).then_inc(post_dve.did("den"), 1)
                dve.wait_ge(*own("den", b))
                dve.reciprocal(wts[:, :, 0], den[:, :]).then_inc(post_dve.did("w1"), 1)
                dve.wait_ge(*own("w1", b))
                dve.tensor_tensor(wts[:, :, 1], e2[:, :], wts[:, :, 0], ALU.mult).then_inc(post_dve.did("w2"), 1)
                dve.wait_ge(*own("w2", b))
                dve.tensor_scalar(pos2[:, :], wts[:, :, 1], 0.0, None, ALU.is_gt).then_inc(post_dve.did("pos2"), 1)
                for i in range(2):
                    dve.tensor_tensor(oh[i][:, :, :], iota8[:, :].unsqueeze(1).to_broadcast([P, TT, NE]),
                                      top_f[:, :, i:i + 1].to_broadcast([P, TT, NE]), ALU.is_equal)\
                        .then_inc(post_dve.did(f"oh{i}"), 1)
                dve.wait_ge(*own("oh1", b))
                dve.tensor_tensor(oh[1][:, :, :], oh[1][:, :, :], pos2[:, :].unsqueeze(2).to_broadcast([P, TT, NE]),
                                  ALU.mult).then_inc(post_dve.did("oh1_pos"), 1)
                dve.wait_ge(*own("oh1_pos", b))
                dve.tensor_tensor(asg[:, :, :], oh[0][:, :, :], oh[1][:, :, :], ALU.add)\
                    .then_inc(post_dve.did("asg"), 1)
                yield
                dve.wait_ge(*post_pe.at("cum", b))
                dve.tensor_tensor(cum[:, :, :], PB[1][:, 0:TT * NE].rearrange("p (t e) -> p t e", t=TT),
                                  run[:, :].unsqueeze(1).to_broadcast([P, TT, NE]), ALU.add)\
                    .then_inc(post_dve.did("cum"), 1)
                dve.wait_ge(*own("cum", b))
                dve.tensor_scalar(keep[:, :, :], cum[:, :, :], float(CAP), None, ALU.is_le)\
                    .then_inc(post_dve.did("keep"), 1)
                dve.tensor_tensor(run[:, :], PB[1][:, TT * NE:(TT + 1) * NE], run[:, :], ALU.add)\
                    .then_inc(post_dve.did("run"), 1)
                dve.tensor_tensor(cum[:, :, :], cum[:, :, :], slot0[:, :].unsqueeze(1).to_broadcast([P, TT, NE]),
                                  ALU.add).then_inc(post_dve.did("slotv"), 1)
                dve.wait_ge(*own("slotv", b))
                dve.tensor_tensor(cum[:, :, :], cum[:, :, :], keep[:, :, :], ALU.mult)\
                    .then_inc(post_dve.did("slotk"), 1)
                dve.wait_ge(*own("slotk", b))
                for i in range(2):
                    dve.tensor_tensor(pick[i][:, :, :], cum[:, :, :], oh[i][:, :, :], ALU.mult)\
                        .then_inc(post_dve.did(f"pick{i}"), 1)
                for i in range(2):
                    dve.wait_ge(*own(f"pick{i}", b))
                    dve.tensor_reduce(slot_f[:, :, i], pick[i][:, :, :], AX_X, ALU.add)\
                        .then_inc(post_dve.did(f"slot{i}"), 1)
                dve.wait_ge(*own("slot1", b))
                dve.tensor_scalar(idx[:, :, :], slot_f[:, :, :], FAR, None, ALU.add).then_inc(post_dve.did("idx"), 1)
                dve.wait_ge(*own("idx", b))
                dve.tensor_copy(idx_all[:, bass.ds(b * TT, TT), :], idx[:, :, :]).then_inc(post_dve.did("idx_all"), 1)
                dve.tensor_copy(w_all[:, bass.ds(b * TT, TT), :], wts[:, :, :]).then_inc(post_dve.did("w_all"), 1)

            for _ in pre(0, 0):
                pass
            dve.wait_ge(zeroed, 16 * xe_zero_v.shape[0])
            pre_done = pre
            first = [True]

            def pre_after_first(b, par):
                if first[0]:
                    first[0] = False
                    return iter(())
                return pre_done(b, par)

            all_sequences(dve, pre_after_first, scan, post)


def expert_phase(nc, t, env, sem):
    D, NE, EI, KD, KE, CAP, TB, QB, BLK = (env[k] for k in ("D", "NE", "EI", "KD", "KE", "CAP", "TB", "QB", "BLK"))
    ident, bank, xe_v, ye_v = (env[k] for k in ("ident", "bank", "xe_v", "ye_v"))
    NB = 2 * QB
    with ExitStack() as ctx:
        def sb(name, shape, dt=F32):
            return ctx.enter_context(nc.sbuf_tensor(name, shape, dt))

        w1 = [sb(f"w1_{i}", [P, KD, EI]) for i in range(2)]
        w2 = [sb(f"w2_{i}", [P, KE, D]) for i in range(2)]
        X = [sb(f"X{i}", [P, TB, D]) for i in range(2)]
        XT = [sb(f"XT{i}", [P, KD, BLK]) for i in range(2)]
        I = [sb(f"I{i}", [P, KE, BLK]) for i in range(2)]
        O = [sb(f"O{i}", [P, TB, D]) for i in range(2)]
        XB, MB, OB = bank[0:2], bank[2:6], bank[6:8]

        carried_sp_e = sem("carried_sp_e")
        w_loaded = [sem(f"w_loaded{i}") for i in range(2)]
        slots_loaded = [sem(f"slots_loaded{i}") for i in range(2)]
        stored = [sem(f"stored{i}") for i in range(2)]
        e_turn = Steps(sem("e_turn"), range(NB))
        e_turned = Steps(sem("e_turned"), range(NB))
        e_mm1 = Steps(sem("e_mm1"), range(NB * KE))
        e_relu_act = Steps(sem("e_relu_act"), range(NB * KE // 2))
        e_relu_dve = Steps(sem("e_relu_dve"), range(NB * KE // 2))
        e_mm2 = Steps(sem("e_mm2"), range(NB))
        e_out = Steps(sem("e_out"), range(NB))

        def before(steps, n, back, i):
            return steps.at(n - back, i) if n >= back else steps.at(len(steps.names) + n - back, i - 1)

        block = ctx.enter_context(nc.Block())

        @block.sync
        def _(sp):
            with sp.Fori(0, NE // 2) as i:
                for n in range(NB):
                    e, q = divmod(n, QB)
                    if q == 0:
                        sp.wait_ge(*e_mm2.at(n + QB - 1, i - 1))
                        sp.sem_inc(carried_sp_e, 1)
                        sp.dma_start(w1[e][:, :, :], t["e1_w"][2 * i + e].rearrange("(k p) n -> p k n", p=P))\
                            .then_inc(w_loaded[e], 16)
                        sp.dma_start(w2[e][:, :, :], t["e2_w"][2 * i + e].rearrange("(k p) n -> p k n", p=P))\
                            .then_inc(w_loaded[e], 16)
                    sp.wait_ge(*before(e_turn, n, 2, i))
                    sp.sem_inc(carried_sp_e, 1)
                    sp.dma_start(X[n % 2][:, :, :], xe_v[i * NB + n]).then_inc(slots_loaded[n % 2], 16)

        @block.tensor
        def _(pe):
            for steps in (e_turn, e_mm1, e_mm2):
                steps.credit(pe)

            def turn(n, i):
                pe.wait_ge(slots_loaded[n % 2], 16 * (NB // 2) * i + 16 * (n // 2 + 1))
                pe.wait_ge(*before(e_turned, n, 1, i))
                for c in range(KD):
                    for tile in range(TB):
                        last = pe.transpose(XB[c][:, tile * P:(tile + 1) * P], X[n % 2][:, tile, c * P:(c + 1) * P],
                                            ident[:, :])
                last.then_inc(e_turn.did(n), 1)

            with pe.Fori(0, NE // 2) as i:
                turn(0, i)
                for n in range(NB):
                    e = n // QB
                    if n % QB == 0:
                        pe.wait_ge(w_loaded[e], 32 * (i + 1))
                    pe.wait_ge(*e_turned.at(n, i))
                    for m in range(KE):
                        relu = e_relu_act if m % 2 == 0 else e_relu_dve
                        pe.wait_ge(*before(relu, n * KE // 2 + m // 2, KE // 2, i))
                        for c in range(KD):
                            last = pe.matmul(MB[m][:, 0:BLK], w1[e][:, c, m * P:(m + 1) * P], XT[n % 2][:, c, :],
                                             start=c == 0, stop=c == KD - 1)
                        last.then_inc(e_mm1.did(n * KE + m), 1)
                    if n + 1 < NB:
                        turn(n + 1, i)
                    pe.wait_ge(*e_relu_act.at(n * KE // 2 + KE // 2 - 1, i))
                    pe.wait_ge(*e_relu_dve.at(n * KE // 2 + KE // 2 - 1, i))
                    pe.wait_ge(*before(e_out, n, 1, i))
                    for tile in range(TB):
                        for c in range(KE):
                            last = pe.matmul(OB[tile // 2][:, (tile % 2) * D:(tile % 2 + 1) * D],
                                             I[n % 2][:, c, tile * P:(tile + 1) * P], w2[e][:, c, :],
                                             start=c == 0, stop=c == KE - 1)
                    last.then_inc(e_mm2.did(n), 1)

        @block.scalar
        def _(act):
            for steps in (e_turned, e_relu_act):
                steps.credit(act)
            for half in range(2):
                act.sem_inc(stored[half], 16)
            with act.Fori(0, NE // 2) as i:
                def copy_turned(n):
                    act.wait_ge(*e_turn.at(n, i))
                    act.wait_ge(*before(e_mm1, n * KE + KE - 1, 2 * KE, i))
                    for c in range(KD):
                        last = act.copy(XT[n % 2][:, c, :], XB[c][:, 0:BLK])
                    last.then_inc(e_turned.did(n), 1)

                copy_turned(0)
                for n in range(NB):
                    act.wait_ge(*before(e_mm2, n, 2, i))
                    for m in range(0, KE, 2):
                        act.wait_ge(*e_mm1.at(n * KE + m, i))
                        act.activation(I[n % 2][:, m, :], MB[m][:, 0:BLK], ACT.Relu)\
                            .then_inc(e_relu_act.did(n * KE // 2 + m // 2), 1)
                    if n + 1 < NB:
                        copy_turned(n + 1)
                    act.wait_ge(*e_out.at(n, i))
                    act.dma_start(ye_v[i * NB + n], O[n % 2][:, :, :]).then_inc(stored[n % 2], 16)
            for half in range(2):
                act.wait_ge(stored[half], 16 * (NE // 2) * (NB // 2) + 16)

        @block.vector
        def _(dve):
            for steps in (e_relu_dve, e_out):
                steps.credit(dve)
            with dve.Fori(0, NE // 2) as i:
                for n in range(NB):
                    dve.wait_ge(*before(e_mm2, n, 2, i))
                    for m in range(1, KE, 2):
                        dve.wait_ge(*e_mm1.at(n * KE + m, i))
                        dve.tensor_scalar(I[n % 2][:, m, :], MB[m][:, 0:BLK], 0.0, None, ALU.max)\
                            .then_inc(e_relu_dve.did(n * KE // 2 + m // 2), 1)
                    dve.wait_ge(*e_mm2.at(n, i))
                    dve.wait_ge(stored[n % 2], 16 * (NB // 2) * i + 16 * (n // 2 + 1))
                    for tile in range(0, TB, 2):
                        last = dve.tensor_copy(O[n % 2][:, tile:tile + 2, :],
                                               OB[tile // 2][:, :].rearrange("p (a d) -> p a d", a=2))
                    last.then_inc(e_out.did(n), 1)


def combine_phase(nc, t, env, sem):
    S, D, TT, NSLOT = (env[k] for k in ("S", "D", "TT", "NSLOT"))
    idx_all, w_all, eps5, ye_dram, x1_v, out_v = (
        env[k] for k in ("idx_all", "w_all", "eps5", "ye_dram", "x1_v", "out_v"))
    with ExitStack() as ctx:
        def sb(name, shape, dt=F32):
            return ctx.enter_context(nc.sbuf_tensor(name, shape, dt))

        rows = [[sb(f"rows{i}_{c}", [P, TT, D]) for c in range(2)] for i in range(2)]
        idx_c = [sb(f"idx_c{i}", [P, TT, 2], U32) for i in range(2)]
        w_c = [sb(f"w_c{i}", [P, TT, 2]) for i in range(2)]
        x1 = [sb(f"x1_{i}", [P, TT, D]) for i in range(2)]
        stat = [sb(f"c_stat{i}", [P, TT, 6]) for i in range(2)]
        mv = [sb(f"c_mv{i}", [P, TT, 2]) for i in range(2)]
        r = [sb(f"c_r{i}", [P, TT]) for i in range(2)]

        gathered = [sem(f"gathered{i}") for i in range(2)]
        gathers_begun = sem("gathers_begun")
        carried = sem("carried")
        carried_sp_c = sem("carried_sp_c")
        x1_loaded = [sem(f"x1_loaded{i}") for i in range(2)]
        out_stored = [sem(f"out_stored{i}") for i in range(2)]
        ready = Steps(sem("c_ready"), range(2))
        dve_s = Steps(sem("c_dve"), [f"{n}{par}" for par in range(2) for n in
                                     ("scaled", "sum", "stats", "aggr", "normed", "out")])
        act_s = Steps(sem("c_act"), [f"{n}{par}" for par in range(2) for n in ("ln", "r")])
        block = ctx.enter_context(nc.Block())

        @block.sync
        def _(sp):
            for par in range(2):
                sp.sem_inc(out_stored[par], 16)
            with sp.Fori(0, S // 2) as i:
                for par in range(2):
                    sp.wait_ge(out_stored[par], 16 * (i + 1))
                    sp.sem_inc(carried_sp_c, 1)
                    sp.dma_start(x1[par][:, :, :], x1_v[2 * i + par]).then_inc(x1_loaded[par], 16)
                    if par == 1:
                        for half in range(2):
                            sp.wait_ge(*dve_s.at(f"out{half}", i))
                            sp.sem_inc(carried_sp_c, 1)
                            sp.dma_start(out_v[2 * i + half], x1[half][:, :, :]).then_inc(out_stored[half], 16)
            for par in range(2):
                sp.wait_ge(out_stored[par], 16 * (S // 2 + 1))

        @block.gpsimd
        def _(pool):
            with pool.Fori(0, S // 2) as i:
                for par in range(2):
                    pool.wait_ge(*ready.at(par, i))
                    pool.sem_inc(gathers_begun, 1)
                    for tile in range(TT):
                        for c in range(2):
                            pool.indirect_dma_start(
                                out=rows[par][c][:, tile, :], out_offset=None, in_=ye_dram,
                                in_offset=bass.IndirectOffsetOnAxis(ap=idx_c[par][:, tile, c:c + 1], axis=0),
                                bounds_check=NSLOT - 1, oob_is_err=False).then_inc(gathered[par], 16)

        @block.scalar
        def _(act):
            act_s.credit(act)
            with act.Fori(0, S // 2) as i:
                for par in range(2):
                    act.wait_ge(*dve_s.at(f"aggr{par}", i))
                    act.activation(r[par][:, :], mv[par][:, :, 1], ACT.Ln, bias=eps5[:, 0:1])\
                        .then_inc(act_s.did(f"ln{par}"), 1)
                    act.wait_ge(*act_s.at(f"ln{par}", i))
                    act.activation(r[par][:, :], r[par][:, :], ACT.Exp, scale=-0.5).then_inc(act_s.did(f"r{par}"), 1)

        @block.vector
        def _(dve):
            for steps in (ready, dve_s):
                steps.credit(dve)

            def prepare(par, i):
                dve.wait_ge(*dve_s.at(f"out{par}", i - 1))
                for c in range(2):
                    dve.memset(rows[par][c][:, :, :], 0.0)
                dve.tensor_copy(w_c[par][:, :, :], w_all[:, bass.ds((2 * i + par) * TT, TT), :])
                dve.tensor_copy(idx_c[par][:, :, :], idx_all[:, bass.ds((2 * i + par) * TT, TT), :])\
                    .then_inc(ready.did(par), 1)

            def combine(par, i):
                a, b = rows[par]
                dve.wait_ge(gathered[par], 16 * 2 * TT * (i + 1))
                dve.wait_ge(*ready.at(par, i))
                for tile in range(TT):
                    last = dve.tensor_scalar(a[:, tile, :], a[:, tile, :], w_c[par][:, tile, 0:1], None, ALU.mult)
                last.then_inc(dve_s.did(f"scaled{par}"), 1)
                dve.wait_ge(*dve_s.at(f"scaled{par}", i))
                for tile in range(TT):
                    last = dve.scalar_tensor_tensor(a[:, tile, :], b[:, tile, :], w_c[par][:, tile, 1:2],
                                                    a[:, tile, :], ALU.mult, ALU.add)
                last.then_inc(dve_s.did(f"sum{par}"), 1)
                dve.wait_ge(*dve_s.at(f"sum{par}", i))
                for tile in range(TT):
                    last = dve.bn_stats(stat[par][:, tile, :], a[:, tile, :])
                last.then_inc(dve_s.did(f"stats{par}"), 1)
                dve.wait_ge(*dve_s.at(f"stats{par}", i))
                dve.sem_inc(carried, 1)
                for tile in range(TT):
                    last = dve.bn_aggr(mv[par][:, tile, :], stat[par][:, tile, :])
                last.then_inc(dve_s.did(f"aggr{par}"), 1)
                dve.wait_ge(*act_s.at(f"r{par}", i))
                for tile in range(TT):
                    last = dve.tensor_scalar(a[:, tile, :], a[:, tile, :], mv[par][:, tile, 0:1],
                                             r[par][:, tile:tile + 1], ALU.subtract, ALU.mult)
                last.then_inc(dve_s.did(f"normed{par}"), 1)
                dve.wait_ge(*dve_s.at(f"normed{par}", i))
                dve.wait_ge(x1_loaded[par], 16 * (i + 1))
                dve.tensor_tensor(x1[par][:, :, :], x1[par][:, :, :], a[:, :, :], ALU.add)\
                    .then_inc(dve_s.did(f"out{par}"), 1)

            for par in range(2):
                prepare(par, 0)
            with dve.Fori(0, S // 2 - 1) as i:
                for par in range(2):
                    combine(par, i)
                    prepare(par, i + 1)
            for par in range(2):
                combine(par, S // 2 - 1)


def kernel(**inputs):
    import numpy as _np
    import concourse.bacc as _bacc
    from concourse import mybir as _mybir
    from concourse.bass_utils import run_bass_kernel_spmd as _run

    def a(name):
        return _np.asarray(inputs[f"L0_attn_{name}"])

    def f(name):
        return _np.asarray(inputs[f"L0_ffn_{name}"])

    host = {"x": a("input_tensor"), "in_w": a("in_proj_w").T, "conv_w": a("conv_w"), "conv_b": a("conv_b"),
            "xp_w": a("x_proj_w").T, "dt_w": a("dt_proj_w").T, "dt_b": a("dt_proj_b"), "A_log": a("A_log"),
            "D_skip": a("D_skip"), "out_w": a("out_proj_w").T, "ln0_g": a("ln0_g"), "ln0_b": a("ln0_b"),
            "q_w": a("q_w").T, "q_b": a("q_b"), "k_w": a("k_w").T, "k_b": a("k_b"), "w_g": a("w_g").reshape(-1),
            "pr_w": a("proj_w").T, "pr_b": a("proj_b"), "fl_w": a("fl_w").T, "fl_b": a("fl_b"),
            "lni_g": a("lni_g"), "lni_b": a("lni_b"), "ln1_g": a("ln1_g"), "ln1_b": a("ln1_b"),
            "d1_w": a("d1_w").T, "d1_b": a("d1_b"), "d2_w": a("d2_w").T, "d2_b": a("d2_b"),
            "ln2_g": a("ln2_g"), "ln2_b": a("ln2_b"), "emb": f("expert_embeddings").T,
            "e1_w": f("first_linear").transpose(0, 2, 1), "e2_w": f("second_linear").transpose(0, 2, 1)}
    nc = _bacc.Bacc("TRN2", target_bir_lowering=False, num_devices=1)
    arrays, t = {}, {}
    for name, value in host.items():
        value = _np.ascontiguousarray(value)
        arrays[f"in_{name}"] = value
        t[name] = nc.dram_tensor(f"in_{name}", value.shape, _mybir.dt.from_np(value.dtype), kind="ExternalInput").ap()
    t["out"] = nc.dram_tensor("out_0", host["x"].shape, _mybir.dt.float32, kind="ExternalOutput").ap()
    build(nc, t)
    result = _run(nc, [arrays], core_ids=[0])
    return result.results[0]["out_0"]
```

```python
from contextlib import ExitStack

import concourse.bass as bass
from concourse import mybir

ALU = mybir.AluOpType
ACT = mybir.ActivationFunctionType
F32 = mybir.dt.float32
BF16 = mybir.dt.bfloat16
U32 = mybir.dt.uint32
AX_X = mybir.AxisListType.X

P = 128
LEAD = 2
LN_EPS = 1e-5
EPS = 1e-12


class Steps:

    def __init__(self, sem, names):
        self.sem, self.names, self.next = sem, list(names), 0

    def did(self, name):
        assert self.names[self.next % len(self.names)] == name, (name, self.names[self.next % len(self.names)])
        self.next += 1
        return self.sem

    def value(self, index, n):
        return (n + LEAD) * len(self.names) + index + 1

    def at(self, name, n):
        return self.sem, self.value(self.names.index(name), n)

    def credit(self, engine):
        engine.sem_inc(self.sem, LEAD * len(self.names))


class Stage:

    def __init__(self, instructions):
        self.instructions = instructions
        self.slot = next(instructions, None)

    def run_to(self, slot):
        while self.slot is not None and self.slot <= slot:
            self.slot = next(self.instructions, None)


def build(nc, t):
    S, L, D = t["x"].shape
    DI = t["conv_w"].shape[0]
    NS = t["A_log"].shape[1]
    R = t["dt_w"].shape[0]
    FF = t["d1_w"].shape[1]
    NE, _, EI = t["e1_w"].shape
    TT = L // P
    KD, KI, KF, KE = D // P, DI // P, FF // P, EI // P
    NX = R + 2 * NS
    NTOK = S * L
    CAP = -(-NTOK // NE)
    NSLOT = NE * CAP
    BLK = min(512, CAP)
    TB = BLK // P
    QB = CAP // BLK
    FAR = float(1 << 20)
    assert S % 2 == 0 and L == 512 and CAP % BLK == 0 and NSLOT % (16 * P) == 0 and S >= 4

    NP2 = NS // 2
    NU = NP2 * KI
    RING = 4

    x_v = t["x"].rearrange("s (t p) d -> s p t d", p=P)
    out_v = t["out"].rearrange("s (t p) d -> s p t d", p=P)
    bc_dram = [nc.dram_tensor(f"bc_rows{i}", (2 * NS, L), F32, kind="Internal").ap() for i in range(2)]
    x1_dram = nc.dram_tensor("x1_rows", (S, L, D), F32, kind="Internal").ap()
    x1_v = x1_dram.rearrange("s (t p) d -> s p t d", p=P)
    xe_dram = nc.dram_tensor("expert_in", (NSLOT, D), F32, kind="Internal").ap()
    ye_dram = nc.dram_tensor("expert_out", (NSLOT, D), F32, kind="Internal").ap()
    xe_zero_v = xe_dram.rearrange("(a p r) d -> a p (r d)", p=P, r=16)
    xe_v = xe_dram.rearrange("(n t p) d -> n p t d", t=TB, p=P)
    ye_v = ye_dram.rearrange("(n t p) d -> n p t d", t=TB, p=P)

    with ExitStack() as whole:
        def sem(name):
            return whole.enter_context(nc.semaphore(name))

        idx_all = whole.enter_context(nc.sbuf_tensor("idx_all", [P, S * TT, 2], U32))
        w_all = whole.enter_context(nc.sbuf_tensor("w_all", [P, S * TT, 2], F32))
        ident = whole.enter_context(nc.sbuf_tensor("ident", [P, P], F32))
        ones = whole.enter_context(nc.sbuf_tensor("ones", [P, P], F32))
        eps5 = whole.enter_context(nc.sbuf_tensor("eps5", [P, 1], F32))
        bank = [whole.enter_context(nc.psum_tensor(f"bank{i}", [P, 512], F32)) for i in range(8)]

        attention_phase(nc, t, dict(locals()), sem)
        expert_phase(nc, t, dict(locals()), sem)
        combine_phase(nc, t, dict(locals()), sem)


def attention_phase(nc, t, env, sem):
    S, L, D, DI, NS, R, NE, TT = (env[k] for k in ("S", "L", "D", "DI", "NS", "R", "NE", "TT"))
    KD, KI, KF, NX, CAP, NSLOT, FAR = (env[k] for k in ("KD", "KI", "KF", "NX", "CAP", "NSLOT", "FAR"))
    NP2, NU, RING = env["NP2"], env["NU"], env["RING"]
    x_v, x1_v, xe_dram, bc_dram, xe_zero_v = (env[k] for k in ("x_v", "x1_v", "xe_dram", "bc_dram", "xe_zero_v"))
    idx_all, w_all, ident, ones, eps5, bank = (
        env[k] for k in ("idx_all", "w_all", "ident", "ones", "eps5", "bank"))
    Y, RB, PB = bank[0:4], bank[4:6], bank[6:8]
    FB = [*PB, *RB]

    with ExitStack() as ctx:
        def sb(name, shape, dt=F32):
            return ctx.enter_context(nc.sbuf_tensor(name, shape, dt))

        in_w = sb("in_w", [P, KD, 2 * DI])
        xp_w = sb("xp_w", [P, KI, NX])
        dt_w = sb("dt_w", [R, DI])
        out_w = sb("out_w", [P, KI, D])
        q_w = sb("q_w", [P, KD, D])
        k_w = sb("k_w", [P, KD, D])
        pr_w = sb("pr_w", [P, KD, D])
        fl_w = sb("fl_w", [P, KD, D])
        d1_w = sb("d1_w", [P, KD, KF * P])
        d2_w = sb("d2_w", [P, KF, D])
        emb = sb("emb", [P, KD, NE])
        conv_w = sb("conv_w", [P, KI, 4])
        conv_b = sb("conv_b", [P, KI])
        dt_b = sb("dt_b", [P, KI])
        a_neg = sb("a_neg", [P, KI, NS])
        d_skip = sb("d_skip", [P, KI])
        k_b = sb("k_b", [P, KD])
        g0f = sb("g0f", [P, KD])
        b0f = sb("b0f", [P, KD])
        g1f = sb("g1f", [P, KD])
        b1f = sb("b1f", [P, KD])
        d1_b = sb("d1_b", [P, KF])
        rows = {n: sb(f"row_{n}", [P, D]) for n in
                ("q_b", "pr_b", "fl_b", "ln0_g", "ln0_b", "lni_g", "lni_b", "ln1_g", "ln2_g", "ln2_b", "w_g")}
        d2_row = sb("d2_row", [P, D])
        tri = sb("tri", [P, P], BF16)
        ones_bf = sb("ones_bf", [P, P], BF16)
        iota8 = sb("iota8", [P, NE])
        slot0 = sb("slot0", [P, NE])
        xin = [sb(f"xin{i}", [P, TT, D]) for i in range(2)]
        u = [sb(f"u{i}", [P, KI, L]) for i in range(2)]
        g = [sb(f"g{i}", [P, KI, L]) for i in range(2)]
        delta = [sb(f"delta{i}", [P, KI, L]) for i in range(2)]
        du = [sb(f"du{i}", [P, KI, L]) for i in range(2)]
        xT = [d[:, 0:KD, :] for d in du]
        xd = sb("xd", [NX, L])
        minus_half = sb("minus_half", [P, TT])
        rest = sb("rest", [P, 2, L])
        bc = [[sb(f"{n}{i}", [P, 2, L]) for i in range(2)] for n in ("B_rows", "C_rows")]
        dA = [sb(f"dA{i}", [P, 2, L]) for i in range(2)]
        st = [sb(f"st{i}", [P, 2, L]) for i in range(RING)]
        stat_pre = sb("stat_pre", [P, TT, 6])
        mv_pre = sb("mv_pre", [P, TT, 2])
        r_pre = sb("r_pre", [P, TT])
        F = sb("F", [P, KD, L])
        gT = sb("gT", [P, KF, L])
        h = sb("h", [P, TT, D])
        tb = sb("tb", [P, TT, D])
        s = sb("s", [P, TT, D])
        gT_flat = gT[:, :, :].rearrange("p a b -> p (a b)")
        part = TT * D
        q = gT_flat[:, 0:part].rearrange("p (t d) -> p t d", t=TT)
        li = gT_flat[:, part:2 * part].rearrange("p (t d) -> p t d", t=TT)
        kT = gT_flat[:, 2 * part:3 * part].rearrange("p (k l) -> p k l", k=KD)
        ksq = gT_flat[:, 3 * part:4 * part].rearrange("p (k l) -> p k l", k=KD)
        proj_g = F[:, :, 0:D]
        junk_act = li
        junk_dve = gT_flat[:, 3 * part:4 * part].rearrange("p (t d) -> p t d", t=TT)
        stat = sb("stat", [P, TT, 6])
        mv = sb("mv", [P, TT, 2])
        r = sb("r", [P, TT])
        ssq = sb("ssq", [P, TT])
        rq = sb("rq", [P, TT])
        ssk = sb("ssk", [P, TT])
        rk = sb("rk", [P, TT])
        qw = sb("qw", [P, TT])
        qw2 = sb("qw2", [P, TT])
        ssg = sb("ssg", [P, 1])
        rg = sb("rg", [P, 1])
        gcol = sb("gcol", [P, KD])
        dots = sb("dots", [P, TT, NE])
        top = sb("top", [P, TT, 8])
        top_i = sb("top_i", [P, TT, 8], U32)
        top_f = sb("top_f", [P, TT, 2])
        dv = sb("dv", [P, TT])
        e2 = sb("e2", [P, TT])
        den = sb("den", [P, TT])
        wts = sb("wts", [P, TT, 2])
        pos2 = sb("pos2", [P, TT])
        oh = [sb(f"oh{i}", [P, TT, NE]) for i in range(2)]
        asg = sb("asg", [P, TT, NE], BF16)
        cum = sb("cum", [P, TT, NE])
        keep = sb("keep", [P, TT, NE])
        pick = [sb(f"pick{i}", [P, TT, NE]) for i in range(2)]
        slot_f = sb("slot_f", [P, TT, 2])
        idx = sb("idx", [P, TT, 2], U32)
        run = sb("run", [P, NE])

        pre_weights_in = sem("pre_weights_in")
        post_weights_in = sem("post_weights_in")
        consts = sem("consts")
        setup_dve = sem("setup_dve")
        setup_act = sem("setup_act")
        x_loaded = sem("x_loaded")
        xd_stored = sem("xd_stored")
        bc_loaded = [[sem(f"{n}_loaded{i}") for i in range(2)] for n in "BC"]
        xr_loaded = sem("xr_loaded")
        x1_stored = sem("x1_stored")
        scattered = sem("scattered")
        carried_pool = sem("carried_pool")
        carried_sp = sem("carried_sp")
        carried_dve = sem("carried_dve")
        zero_tile = sem("zero_tile")
        zeroed = sem("zeroed")

        def ln_names(n):
            return [f"{n}_stats", f"{n}_aggr"]

        pre_dve = Steps(sem("pre_dve"), ["x_stats", "x_aggr", "x_normed"]
                        + [f"conv{c}_{j}" for c in range(KI) for j in range(3)]
                        + ["xd"] + [f"z{c}" for c in range(KI)] + ["w0", "w2", "delta0", "delta2"])
        pre_act = Steps(sem("pre_act"), ["xT"] + [f"tap{c}" for c in range(KI)] + ["u"]
                        + [f"g{c}" for c in range(KI)] + ["z_abs", "sp_exp", "sp_ln0", "sp_ln2"])
        pre_pe = Steps(sem("pre_pe"), ["xT"] + [f"u{c}" for c in range(KI)] + [f"g{c}" for c in range(KI)]
                       + ["xd"] + [f"dt{c}" for c in range(KI)])
        pre_pool = Steps(sem("pre_pool"), ["x_v", "x_r", "rest0", "log1p0", "rest2", "log1p2", "du0", "du2"])
        scan_exp = Steps(sem("scan_exp"), range(NU))
        scan_in = Steps(sem("scan_in"), range(NU))
        scan_h = Steps(sem("scan_h"), range(NU))
        scan_hc = Steps(sem("scan_hc"), range(NU))
        scan_sum = Steps(sem("scan_sum"), range(NU))
        post_pe = Steps(sem("post_pe"), ["m0", "m1", "hT", "q", "k", "ssk", "G", "hs", "tT", "fl", "sT"]
                        + [f"d1_{j}" for j in range(KF)] + [f"d2_{tile}" for tile in range(TT)] + ["nT", "dots", "cum"])
        post_act = Steps(sem("post_act"), ["hT", "q_sq", "kT", "k_sq", "q_gelu", "tT", "sT"]
                         + [f"gelu{j}" for j in range(KF)] + ["nT", "e2"])
        post_dve = Steps(sem("post_dve"), [f"y_{a}{c}" for a in "ab" for c in (0, 1)]
                         + [f"y_{a}{c}" for a in "ab" for c in (2, 3)]
                         + ["h_sum", "h_stats", "h_aggr", "h_normed", "q_sum"]
                         + ["hi_stats", "hi_aggr", "li", "qw", "qw2", "ssk", "ssg", "G", "proj_g", "t",
                            "s_sum", "s_stats", "s_aggr", "s_normed", "f_sum0", "f_sum1", "f_stats", "f_aggr",
                            "f_normed", "o_stats", "o_aggr", "o_normed", "n_stats", "n_aggr", "n_normed",
                            "dots", "top", "top_i", "dv", "top_f", "den", "w1", "w2", "pos2", "oh0", "oh1",
                            "oh1_pos", "asg", "cum", "keep", "run", "slotv", "slotk", "pick0", "pick1",
                            "slot0", "slot1", "idx", "idx_all", "w_all"])
        post_pool = Steps(sem("post_pool"), ["h_v", "h_r", "h_g", "h_b", "q_v", "q_r", "hi_v", "hi_r", "li_g", "li_b",
                                             "k_v", "k_r", "G_v", "G_r", "h_fl", "t_li", "s_v", "s_r", "s_g", "s_b",
                                             "f_v", "f_r", "f_g", "f_b", "o_v", "o_r", "x1", "n_v", "n_r"])
        sp_sent = Steps(sem("sp_sent"), ["sent"])

        def matrix(name):
            return t[name].rearrange("(k p) n -> p k n", p=P)

        def vectors(pairs):
            return [(dst[:, :], t[name].rearrange("(k p) -> p k", p=P)) for dst, name in pairs]

        PRE_IN = [(in_w[:, :, :], matrix("in_w")), (conv_w[:, :, :], matrix("conv_w")),
                  (a_neg[:, :, :], matrix("A_log")), (xp_w[:, :, :], matrix("xp_w")), (dt_w[:, :], t["dt_w"])]
        PRE_IN += vectors(((conv_b, "conv_b"), (dt_b, "dt_b")))
        POST_IN = [(dst[:, :, :], matrix(name)) for dst, name in
                   ((out_w, "out_w"), (q_w, "q_w"), (k_w, "k_w"), (pr_w, "pr_w"), (fl_w, "fl_w"), (d1_w, "d1_w"),
                    (d2_w, "d2_w"), (emb, "emb"))]
        POST_IN += vectors(((d_skip, "D_skip"), (k_b, "k_b"), (g0f, "ln0_g"), (b0f, "ln0_b"), (g1f, "ln1_g"),
                            (b1f, "ln1_b"), (d1_b, "d1_b")))
        POST_IN += [(rows[n][:, :], t[n].partition_broadcast(P)) for n in rows]
        POST_IN += [(d2_row[:, :], t["d2_b"].partition_broadcast(P)), (s[:, 0, :], t["ln1_b"].partition_broadcast(P))]

        SLOTS = 3

        def run_stages(parts, post, pre):
            stages = [Stage(stage) for stage in (post, pre) if stage is not None]
            for slot in range(SLOTS * NU):
                parts[slot % SLOTS](slot // SLOTS)
                for stage in stages:
                    stage.run_to(slot)

        def nothing(k):
            pass

        def all_sequences(engine, pre, scan, post):
            Stage(pre(0, 0)).run_to(SLOTS * NU)
            scan(0, 0, None, pre(1, 1))
            with engine.Fori(0, (S - 2) // 2) as i:
                for half in range(2):
                    b = 2 * i + (1 + half)
                    par = (1 + half) % 2
                    scan(b, par, post(b - 1, 1 - par, True), pre(b + 1, 1 - par))
            scan(S - 1, 1, post(S - 2, 0, False), None)
            Stage(post(S - 1, 1, False)).run_to(SLOTS * NU)

        block = ctx.enter_context(nc.Block())

        @block.sync
        def _(sp):
            sp.sem_inc(x1_stored, 16)
            sp_sent.credit(sp)
            for dst, src in PRE_IN:
                with nc.allow_non_contiguous_dma(reason="small per-channel vectors, once"):
                    sp.dma_start(dst, src).then_inc(pre_weights_in, 16)

            def load_rows(half, b, par, pair):
                src = bc_dram[par].rearrange("(s n) l -> s n l", s=2)[half, 2 * pair:2 * pair + 2, :]
                sp.dma_start(bc[half][pair % 2][:, :, :], src.partition_broadcast(P))\
                    .then_inc(bc_loaded[half][pair % 2], 16)

            def load_bc(b, par, pair):
                for half, used in ((0, scan_in), (1, scan_hc)):
                    k = (pair - 2) * KI + KI - 1
                    sp.wait_ge(*(used.at(k, b) if pair >= 2 else used.at(NU + k, b - 1)))
                    sp.sem_inc(carried_sp, 1)
                    load_rows(half, b, par, pair)

            def pre(b, par):
                yield 9
                sp.wait_ge(*pre_pe.at("xT", b - 2))
                sp.wait_ge(*post_dve.at("h_sum", b - 2))
                sp.sem_inc(carried_sp, 1)
                sp.dma_start(xin[par][:, :, :], x_v[b]).then_inc(x_loaded, 16)
                yield 45
                sp.wait_ge(*pre_dve.at("xd", b))
                sp.dma_start(bc_dram[par], xd[R:NX, :]).then_inc(xd_stored, 16)
                yield 94
                sp.wait_ge(xd_stored, 16 * (b + 1))
                sp.sem_inc(carried_sp, 1)
                load_bc(b, par, 0)

            def scan(b, par, post_stage, pre_stage):
                def rows(k):
                    if k % KI == 0 and k // KI + 1 < NP2:
                        load_bc(b, par, k // KI + 1)
                run_stages((rows, nothing, nothing), post_stage, pre_stage)

            def post(b, par, more):
                yield 47
                sp.wait_ge(*post_dve.at("s_sum", b))
                sp.sem_inc(carried_sp, 1)
                sp.dma_start(h[:, :, :], x_v[b]).then_inc(xr_loaded, 16)
                yield 84
                sp.wait_ge(*post_pool.at("x1", b))
                sp.sem_inc(carried_sp, 1)
                sp.dma_start(x1_v[b], h[:, :, :]).then_inc(x1_stored, 16)
                yield 95
                sp.wait_ge(scattered, 16 * 2 * TT * (b + 1))
                sp.sem_inc(sp_sent.did("sent"), 1)

            all_sequences(sp, pre, scan, post)
            sp.wait_ge(x1_stored, 16 * (S + 1))

        @block.gpsimd
        def _(pool):
            pool.memset(ident[:, :], 0.0).then_inc(consts, 1)
            pool.memset(ones[:, :], 1.0).then_inc(consts, 1)
            pool.memset(ones_bf[:, :], 1.0).then_inc(consts, 1)
            pool.memset(tri[:, :], 1.0).then_inc(consts, 1)
            pool.memset(eps5[:, :], LN_EPS).then_inc(consts, 1)
            pool.memset(run[:, :], 0.0).then_inc(consts, 1)
            pool.memset(minus_half[:, :], -0.5).then_inc(consts, 1)
            for i in range(2):
                pool.memset(dA[i][:, :, 0:1], 0.0).then_inc(consts, 1)
            pool.iota(iota8[:, :], pattern=[[1, NE]], base=0, channel_multiplier=0,
                      allow_small_or_imprecise_dtypes=True).then_inc(consts, 1)
            pool.iota(slot0[:, :], pattern=[[CAP, NE]], base=-1 - int(FAR), channel_multiplier=0,
                      allow_small_or_imprecise_dtypes=True).then_inc(consts, 1)
            pool.wait_ge(consts, 11)
            pool.affine_select(out=ident[:, :], in_=ident[:, :], compare_op=ALU.not_equal, fill=1.0, base=0,
                               pattern=[[-1, P]], channel_multiplier=1).then_inc(consts, 1)
            pool.affine_select(out=tri[:, :], in_=tri[:, :], compare_op=ALU.is_ge, fill=0.0, base=0,
                               pattern=[[1, P]], channel_multiplier=-1).then_inc(consts, 1)
            for steps in (pre_pool, scan_hc, post_pool):
                steps.credit(pool)

            def power(steps, name, out, value, least, op, b):
                pool.sem_inc(carried_pool, 1)
                pool.tensor_scalar(out[:, :], value, least, None, op).then_inc(steps.did(f"{name}_v"), 1)
                pool.wait_ge(*steps.at(f"{name}_v", b))
                pool.tensor_tensor(out[:, :], out[:, :], minus_half[:, 0:out.shape[1]], ALU.pow)\
                    .then_inc(steps.did(f"{name}_r"), 1)

            def pre(b, par):
                yield 15
                pool.wait_ge(*pre_dve.at("x_aggr", b))
                power(pre_pool, "x", r_pre, mv_pre[:, :, 1], LN_EPS, ALU.add, b)
                for c, slot in ((0, 58), (2, 64)):
                    yield slot
                    two = du[par][:, c:c + 2, :]
                    pool.wait_ge(*pre_dve.at(f"w{c}", b))
                    pool.tensor_tensor(rest[:, :, :], two, rest[:, :, :], ALU.subtract)\
                        .then_inc(pre_pool.did(f"rest{c}"), 1)
                    yield slot + 4
                    pool.wait_ge(*pre_act.at(f"sp_ln{c}", b))
                    pool.wait_ge(*pre_pool.at(f"rest{c}", b))
                    pool.tensor_tensor(two, two, rest[:, :, :], ALU.add).then_inc(pre_pool.did(f"log1p{c}"), 1)
                for c, slot in ((0, 73), (2, 77)):
                    yield slot
                    pool.wait_ge(*pre_dve.at(f"delta{c}", b))
                    pool.tensor_tensor(du[par][:, c:c + 2, :], delta[par][:, c:c + 2, :], u[par][:, c:c + 2, :],
                                       ALU.mult).then_inc(pre_pool.did(f"du{c}"), 1)

            def scan(b, par, post_stage, pre_stage):
                def times_c(k):
                    pair, c = k // KI, k % KI
                    tile = st[k % RING]
                    if c == 0:
                        pool.wait_ge(bc_loaded[1][pair % 2], 16 * (NP2 // 2) * b + 16 * (pair // 2 + 1))
                    pool.wait_ge(*scan_h.at(k, b))
                    pool.tensor_tensor(tile[:, :, :], tile[:, :, :], bc[1][pair % 2][:, :, :], ALU.mult)\
                        .then_inc(scan_hc.did(k), 1)

                def behind(k):
                    if k >= 1:
                        times_c(k - 1)
                run_stages((nothing, behind, nothing), post_stage, pre_stage)
                times_c(NU - 1)
                if isinstance(b, int) and b == 0:
                    pool.wait_ge(setup_dve, 2)
                    pool.wait_ge(zeroed, 16 * xe_zero_v.shape[0])

            def times(name, dst, row):
                pool.tensor_tensor(dst[:, :, :], dst[:, :, :], row[:, :].unsqueeze(1).to_broadcast([P, TT, D]),
                                   ALU.mult).then_inc(post_pool.did(name), 1)

            def plus(name, dst, row):
                pool.tensor_tensor(dst[:, :, :], dst[:, :, :], row[:, :].unsqueeze(1).to_broadcast([P, TT, D]),
                                   ALU.add).then_inc(post_pool.did(name), 1)

            def post(b, par, more):
                yield 10
                pool.wait_ge(*post_dve.at("h_aggr", b))
                power(post_pool, "h", r, mv[:, :, 1], EPS, ALU.add, b)
                yield 13
                pool.wait_ge(*post_pe.at("hT", b))
                times("h_g", h, rows["ln0_g"])
                yield 16
                pool.wait_ge(*post_pool.at("h_g", b))
                plus("h_b", h, rows["ln0_b"])
                yield 21
                pool.wait_ge(*post_act.at("q_sq", b))
                power(post_pool, "q", rq, ssq[:, :], EPS * EPS, ALU.max, b)
                pool.wait_ge(*post_dve.at("hi_aggr", b))
                power(post_pool, "hi", r, mv[:, :, 1], EPS, ALU.add, b)
                yield 24
                pool.wait_ge(*post_dve.at("li", b))
                times("li_g", li, rows["lni_g"])
                yield 27
                pool.wait_ge(*post_pool.at("li_g", b))
                plus("li_b", li, rows["lni_b"])
                yield 28
                pool.wait_ge(*post_dve.at("ssk", b))
                power(post_pool, "k", rk, ssk[:, :], EPS * EPS, ALU.max, b)
                yield 31
                pool.wait_ge(*post_dve.at("ssg", b))
                power(post_pool, "G", rg, ssg[:, :], EPS * EPS, ALU.max, b)
                yield 34
                plus("h_fl", h, rows["fl_b"])
                yield 38
                pool.wait_ge(*post_dve.at("t", b))
                pool.wait_ge(*post_pool.at("li_b", b))
                pool.tensor_tensor(tb[:, :, :], tb[:, :, :], li, ALU.mult).then_inc(post_pool.did("t_li"), 1)
                yield 48
                pool.wait_ge(*post_dve.at("s_aggr", b))
                power(post_pool, "s", r, mv[:, :, 1], EPS, ALU.add, b)
                yield 52
                pool.wait_ge(*post_pe.at("sT", b))
                times("s_g", s, rows["ln1_g"])
                yield 55
                pool.wait_ge(*post_pool.at("s_g", b))
                plus("s_b", s, d2_row)
                yield 75
                pool.wait_ge(*post_dve.at("f_aggr", b))
                power(post_pool, "f", r, mv[:, :, 1], EPS, ALU.add, b)
                yield 77
                pool.wait_ge(*post_dve.at("f_normed", b))
                times("f_g", s, rows["ln2_g"])
                pool.wait_ge(*post_pool.at("f_g", b))
                plus("f_b", s, rows["ln2_b"])
                yield 81
                pool.wait_ge(*post_dve.at("o_aggr", b))
                power(post_pool, "o", r, mv[:, :, 1], LN_EPS, ALU.add, b)
                yield 83
                pool.wait_ge(*post_dve.at("o_normed", b))
                pool.wait_ge(xr_loaded, 16 * (b + 1))
                pool.tensor_tensor(h[:, :, :], h[:, :, :], s[:, :, :], ALU.add).then_inc(post_pool.did("x1"), 1)
                yield 86
                pool.wait_ge(*post_dve.at("n_aggr", b))
                power(post_pool, "n", r, mv[:, :, 1], LN_EPS, ALU.add, b)
                yield 95
                pool.wait_ge(*post_dve.at("idx", b))
                pool.sem_inc(carried_pool, 1)
                for tile in range(TT):
                    for choice in range(2):
                        pool.indirect_dma_start(
                            out=xe_dram, out_offset=bass.IndirectOffsetOnAxis(ap=idx[:, tile, choice:choice + 1], axis=0),
                            in_=tb[:, tile, :], in_offset=None, bounds_check=NSLOT - 1, oob_is_err=False)\
                            .then_inc(scattered, 16)

            all_sequences(pool, pre, scan, post)

        @block.scalar
        def _(act):
            for steps in (pre_act, scan_exp, post_act):
                steps.credit(act)
            for dst, src in POST_IN:
                with nc.allow_non_contiguous_dma(reason="small per-channel vectors, once"):
                    act.dma_start(dst, src).then_inc(post_weights_in, 16)
            act.wait_ge(zero_tile, 1)
            for a in range(xe_zero_v.shape[0]):
                act.dma_start(xe_zero_v[a], gT_flat).then_inc(zeroed, 16)
            act.wait_ge(consts, 13)
            act.wait_ge(pre_weights_in, 16 * len(PRE_IN))
            act.activation(a_neg[:, :, :], a_neg[:, :, :], ACT.Exp).then_inc(setup_act, 1)
            act.wait_ge(setup_dve, 1)

            def pre(b, par):
                yield 19
                act.wait_ge(*pre_pe.at("xT", b))
                act.copy(xT[par][:, 0, :], RB[0][:, :])
                act.copy(xT[par][:, 1, :], RB[1][:, :]).then_inc(pre_act.did("xT"), 1)
                for c in range(KI):
                    yield 22 + 3 * c
                    act.wait_ge(*pre_pe.at(f"u{c}", b))
                    if c == 0:
                        act.wait_ge(*post_pe.at("m1", b - 2))
                    act.activation(u[par][:, c, :], RB[c % 2][:, :], ACT.Identity, bias=conv_b[:, c:c + 1],
                                   scale=conv_w[:, c, 3:4]).then_inc(pre_act.did(f"tap{c}"), 1)
                yield 36
                act.wait_ge(*pre_dve.at("conv3_2", b))
                act.activation(u[par][:, :, :], u[par][:, :, :], ACT.Silu).then_inc(pre_act.did("u"), 1)
                for c in range(KI):
                    if c == 2:
                        yield 40
                    act.wait_ge(*pre_pe.at(f"g{c}", b))
                    act.activation(g[par][:, c, :], RB[c % 2][:, :], ACT.Silu).then_inc(pre_act.did(f"g{c}"), 1)
                yield 52
                act.wait_ge(*pre_dve.at("z3", b))
                act.activation(du[par][:, :, :], delta[par][:, :, :], ACT.Abs).then_inc(pre_act.did("z_abs"), 1)
                yield 53
                act.wait_ge(*pre_act.at("z_abs", b))
                act.activation(du[par][:, :, :], du[par][:, :, :], ACT.Exp, scale=-1.0)\
                    .then_inc(pre_act.did("sp_exp"), 1)
                for c, slot in ((0, 60), (2, 66)):
                    yield slot
                    act.wait_ge(*pre_pool.at(f"rest{c}", b))
                    act.activation(du[par][:, c:c + 2, :], du[par][:, c:c + 2, :], ACT.Ln, bias=ones[:, 0:1])\
                        .then_inc(pre_act.did(f"sp_ln{c}"), 1)

            def scan(b, par, post_stage, pre_stage):
                def decay(k, j):
                    pair, c = k // KI, k % KI
                    if j == 0:
                        if k == 0:
                            act.wait_ge(*pre_dve.at("delta2", b))
                        act.wait_ge(*(scan_h.at(NU - 2 + k, b - 1) if k < 2 else scan_h.at(k - 2, b)))
                    return act.activation(dA[k % 2][:, j, 1:L], delta[par][:, c, 1:L], ACT.Exp,
                                          scale=a_neg[:, c, 2 * pair + j:2 * pair + j + 1])

                def first_half(k):
                    if k == 0:
                        decay(0, 0)
                        decay(0, 1).then_inc(scan_exp.did(0), 1)
                    if k + 1 < NU:
                        decay(k + 1, 0)

                def second_half(k):
                    if k + 1 < NU:
                        decay(k + 1, 1).then_inc(scan_exp.did(k + 1), 1)
                run_stages((first_half, second_half, nothing), post_stage, pre_stage)
                if isinstance(b, int) and b == 0:
                    act.wait_ge(post_weights_in, 16 * len(POST_IN))

            def post(b, par, more):
                yield 14
                act.wait_ge(*post_pe.at("hT", b))
                for c in range(KD):
                    last = act.activation(F[:, c, :], PB[c][:, :], ACT.Identity, bias=b0f[:, c:c + 1],
                                          scale=g0f[:, c:c + 1])
                last.then_inc(post_act.did("hT"), 1)
                yield 19
                act.wait_ge(*post_dve.at("q_sum", b))
                for tile in range(TT):
                    last = act.activation(junk_act[:, tile, :], q[:, tile, :], ACT.Square, accum_out=ssq[:, tile:tile + 1])
                last.then_inc(post_act.did("q_sq"), 1)
                yield 22
                act.wait_ge(*post_pe.at("k", b))
                for c in range(KD):
                    last = act.activation(kT[:, c, :], PB[c][:, :], ACT.Identity, bias=k_b[:, c:c + 1])
                last.then_inc(post_act.did("kT"), 1)
                yield 23
                act.wait_ge(*post_act.at("kT", b))
                act.activation(ksq, kT, ACT.Square).then_inc(post_act.did("k_sq"), 1)
                yield 24
                act.wait_ge(*post_pool.at("q_r", b))
                for tile in range(TT):
                    last = act.activation(q[:, tile, :], q[:, tile, :], ACT.Gelu, scale=rq[:, tile:tile + 1])
                last.then_inc(post_act.did("q_gelu"), 1)
                yield 42
                act.wait_ge(*post_pe.at("tT", b))
                act.copy(F[:, 0, :], PB[0][:, :])
                act.copy(F[:, 1, :], PB[1][:, :]).then_inc(post_act.did("tT"), 1)
                yield 52
                act.wait_ge(*post_pe.at("sT", b))
                for c in range(KD):
                    last = act.activation(F[:, c, :], PB[c][:, :], ACT.Identity, bias=b1f[:, c:c + 1],
                                          scale=g1f[:, c:c + 1])
                last.then_inc(post_act.did("sT"), 1)
                for j in range(KF):
                    if j % 4 == 0:
                        yield 57 + 7 * (j // 4)
                    act.wait_ge(*post_pe.at(f"d1_{j}", b))
                    act.activation(gT[:, j, :], FB[j % 4][:, :], ACT.Gelu, bias=d1_b[:, j:j + 1])\
                        .then_inc(post_act.did(f"gelu{j}"), 1)
                yield 88
                act.wait_ge(*post_pe.at("nT", b))
                act.copy(F[:, 0, :], PB[0][:, :])
                act.copy(F[:, 1, :], PB[1][:, :]).then_inc(post_act.did("nT"), 1)
                yield 91
                act.wait_ge(*post_dve.at("dv", b))
                act.activation(e2[:, :], dv[:, :], ACT.Exp).then_inc(post_act.did("e2"), 1)

            all_sequences(act, pre, scan, post)

        @block.tensor
        def _(pe):
            for steps in (pre_pe, scan_sum, post_pe):
                steps.credit(pe)
            pe.wait_ge(consts, 13)
            pe.wait_ge(pre_weights_in, 16 * len(PRE_IN))

            def turn(src, banks):
                for c in range(KD):
                    for tile in range(TT):
                        last = pe.transpose(banks[c][:, tile * P:(tile + 1) * P], src[:, tile, c * P:(c + 1) * P],
                                            ident[:, :])
                return last

            def token_major(srcT, w, K, tiles=range(TT)):
                for tile in tiles:
                    for c in range(K):
                        last = pe.matmul(PB[tile // 2][:, (tile % 2) * D:(tile % 2 + 1) * D],
                                         srcT[:, c, tile * P:(tile + 1) * P], w[:, c, :], start=c == 0, stop=c == K - 1)
                return last

            def pre(b, par):
                yield 17
                pe.wait_ge(*pre_dve.at("x_normed", b))
                if not isinstance(b, int) or b >= 2:
                    pe.wait_ge(*post_act.at(f"gelu{KF - 1}", b - 3))
                turn(xin[par], RB).then_inc(pre_pe.did("xT"), 1)
                for m in range(2 * KI):
                    name = f"u{m}" if m < KI else f"g{m - KI}"
                    yield (20, 23, 26, 29, 32, 34, 37, 39)[m]
                    if m == 0:
                        pe.wait_ge(*pre_act.at("xT", b))
                    elif 2 <= m < KI + 2:
                        pe.wait_ge(*pre_dve.at(f"conv{m - 2}_2", b))
                    elif m >= KI + 2:
                        pe.wait_ge(*pre_act.at(f"g{m - KI - 2}", b))
                    for c in range(KD):
                        last = pe.matmul(RB[m % 2][:, :], in_w[:, c, m * P:(m + 1) * P], xT[par][:, c, :],
                                         start=c == 0, stop=c == KD - 1)
                    last.then_inc(pre_pe.did(name), 1)
                yield 42
                pe.wait_ge(*pre_act.at("g2", b))
                for c in range(KI):
                    last = pe.matmul(RB[0][0:NX, :], xp_w[:, c, :], u[par][:, c, :], start=c == 0, stop=c == KI - 1)
                last.then_inc(pre_pe.did("xd"), 1)
                for c in range(KI):
                    yield 45 + c
                    if c == 0:
                        pe.wait_ge(*pre_act.at("g3", b))
                        pe.wait_ge(*pre_dve.at("xd", b))
                    elif c >= 2:
                        pe.wait_ge(*pre_dve.at(f"z{c - 2}", b))
                    pe.matmul(RB[(c + 1) % 2][:, :], dt_w[:, c * P:(c + 1) * P], xd[0:R, :], start=True, stop=True)\
                        .then_inc(pre_pe.did(f"dt{c}"), 1)

            def scan(b, par, post_stage, pre_stage):
                def add_state(k, j):
                    pair, c = k // KI, k % KI
                    if j == 0:
                        if pair == 0:
                            pe.wait_ge(*post_dve.at(f"y_a{c}", b - 1))
                        pe.wait_ge(*scan_hc.at(k, b))
                    return pe.matmul(Y[c][:, :], ident[:, :], st[k % RING][:, j, :],
                                     start=pair == 0 and j == 0, stop=pair == NP2 - 1 and j == 1)

                def first_half(k):
                    if k >= 2:
                        add_state(k - 2, 0)

                def second_half(k):
                    if k >= 2:
                        add_state(k - 2, 1).then_inc(scan_sum.did(k - 2), 1)
                run_stages((first_half, second_half, nothing), post_stage, pre_stage)
                for k in (NU - 2, NU - 1):
                    add_state(k, 0)
                    add_state(k, 1).then_inc(scan_sum.did(k), 1)
                if isinstance(b, int) and b == 0:
                    pe.wait_ge(post_weights_in, 16 * len(POST_IN))

            def post(b, par, more):
                for half in range(2):
                    yield 3 + 3 * half
                    if half == 0:
                        pe.wait_ge(*post_dve.at("y_b3", b))
                    token_major(u[par], out_w, KI, (2 * half, 2 * half + 1)).then_inc(post_pe.did(f"m{half}"), 1)
                yield 12
                pe.wait_ge(*post_dve.at("h_normed", b))
                turn(h, PB).then_inc(post_pe.did("hT"), 1)
                yield 15
                pe.wait_ge(*post_act.at("hT", b))
                token_major(F, q_w, KD).then_inc(post_pe.did("q"), 1)
                yield 19
                pe.wait_ge(*post_dve.at("q_sum", b))
                for m in range(KD):
                    for c in range(KD):
                        last = pe.matmul(PB[m][:, :], k_w[:, c, m * P:(m + 1) * P], F[:, c, :],
                                         start=c == 0, stop=c == KD - 1)
                last.then_inc(post_pe.did("k"), 1)
                yield 25
                pe.wait_ge(*post_act.at("k_sq", b))
                for tile in range(TT):
                    for c in range(KD):
                        last = pe.matmul(PB[0][:, tile:tile + 1], ksq[:, c, tile * P:(tile + 1) * P], ones[:, 0:1],
                                         start=c == 0, stop=c == KD - 1)
                last.then_inc(post_pe.did("ssk"), 1)
                yield 28
                pe.wait_ge(*post_dve.at("qw2", b))
                for c in range(KD):
                    for tile in range(TT):
                        pe.matmul(PB[1][:, c:c + 1], q[:, tile, c * P:(c + 1) * P], qw[:, tile:tile + 1],
                                  start=tile == 0, stop=tile == TT - 1)
                pe.matmul(PB[1][:, 8:8 + TT], ones[:, :], qw2[:, :], start=True, stop=True)\
                    .then_inc(post_pe.did("G"), 1)
                yield 34
                pe.wait_ge(*post_dve.at("proj_g", b))
                token_major(kT, proj_g, KD).then_inc(post_pe.did("hs"), 1)
                yield 40
                pe.wait_ge(*post_pool.at("t_li", b))
                turn(tb, PB).then_inc(post_pe.did("tT"), 1)
                yield 43
                pe.wait_ge(*post_act.at("tT", b))
                token_major(F, fl_w, KD).then_inc(post_pe.did("fl"), 1)
                yield 50
                pe.wait_ge(*post_dve.at("s_normed", b))
                turn(s, PB).then_inc(post_pe.did("sT"), 1)
                for j in range(KF):
                    if j % 2 == 0:
                        yield (53, 55, 59, 61)[j // 2]
                    if j == 0:
                        pe.wait_ge(*post_act.at("sT", b))
                    elif j == 2 and more:
                        pe.wait_ge(*pre_dve.at("z3", b + 2))
                    elif j >= 4:
                        pe.wait_ge(*post_act.at(f"gelu{j - 4}", b))
                    for c in range(KD):
                        last = pe.matmul(FB[j % 4][:, :], d1_w[:, c, j * P:(j + 1) * P], F[:, c, :],
                                         start=c == 0, stop=c == KD - 1)
                    last.then_inc(post_pe.did(f"d1_{j}"), 1)
                for tile in range(TT):
                    yield (65, 67, 69, 71)[tile]
                    pe.wait_ge(*post_act.at(f"gelu{KF - 1}", b))
                    token_major(gT, d2_w, KF, (tile,)).then_inc(post_pe.did(f"d2_{tile}"), 1)
                yield 87
                pe.wait_ge(*post_dve.at("n_normed", b))
                turn(tb, PB).then_inc(post_pe.did("nT"), 1)
                yield 89
                pe.wait_ge(*post_act.at("nT", b))
                for tile in range(TT):
                    for c in range(KD):
                        last = pe.matmul(PB[0][:, tile * NE:(tile + 1) * NE], F[:, c, tile * P:(tile + 1) * P],
                                         emb[:, c, :], start=c == 0, stop=c == KD - 1)
                last.then_inc(post_pe.did("dots"), 1)
                yield 93
                pe.wait_ge(*post_dve.at("asg", b))
                for tile in range(TT):
                    dst = PB[1][:, tile * NE:(tile + 1) * NE]
                    for before in range(tile):
                        pe.matmul(dst, ones_bf[:, :], asg[:, before, :], start=before == 0, stop=False)
                    pe.matmul(dst, tri[:, :], asg[:, tile, :], start=tile == 0, stop=True)
                for tile in range(TT):
                    last = pe.matmul(PB[1][:, TT * NE:(TT + 1) * NE], ones_bf[:, :], asg[:, tile, :],
                                     start=tile == 0, stop=tile == TT - 1)
                last.then_inc(post_pe.did("cum"), 1)

            all_sequences(pe, pre, scan, post)

        @block.vector
        def _(dve):
            dve.memset(gT_flat, 0.0).then_inc(zero_tile, 1)
            for steps in (pre_dve, scan_in, scan_h, post_dve):
                steps.credit(dve)
            dve.wait_ge(consts, 13)
            dve.wait_ge(pre_weights_in, 16 * len(PRE_IN))
            dve.wait_ge(setup_act, 1)
            dve.tensor_scalar(a_neg[:, :, :], a_neg[:, :, :], -1.0, None, ALU.mult).then_inc(setup_dve, 1)

            def stats(steps, name, src, stat_t, mv_t, b):
                for tile in range(TT):
                    last = dve.bn_stats(stat_t[:, tile, :], src[:, tile, :])
                last.then_inc(steps.did(f"{name}_stats"), 1)
                dve.wait_ge(*steps.at(f"{name}_stats", b))
                dve.sem_inc(carried_dve, 1)
                for tile in range(TT):
                    last = dve.bn_aggr(mv_t[:, tile, :], stat_t[:, tile, :])
                last.then_inc(steps.did(f"{name}_aggr"), 1)

            def normalise(dst, src, mv_t, r_t):
                for tile in range(TT):
                    last = dve.tensor_scalar(dst[:, tile, :], src[:, tile, :], mv_t[:, tile, 0:1],
                                             r_t[:, tile:tile + 1], ALU.subtract, ALU.mult)
                return last

            def pre(b, par):
                yield 14
                dve.wait_ge(x_loaded, 16 * (b + 1))
                stats(pre_dve, "x", xin[par], stat_pre, mv_pre, b)
                yield 16
                dve.wait_ge(*pre_pool.at("x_r", b))
                normalise(xin[par], xin[par], mv_pre, r_pre).then_inc(pre_dve.did("x_normed"), 1)
                for c in range(KI):
                    yield 23 + 3 * c
                    for j in range(3):
                        if j == 0:
                            dve.wait_ge(*pre_act.at(f"tap{c}", b))
                        else:
                            dve.wait_ge(*pre_dve.at(f"conv{c}_{j - 1}", b))
                        late = u[par][:, c, j + 1:L]
                        dve.scalar_tensor_tensor(late, RB[c % 2][:, 0:L - 1 - j], conv_w[:, c, 2 - j:3 - j], late,
                                                 ALU.mult, ALU.add).then_inc(pre_dve.did(f"conv{c}_{j}"), 1)
                yield 44
                dve.wait_ge(*pre_pe.at("xd", b))
                dve.wait_ge(xd_stored, 16 * b)
                dve.tensor_copy(xd[:, :], RB[0][0:NX, :]).then_inc(pre_dve.did("xd"), 1)
                for c in range(KI):
                    yield 46 + c
                    dve.wait_ge(*pre_pe.at(f"dt{c}", b))
                    dve.tensor_scalar(delta[par][:, c, :], RB[(c + 1) % 2][:, :], dt_b[:, c:c + 1], None, ALU.add)\
                        .then_inc(pre_dve.did(f"z{c}"), 1)
                for c, slot in ((0, 56), (2, 63)):
                    yield slot
                    if c == 0:
                        dve.wait_ge(*pre_act.at("sp_exp", b))
                    else:
                        dve.wait_ge(*pre_pool.at("log1p0", b))
                    dve.tensor_scalar(rest[:, :, :], du[par][:, c:c + 2, :], 1.0, 1.0, ALU.add, ALU.subtract)\
                        .then_inc(pre_dve.did(f"w{c}"), 1)
                for c, slot in ((0, 65), (2, 71)):
                    yield slot
                    dve.wait_ge(*pre_pool.at(f"log1p{c}", b))
                    dve.scalar_tensor_tensor(delta[par][:, c:c + 2, :], delta[par][:, c:c + 2, :], 0.0,
                                             du[par][:, c:c + 2, :], ALU.max, ALU.add)\
                        .then_inc(pre_dve.did(f"delta{c}"), 1)

            def scan(b, par, post_stage, pre_stage):
                def drive(k):
                    pair, c = k // KI, k % KI
                    if k == 0:
                        dve.wait_ge(*pre_pool.at("du2", b))
                    if c == 0:
                        dve.wait_ge(bc_loaded[0][pair % 2], 16 * (NP2 // 2) * b + 16 * (pair // 2 + 1))
                    dve.wait_ge(*(scan_sum.at(NU - RING + k, b - 1) if k < RING else scan_sum.at(k - RING, b)))
                    dve.tensor_tensor(st[k % RING][:, :, :],
                                      du[par][:, c, :].unsqueeze(1).to_broadcast([P, 2, L]),
                                      bc[0][pair % 2][:, :, :], ALU.mult).then_inc(scan_in.did(k), 1)

                def ahead(k):
                    if k == 0:
                        drive(0)
                    if k + 1 < NU:
                        drive(k + 1)

                def recur(k):
                    dve.wait_ge(*scan_exp.at(k, b))
                    dve.wait_ge(*scan_in.at(k, b))
                    flat = st[k % RING][:, :, :].rearrange("p a l -> p (a l)")
                    dve.tensor_tensor_scan(flat, dA[k % 2][:, :, :].rearrange("p a l -> p (a l)"), flat, 0.0,
                                           ALU.mult, ALU.add).then_inc(scan_h.did(k), 1)
                run_stages((ahead, nothing, recur), post_stage, pre_stage)
                if isinstance(b, int) and b == 0:
                    dve.wait_ge(post_weights_in, 16 * len(POST_IN))
                    dve.wait_ge(zeroed, 16 * xe_zero_v.shape[0])
                    dve.tensor_tensor(d2_row[:, :], d2_row[:, :], s[:, 0, :], ALU.add).then_inc(setup_dve, 1)

            def own(name, b):
                return post_dve.at(name, b)

            def post(b, par, more):
                for c0 in (0, 2):
                    yield c0
                    for c in (c0, c0 + 1):
                        dve.wait_ge(*scan_sum.at(NU - KI + c, b))
                        dve.scalar_tensor_tensor(u[par][:, c, :], u[par][:, c, :], d_skip[:, c:c + 1], Y[c][:, :],
                                                 ALU.mult, ALU.add).then_inc(post_dve.did(f"y_a{c}"), 1)
                    for c in (c0, c0 + 1):
                        dve.wait_ge(*own(f"y_a{c}", b))
                        dve.tensor_tensor(u[par][:, c, :], u[par][:, c, :], g[par][:, c, :], ALU.mult)\
                            .then_inc(post_dve.did(f"y_b{c}"), 1)
                yield 8
                dve.wait_ge(*post_pe.at("m1", b))
                dve.wait_ge(x1_stored, 16 * (b + 1))
                for i in range(2):
                    last = dve.tensor_tensor(h[:, 2 * i:2 * i + 2, :], PB[i][:, :].rearrange("p (a d) -> p a d", a=2),
                                             xin[par][:, 2 * i:2 * i + 2, :], ALU.add)
                last.then_inc(post_dve.did("h_sum"), 1)
                yield 9
                dve.wait_ge(*own("h_sum", b))
                stats(post_dve, "h", h, stat, mv, b)
                yield 11
                dve.wait_ge(*post_pool.at("h_r", b))
                normalise(h, h, mv, r).then_inc(post_dve.did("h_normed"), 1)
                yield 18
                dve.wait_ge(*post_pe.at("q", b))
                for i in range(2):
                    last = dve.tensor_tensor(q[:, 2 * i:2 * i + 2, :], PB[i][:, :].rearrange("p (a d) -> p a d", a=2),
                                             rows["q_b"][:, :].unsqueeze(1).to_broadcast([P, 2, D]), ALU.add)
                last.then_inc(post_dve.did("q_sum"), 1)
                yield 20
                dve.wait_ge(*post_pool.at("h_b", b))
                stats(post_dve, "hi", h, stat, mv, b)
                yield 22
                dve.wait_ge(*post_pool.at("hi_r", b))
                normalise(li, h, mv, r).then_inc(post_dve.did("li"), 1)
                yield 26
                dve.wait_ge(*post_act.at("q_gelu", b))
                dve.wait_ge(*post_pe.at("ssk", b))
                for tile in range(TT):
                    last = dve.tensor_tensor_reduce(out=junk_dve[:, tile, :], in0=q[:, tile, :], in1=rows["w_g"][:, :],
                                                    scale=D ** -0.5, scalar=0.0, op0=ALU.mult, op1=ALU.add,
                                                    accum_out=qw[:, tile:tile + 1])
                last.then_inc(post_dve.did("qw"), 1)
                dve.wait_ge(*own("qw", b))
                dve.tensor_tensor(qw2[:, :], qw[:, :], qw[:, :], ALU.mult).then_inc(post_dve.did("qw2"), 1)
                dve.tensor_copy(ssk[:, :], PB[0][:, 0:TT]).then_inc(post_dve.did("ssk"), 1)
                yield 30
                dve.wait_ge(*post_pe.at("G", b))
                dve.tensor_reduce(ssg[:, :], PB[1][:, 8:8 + TT], AX_X, ALU.add).then_inc(post_dve.did("ssg"), 1)
                yield 33
                dve.wait_ge(*post_pool.at("G_r", b))
                dve.tensor_scalar(gcol[:, :], PB[1][:, 0:KD], rg[:, 0:1], None, ALU.mult)\
                    .then_inc(post_dve.did("G"), 1)
                dve.wait_ge(*own("G", b))
                for c in range(KD):
                    last = dve.tensor_scalar(proj_g[:, c, :], pr_w[:, c, :], gcol[:, c:c + 1], None, ALU.mult)
                last.then_inc(post_dve.did("proj_g"), 1)
                yield 37
                dve.wait_ge(*post_pe.at("hs", b))
                dve.wait_ge(*sp_sent.at("sent", b - 1))
                for tile in range(TT):
                    last = dve.scalar_tensor_tensor(tb[:, tile, :], PB[tile // 2][:, (tile % 2) * D:(tile % 2 + 1) * D],
                                                    rk[:, tile:tile + 1], rows["pr_b"][:, :], ALU.mult, ALU.add)
                last.then_inc(post_dve.did("t"), 1)
                yield 46
                dve.wait_ge(*post_pe.at("fl", b))
                dve.wait_ge(*post_pool.at("h_fl", b))
                for i in range(2):
                    last = dve.tensor_tensor(s[:, 2 * i:2 * i + 2, :], PB[i][:, :].rearrange("p (a d) -> p a d", a=2),
                                             h[:, 2 * i:2 * i + 2, :], ALU.add)
                last.then_inc(post_dve.did("s_sum"), 1)
                dve.wait_ge(*own("s_sum", b))
                stats(post_dve, "s", s, stat, mv, b)
                yield 49
                dve.wait_ge(*post_pool.at("s_r", b))
                normalise(s, s, mv, r).then_inc(post_dve.did("s_normed"), 1)
                for i in range(2):
                    yield 69 + 4 * i
                    dve.wait_ge(*post_pe.at(f"d2_{2 * i + 1}", b))
                    if i == 0:
                        dve.wait_ge(*post_pool.at("s_b", b))
                    part_s = s[:, 2 * i:2 * i + 2, :]
                    dve.tensor_tensor(part_s, PB[i][:, :].rearrange("p (a d) -> p a d", a=2), part_s, ALU.add)\
                        .then_inc(post_dve.did(f"f_sum{i}"), 1)
                dve.wait_ge(*own("f_sum1", b))
                stats(post_dve, "f", s, stat, mv, b)
                yield 76
                dve.wait_ge(*post_pool.at("f_r", b))
                normalise(s, s, mv, r).then_inc(post_dve.did("f_normed"), 1)
                yield 80
                dve.wait_ge(*post_pool.at("f_b", b))
                stats(post_dve, "o", s, stat, mv, b)
                yield 82
                dve.wait_ge(*post_pool.at("o_r", b))
                normalise(s, s, mv, r).then_inc(post_dve.did("o_normed"), 1)
                yield 84
                dve.wait_ge(*post_pool.at("x1", b))
                stats(post_dve, "n", h, stat, mv, b)
                yield 86
                dve.wait_ge(*post_pool.at("n_r", b))
                normalise(tb, h, mv, r).then_inc(post_dve.did("n_normed"), 1)
                yield 90
                dve.wait_ge(*post_pe.at("dots", b))
                dve.tensor_copy(dots[:, :, :], PB[0][:, 0:TT * NE].rearrange("p (t e) -> p t e", t=TT))\
                    .then_inc(post_dve.did("dots"), 1)
                dve.wait_ge(*own("dots", b))
                dve.sem_inc(carried_dve, 1)
                for tile in range(TT):
                    last = dve.max(top[:, tile, :], dots[:, tile, :])
                last.then_inc(post_dve.did("top"), 1)
                dve.wait_ge(*own("top", b))
                dve.sem_inc(carried_dve, 1)
                for tile in range(TT):
                    last = dve.max_index(top_i[:, tile, :], top[:, tile, :], dots[:, tile, :])
                last.then_inc(post_dve.did("top_i"), 1)
                dve.tensor_tensor(dv[:, :], top[:, :, 1], top[:, :, 0], ALU.subtract).then_inc(post_dve.did("dv"), 1)
                dve.wait_ge(*own("top_i", b))
                dve.tensor_copy(top_f[:, :, :], top_i[:, :, 0:2]).then_inc(post_dve.did("top_f"), 1)
                yield 92
                dve.wait_ge(*post_act.at("e2", b))
                dve.tensor_scalar(den[:, :], e2[:, :], 1.0, None, ALU.add).then_inc(post_dve.did("den"), 1)
                dve.wait_ge(*own("den", b))
                dve.reciprocal(wts[:, :, 0], den[:, :]).then_inc(post_dve.did("w1"), 1)
                dve.wait_ge(*own("w1", b))
                dve.tensor_tensor(wts[:, :, 1], e2[:, :], wts[:, :, 0], ALU.mult).then_inc(post_dve.did("w2"), 1)
                dve.wait_ge(*own("w2", b))
                dve.tensor_scalar(pos2[:, :], wts[:, :, 1], 0.0, None, ALU.is_gt).then_inc(post_dve.did("pos2"), 1)
                for i in range(2):
                    dve.tensor_tensor(oh[i][:, :, :], iota8[:, :].unsqueeze(1).to_broadcast([P, TT, NE]),
                                      top_f[:, :, i:i + 1].to_broadcast([P, TT, NE]), ALU.is_equal)\
                        .then_inc(post_dve.did(f"oh{i}"), 1)
                dve.wait_ge(*own("oh1", b))
                dve.tensor_tensor(oh[1][:, :, :], oh[1][:, :, :], pos2[:, :].unsqueeze(2).to_broadcast([P, TT, NE]),
                                  ALU.mult).then_inc(post_dve.did("oh1_pos"), 1)
                dve.wait_ge(*own("oh1_pos", b))
                dve.tensor_tensor(asg[:, :, :], oh[0][:, :, :], oh[1][:, :, :], ALU.add)\
                    .then_inc(post_dve.did("asg"), 1)
                yield 94
                dve.wait_ge(*post_pe.at("cum", b))
                dve.tensor_tensor(cum[:, :, :], PB[1][:, 0:TT * NE].rearrange("p (t e) -> p t e", t=TT),
                                  run[:, :].unsqueeze(1).to_broadcast([P, TT, NE]), ALU.add)\
                    .then_inc(post_dve.did("cum"), 1)
                dve.wait_ge(*own("cum", b))
                dve.tensor_scalar(keep[:, :, :], cum[:, :, :], float(CAP), None, ALU.is_le)\
                    .then_inc(post_dve.did("keep"), 1)
                dve.tensor_tensor(run[:, :], PB[1][:, TT * NE:(TT + 1) * NE], run[:, :], ALU.add)\
                    .then_inc(post_dve.did("run"), 1)
                dve.tensor_tensor(cum[:, :, :], cum[:, :, :], slot0[:, :].unsqueeze(1).to_broadcast([P, TT, NE]),
                                  ALU.add).then_inc(post_dve.did("slotv"), 1)
                dve.wait_ge(*own("slotv", b))
                dve.tensor_tensor(cum[:, :, :], cum[:, :, :], keep[:, :, :], ALU.mult)\
                    .then_inc(post_dve.did("slotk"), 1)
                dve.wait_ge(*own("slotk", b))
                for i in range(2):
                    dve.tensor_tensor(pick[i][:, :, :], cum[:, :, :], oh[i][:, :, :], ALU.mult)\
                        .then_inc(post_dve.did(f"pick{i}"), 1)
                for i in range(2):
                    dve.wait_ge(*own(f"pick{i}", b))
                    dve.tensor_reduce(slot_f[:, :, i], pick[i][:, :, :], AX_X, ALU.add)\
                        .then_inc(post_dve.did(f"slot{i}"), 1)
                dve.wait_ge(*own("slot1", b))
                dve.tensor_scalar(idx[:, :, :], slot_f[:, :, :], FAR, None, ALU.add).then_inc(post_dve.did("idx"), 1)
                dve.wait_ge(*own("idx", b))
                dve.tensor_copy(idx_all[:, bass.ds(b * TT, TT), :], idx[:, :, :]).then_inc(post_dve.did("idx_all"), 1)
                dve.tensor_copy(w_all[:, bass.ds(b * TT, TT), :], wts[:, :, :]).then_inc(post_dve.did("w_all"), 1)

            all_sequences(dve, pre, scan, post)


def expert_phase(nc, t, env, sem):
    D, NE, EI, KD, KE, CAP, TB, QB, BLK = (env[k] for k in ("D", "NE", "EI", "KD", "KE", "CAP", "TB", "QB", "BLK"))
    ident, bank, xe_v, ye_v = (env[k] for k in ("ident", "bank", "xe_v", "ye_v"))
    NB = 2 * QB
    with ExitStack() as ctx:
        def sb(name, shape, dt=F32):
            return ctx.enter_context(nc.sbuf_tensor(name, shape, dt))

        w1 = [sb(f"w1_{i}", [P, KD, EI]) for i in range(2)]
        w2 = [sb(f"w2_{i}", [P, KE, D]) for i in range(2)]
        X = [sb(f"X{i}", [P, TB, D]) for i in range(2)]
        XT = [sb(f"XT{i}", [P, KD, BLK]) for i in range(2)]
        I = [sb(f"I{i}", [P, KE, BLK]) for i in range(2)]
        O = [sb(f"O{i}", [P, TB, D]) for i in range(2)]
        XB, MB, OB = bank[0:2], bank[2:6], bank[6:8]

        carried_sp_e = sem("carried_sp_e")
        w_loaded = [sem(f"w_loaded{i}") for i in range(2)]
        slots_loaded = [sem(f"slots_loaded{i}") for i in range(2)]
        stored = [sem(f"stored{i}") for i in range(2)]
        e_turn = Steps(sem("e_turn"), range(NB))
        e_turned = Steps(sem("e_turned"), range(NB))
        e_mm1 = Steps(sem("e_mm1"), range(NB * KE))
        e_relu_act = Steps(sem("e_relu_act"), range(NB * KE // 2))
        e_relu_dve = Steps(sem("e_relu_dve"), range(NB * KE // 2))
        e_mm2 = Steps(sem("e_mm2"), range(NB))
        e_out = Steps(sem("e_out"), range(NB))

        def before(steps, n, back, i):
            return steps.at(n - back, i) if n >= back else steps.at(len(steps.names) + n - back, i - 1)

        block = ctx.enter_context(nc.Block())

        @block.sync
        def _(sp):
            with sp.Fori(0, NE // 2) as i:
                for n in range(NB):
                    e, q = divmod(n, QB)
                    if q == 0:
                        sp.wait_ge(*e_mm2.at(n + QB - 1, i - 1))
                        sp.sem_inc(carried_sp_e, 1)
                        sp.dma_start(w1[e][:, :, :], t["e1_w"][2 * i + e].rearrange("(k p) n -> p k n", p=P))\
                            .then_inc(w_loaded[e], 16)
                        sp.dma_start(w2[e][:, :, :], t["e2_w"][2 * i + e].rearrange("(k p) n -> p k n", p=P))\
                            .then_inc(w_loaded[e], 16)
                    sp.wait_ge(*before(e_turn, n, 2, i))
                    sp.sem_inc(carried_sp_e, 1)
                    sp.dma_start(X[n % 2][:, :, :], xe_v[i * NB + n]).then_inc(slots_loaded[n % 2], 16)

        @block.tensor
        def _(pe):
            for steps in (e_turn, e_mm1, e_mm2):
                steps.credit(pe)

            def turn(n, i):
                pe.wait_ge(slots_loaded[n % 2], 16 * (NB // 2) * i + 16 * (n // 2 + 1))
                pe.wait_ge(*before(e_turned, n, 1, i))
                for c in range(KD):
                    for tile in range(TB):
                        last = pe.transpose(XB[c][:, tile * P:(tile + 1) * P], X[n % 2][:, tile, c * P:(c + 1) * P],
                                            ident[:, :])
                last.then_inc(e_turn.did(n), 1)

            with pe.Fori(0, NE // 2) as i:
                turn(0, i)
                for n in range(NB):
                    e = n // QB
                    if n % QB == 0:
                        pe.wait_ge(w_loaded[e], 32 * (i + 1))
                    pe.wait_ge(*e_turned.at(n, i))
                    for m in range(KE):
                        relu = e_relu_act if m % 2 == 0 else e_relu_dve
                        pe.wait_ge(*before(relu, n * KE // 2 + m // 2, KE // 2, i))
                        for c in range(KD):
                            last = pe.matmul(MB[m][:, 0:BLK], w1[e][:, c, m * P:(m + 1) * P], XT[n % 2][:, c, :],
                                             start=c == 0, stop=c == KD - 1)
                        last.then_inc(e_mm1.did(n * KE + m), 1)
                    if n + 1 < NB:
                        turn(n + 1, i)
                    pe.wait_ge(*e_relu_act.at(n * KE // 2 + KE // 2 - 1, i))
                    pe.wait_ge(*e_relu_dve.at(n * KE // 2 + KE // 2 - 1, i))
                    pe.wait_ge(*before(e_out, n, 1, i))
                    for tile in range(TB):
                        for c in range(KE):
                            last = pe.matmul(OB[tile // 2][:, (tile % 2) * D:(tile % 2 + 1) * D],
                                             I[n % 2][:, c, tile * P:(tile + 1) * P], w2[e][:, c, :],
                                             start=c == 0, stop=c == KE - 1)
                    last.then_inc(e_mm2.did(n), 1)

        @block.scalar
        def _(act):
            for steps in (e_turned, e_relu_act):
                steps.credit(act)
            for half in range(2):
                act.sem_inc(stored[half], 16)
            with act.Fori(0, NE // 2) as i:
                def copy_turned(n):
                    act.wait_ge(*e_turn.at(n, i))
                    act.wait_ge(*before(e_mm1, n * KE + KE - 1, 2 * KE, i))
                    for c in range(KD):
                        last = act.copy(XT[n % 2][:, c, :], XB[c][:, 0:BLK])
                    last.then_inc(e_turned.did(n), 1)

                copy_turned(0)
                for n in range(NB):
                    act.wait_ge(*before(e_mm2, n, 2, i))
                    for m in range(0, KE, 2):
                        act.wait_ge(*e_mm1.at(n * KE + m, i))
                        act.activation(I[n % 2][:, m, :], MB[m][:, 0:BLK], ACT.Relu)\
                            .then_inc(e_relu_act.did(n * KE // 2 + m // 2), 1)
                    if n + 1 < NB:
                        copy_turned(n + 1)
                    act.wait_ge(*e_out.at(n, i))
                    act.dma_start(ye_v[i * NB + n], O[n % 2][:, :, :]).then_inc(stored[n % 2], 16)
            for half in range(2):
                act.wait_ge(stored[half], 16 * (NE // 2) * (NB // 2) + 16)

        @block.vector
        def _(dve):
            for steps in (e_relu_dve, e_out):
                steps.credit(dve)
            with dve.Fori(0, NE // 2) as i:
                for n in range(NB):
                    dve.wait_ge(*before(e_mm2, n, 2, i))
                    for m in range(1, KE, 2):
                        dve.wait_ge(*e_mm1.at(n * KE + m, i))
                        dve.tensor_scalar(I[n % 2][:, m, :], MB[m][:, 0:BLK], 0.0, None, ALU.max)\
                            .then_inc(e_relu_dve.did(n * KE // 2 + m // 2), 1)
                    dve.wait_ge(*e_mm2.at(n, i))
                    dve.wait_ge(stored[n % 2], 16 * (NB // 2) * i + 16 * (n // 2 + 1))
                    for tile in range(0, TB, 2):
                        last = dve.tensor_copy(O[n % 2][:, tile:tile + 2, :],
                                               OB[tile // 2][:, :].rearrange("p (a d) -> p a d", a=2))
                    last.then_inc(e_out.did(n), 1)


def combine_phase(nc, t, env, sem):
    S, D, TT, NSLOT = (env[k] for k in ("S", "D", "TT", "NSLOT"))
    idx_all, w_all, eps5, ye_dram, x1_v, out_v = (
        env[k] for k in ("idx_all", "w_all", "eps5", "ye_dram", "x1_v", "out_v"))
    with ExitStack() as ctx:
        def sb(name, shape, dt=F32):
            return ctx.enter_context(nc.sbuf_tensor(name, shape, dt))

        rows = [[sb(f"rows{i}_{c}", [P, TT, D]) for c in range(2)] for i in range(2)]
        idx_c = [sb(f"idx_c{i}", [P, TT, 2], U32) for i in range(2)]
        w_c = [sb(f"w_c{i}", [P, TT, 2]) for i in range(2)]
        x1 = [sb(f"x1_{i}", [P, TT, D]) for i in range(2)]
        stat = [sb(f"c_stat{i}", [P, TT, 6]) for i in range(2)]
        mv = [sb(f"c_mv{i}", [P, TT, 2]) for i in range(2)]
        r = [sb(f"c_r{i}", [P, TT]) for i in range(2)]

        gathered = [sem(f"gathered{i}") for i in range(2)]
        gathers_begun = sem("gathers_begun")
        carried = sem("carried")
        carried_sp_c = sem("carried_sp_c")
        x1_loaded = [sem(f"x1_loaded{i}") for i in range(2)]
        out_stored = [sem(f"out_stored{i}") for i in range(2)]
        ready = Steps(sem("c_ready"), range(2))
        dve_s = Steps(sem("c_dve"), [f"{n}{par}" for par in range(2) for n in
                                     ("scaled", "sum", "stats", "aggr", "normed", "out")])
        act_s = Steps(sem("c_act"), [f"{n}{par}" for par in range(2) for n in ("ln", "r")])
        block = ctx.enter_context(nc.Block())

        @block.sync
        def _(sp):
            for par in range(2):
                sp.sem_inc(out_stored[par], 16)
            with sp.Fori(0, S // 2) as i:
                for par in range(2):
                    sp.wait_ge(out_stored[par], 16 * (i + 1))
                    sp.sem_inc(carried_sp_c, 1)
                    sp.dma_start(x1[par][:, :, :], x1_v[2 * i + par]).then_inc(x1_loaded[par], 16)
                    if par == 1:
                        for half in range(2):
                            sp.wait_ge(*dve_s.at(f"out{half}", i))
                            sp.sem_inc(carried_sp_c, 1)
                            sp.dma_start(out_v[2 * i + half], x1[half][:, :, :]).then_inc(out_stored[half], 16)
            for par in range(2):
                sp.wait_ge(out_stored[par], 16 * (S // 2 + 1))

        @block.gpsimd
        def _(pool):
            with pool.Fori(0, S // 2) as i:
                for par in range(2):
                    pool.wait_ge(*ready.at(par, i))
                    pool.sem_inc(gathers_begun, 1)
                    for tile in range(TT):
                        for c in range(2):
                            pool.indirect_dma_start(
                                out=rows[par][c][:, tile, :], out_offset=None, in_=ye_dram,
                                in_offset=bass.IndirectOffsetOnAxis(ap=idx_c[par][:, tile, c:c + 1], axis=0),
                                bounds_check=NSLOT - 1, oob_is_err=False).then_inc(gathered[par], 16)

        @block.scalar
        def _(act):
            act_s.credit(act)
            with act.Fori(0, S // 2) as i:
                for par in range(2):
                    act.wait_ge(*dve_s.at(f"aggr{par}", i))
                    act.activation(r[par][:, :], mv[par][:, :, 1], ACT.Ln, bias=eps5[:, 0:1])\
                        .then_inc(act_s.did(f"ln{par}"), 1)
                    act.wait_ge(*act_s.at(f"ln{par}", i))
                    act.activation(r[par][:, :], r[par][:, :], ACT.Exp, scale=-0.5).then_inc(act_s.did(f"r{par}"), 1)

        @block.vector
        def _(dve):
            for steps in (ready, dve_s):
                steps.credit(dve)

            def prepare(par, i):
                dve.wait_ge(*dve_s.at(f"out{par}", i - 1))
                for c in range(2):
                    dve.memset(rows[par][c][:, :, :], 0.0)
                dve.tensor_copy(w_c[par][:, :, :], w_all[:, bass.ds((2 * i + par) * TT, TT), :])
                dve.tensor_copy(idx_c[par][:, :, :], idx_all[:, bass.ds((2 * i + par) * TT, TT), :])\
                    .then_inc(ready.did(par), 1)

            def combine(par, i):
                a, b = rows[par]
                dve.wait_ge(gathered[par], 16 * 2 * TT * (i + 1))
                dve.wait_ge(*ready.at(par, i))
                for tile in range(TT):
                    last = dve.tensor_scalar(a[:, tile, :], a[:, tile, :], w_c[par][:, tile, 0:1], None, ALU.mult)
                last.then_inc(dve_s.did(f"scaled{par}"), 1)
                dve.wait_ge(*dve_s.at(f"scaled{par}", i))
                for tile in range(TT):
                    last = dve.scalar_tensor_tensor(a[:, tile, :], b[:, tile, :], w_c[par][:, tile, 1:2],
                                                    a[:, tile, :], ALU.mult, ALU.add)
                last.then_inc(dve_s.did(f"sum{par}"), 1)
                dve.wait_ge(*dve_s.at(f"sum{par}", i))
                for tile in range(TT):
                    last = dve.bn_stats(stat[par][:, tile, :], a[:, tile, :])
                last.then_inc(dve_s.did(f"stats{par}"), 1)
                dve.wait_ge(*dve_s.at(f"stats{par}", i))
                dve.sem_inc(carried, 1)
                for tile in range(TT):
                    last = dve.bn_aggr(mv[par][:, tile, :], stat[par][:, tile, :])
                last.then_inc(dve_s.did(f"aggr{par}"), 1)
                dve.wait_ge(*act_s.at(f"r{par}", i))
                for tile in range(TT):
                    last = dve.tensor_scalar(a[:, tile, :], a[:, tile, :], mv[par][:, tile, 0:1],
                                             r[par][:, tile:tile + 1], ALU.subtract, ALU.mult)
                last.then_inc(dve_s.did(f"normed{par}"), 1)
                dve.wait_ge(*dve_s.at(f"normed{par}", i))
                dve.wait_ge(x1_loaded[par], 16 * (i + 1))
                dve.tensor_tensor(x1[par][:, :, :], x1[par][:, :, :], a[:, :, :], ALU.add)\
                    .then_inc(dve_s.did(f"out{par}"), 1)

            for par in range(2):
                prepare(par, 0)
            with dve.Fori(0, S // 2 - 1) as i:
                for par in range(2):
                    combine(par, i)
                    prepare(par, i + 1)
            for par in range(2):
                combine(par, S // 2 - 1)


def kernel(**inputs):
    import numpy as _np
    import concourse.bacc as _bacc
    from concourse import mybir as _mybir
    from concourse.bass_utils import run_bass_kernel_spmd as _run

    def a(name):
        return _np.asarray(inputs[f"L0_attn_{name}"])

    def f(name):
        return _np.asarray(inputs[f"L0_ffn_{name}"])

    host = {"x": a("input_tensor"), "in_w": a("in_proj_w").T, "conv_w": a("conv_w"), "conv_b": a("conv_b"),
            "xp_w": a("x_proj_w").T, "dt_w": a("dt_proj_w").T, "dt_b": a("dt_proj_b"), "A_log": a("A_log"),
            "D_skip": a("D_skip"), "out_w": a("out_proj_w").T, "ln0_g": a("ln0_g"), "ln0_b": a("ln0_b"),
            "q_w": a("q_w").T, "q_b": a("q_b"), "k_w": a("k_w").T, "k_b": a("k_b"), "w_g": a("w_g").reshape(-1),
            "pr_w": a("proj_w").T, "pr_b": a("proj_b"), "fl_w": a("fl_w").T, "fl_b": a("fl_b"),
            "lni_g": a("lni_g"), "lni_b": a("lni_b"), "ln1_g": a("ln1_g"), "ln1_b": a("ln1_b"),
            "d1_w": a("d1_w").T, "d1_b": a("d1_b"), "d2_w": a("d2_w").T, "d2_b": a("d2_b"),
            "ln2_g": a("ln2_g"), "ln2_b": a("ln2_b"), "emb": f("expert_embeddings").T,
            "e1_w": f("first_linear").transpose(0, 2, 1), "e2_w": f("second_linear").transpose(0, 2, 1)}
    nc = _bacc.Bacc("TRN2", target_bir_lowering=False, num_devices=1)
    arrays, t = {}, {}
    for name, value in host.items():
        value = _np.ascontiguousarray(value)
        arrays[f"in_{name}"] = value
        t[name] = nc.dram_tensor(f"in_{name}", value.shape, _mybir.dt.from_np(value.dtype), kind="ExternalInput").ap()
    t["out"] = nc.dram_tensor("out_0", host["x"].shape, _mybir.dt.float32, kind="ExternalOutput").ap()
    build(nc, t)
    result = _run(nc, [arrays], core_ids=[0])
    return result.results[0]["out_0"]
```

```python
from contextlib import ExitStack

import concourse.bass as bass
from concourse import mybir

ALU = mybir.AluOpType
ACT = mybir.ActivationFunctionType
F32 = mybir.dt.float32
BF16 = mybir.dt.bfloat16
U32 = mybir.dt.uint32
AX_X = mybir.AxisListType.X

P = 128
LEAD = 2
LN_EPS = 1e-5
EPS = 1e-12


class Steps:

    def __init__(self, sem, names):
        self.sem, self.names, self.next = sem, list(names), 0

    def did(self, name):
        assert self.names[self.next % len(self.names)] == name, (name, self.names[self.next % len(self.names)])
        self.next += 1
        return self.sem

    def value(self, index, n):
        return (n + LEAD) * len(self.names) + index + 1

    def at(self, name, n):
        return self.sem, self.value(self.names.index(name), n)

    def credit(self, engine):
        engine.sem_inc(self.sem, LEAD * len(self.names))


class Stage:

    def __init__(self, instructions):
        self.instructions = instructions
        self.slot = next(instructions, None)

    def run_to(self, slot):
        while self.slot is not None and self.slot <= slot:
            self.slot = next(self.instructions, None)


def build(nc, t):
    S, L, D = t["x"].shape
    DI = t["conv_w"].shape[0]
    NS = t["A_log"].shape[1]
    R = t["dt_w"].shape[0]
    FF = t["d1_w"].shape[1]
    NE, _, EI = t["e1_w"].shape
    TT = L // P
    KD, KI, KF, KE = D // P, DI // P, FF // P, EI // P
    NX = R + 2 * NS
    NTOK = S * L
    CAP = -(-NTOK // NE)
    NSLOT = NE * CAP
    BLK = min(512, CAP)
    TB = BLK // P
    QB = CAP // BLK
    FAR = float(1 << 20)
    assert S % 4 == 0 and L == 512 and CAP % BLK == 0 and NSLOT % (16 * P) == 0 and S >= 4

    NP2 = NS // 2
    NU = NP2 * KI
    RING = 4
    SUMS = 2

    x_v = t["x"].rearrange("s (t p) d -> s p t d", p=P)
    out_v = t["out"].rearrange("s (t p) d -> s p t d", p=P)
    bc_dram = [nc.dram_tensor(f"bc_rows{i}", (2 * NS, L), F32, kind="Internal").ap() for i in range(2)]
    xn_dram = [nc.dram_tensor(f"xn_rows{i}", (L, D), F32, kind="Internal").ap() for i in range(2)]
    xn_v = [rows.rearrange("(t p) d -> p t d", p=P) for rows in xn_dram]
    x1_dram = nc.dram_tensor("x1_rows", (S, L, D), F32, kind="Internal").ap()
    x1_v = x1_dram.rearrange("s (t p) d -> s p t d", p=P)
    xe_dram = nc.dram_tensor("expert_in", (NSLOT, D), F32, kind="Internal").ap()
    ye_dram = nc.dram_tensor("expert_out", (NSLOT, D), F32, kind="Internal").ap()
    xe_zero_v = xe_dram.rearrange("(a p r) d -> a p (r d)", p=P, r=16)
    xe_v = xe_dram.rearrange("(n t p) d -> n p t d", t=TB, p=P)
    ye_v = ye_dram.rearrange("(n t p) d -> n p t d", t=TB, p=P)

    with ExitStack() as whole:
        def sem(name):
            return whole.enter_context(nc.semaphore(name))

        idx_all = whole.enter_context(nc.sbuf_tensor("idx_all", [P, S * TT, 2], U32))
        w_all = whole.enter_context(nc.sbuf_tensor("w_all", [P, S * TT, 2], F32))
        ident = whole.enter_context(nc.sbuf_tensor("ident", [P, P], F32))
        ones = whole.enter_context(nc.sbuf_tensor("ones", [P, P], F32))
        eps5 = whole.enter_context(nc.sbuf_tensor("eps5", [P, 1], F32))
        bank = [whole.enter_context(nc.psum_tensor(f"bank{i}", [P, 512], F32)) for i in range(8)]

        attention_phase(nc, t, dict(locals()), sem)
        expert_phase(nc, t, dict(locals()), sem)
        combine_phase(nc, t, dict(locals()), sem)


def attention_phase(nc, t, env, sem):
    S, L, D, DI, NS, R, NE, TT = (env[k] for k in ("S", "L", "D", "DI", "NS", "R", "NE", "TT"))
    KD, KI, KF, NX, CAP, NSLOT, FAR = (env[k] for k in ("KD", "KI", "KF", "NX", "CAP", "NSLOT", "FAR"))
    NP2, NU, RING, SUMS = (env[k] for k in ("NP2", "NU", "RING", "SUMS"))
    x_v, xn_v, x1_v, xe_dram, bc_dram, xe_zero_v = (
        env[k] for k in ("x_v", "xn_v", "x1_v", "xe_dram", "bc_dram", "xe_zero_v"))
    idx_all, w_all, ident, ones, eps5, bank = (
        env[k] for k in ("idx_all", "w_all", "ident", "ones", "eps5", "bank"))
    Y, RB, PB = bank[0:4], bank[4:6], bank[6:8]
    FB = [*PB, *RB]

    with ExitStack() as ctx:
        def sb(name, shape, dt=F32):
            return ctx.enter_context(nc.sbuf_tensor(name, shape, dt))

        in_w = sb("in_w", [P, KD, 2 * DI])
        xp_w = sb("xp_w", [P, KI, NX])
        dt_w = sb("dt_w", [R, DI])
        out_w = sb("out_w", [P, KI, D])
        q_w = sb("q_w", [P, KD, D])
        k_w = sb("k_w", [P, KD, D])
        pr_w = sb("pr_w", [P, KD, D])
        fl_w = sb("fl_w", [P, KD, D])
        d1_w = sb("d1_w", [P, KD, KF * P])
        d2_w = sb("d2_w", [P, KF, D])
        emb = sb("emb", [P, KD, NE])
        conv_w = sb("conv_w", [P, KI, 4])
        conv_b = sb("conv_b", [P, KI])
        dt_b = sb("dt_b", [P, KI])
        a_neg = sb("a_neg", [P, KI, NS])
        d_skip = sb("d_skip", [P, KI])
        k_b = sb("k_b", [P, KD])
        g0f = sb("g0f", [P, KD])
        b0f = sb("b0f", [P, KD])
        g1f = sb("g1f", [P, KD])
        b1f = sb("b1f", [P, KD])
        d1_b = sb("d1_b", [P, KF])
        rows = {n: sb(f"row_{n}", [P, D]) for n in
                ("q_b", "pr_b", "fl_b", "ln0_g", "ln0_b", "lni_g", "lni_b", "ln1_g", "ln2_g", "ln2_b", "w_g")}
        d2_row = sb("d2_row", [P, D])
        tri = sb("tri", [P, P], BF16)
        ones_bf = sb("ones_bf", [P, P], BF16)
        iota8 = sb("iota8", [P, NE])
        slot0 = sb("slot0", [P, NE])
        xin = sb("xin", [P, TT, D])
        u = [sb(f"u{i}", [P, KI, L]) for i in range(2)]
        g = [sb(f"g{i}", [P, KI, L]) for i in range(2)]
        delta = [sb(f"delta{i}", [P, KI, L]) for i in range(2)]
        du = [sb(f"du{i}", [P, KI, L]) for i in range(2)]
        xT = [d[:, 0:KD, :] for d in du]
        xd = sb("xd", [NX, L])
        minus_half = sb("minus_half", [P, TT])
        x_res = sb("x_res", [P, TT, D])
        stat_late = sb("stat_late", [P, TT, 6])
        mv_late = sb("mv_late", [P, TT, 2])
        r_late = sb("r_late", [P, TT])
        shift_late = sb("shift_late", [P, TT])
        rest = sb("rest", [P, 2, L])
        bc = [[sb(f"{n}{i}", [P, 2, L]) for i in range(2)] for n in ("B_rows", "C_rows")]
        dA = [sb(f"dA{i}", [P, 2, L]) for i in range(2)]
        st = [sb(f"st{i}", [P, 2, L]) for i in range(RING)]
        stat_pre = sb("stat_pre", [P, TT, 6])
        mv_pre = sb("mv_pre", [P, TT, 2])
        r_pre = sb("r_pre", [P, TT])
        shift_pre = sb("shift_pre", [P, TT])
        F = sb("F", [P, KD, L])
        gT = sb("gT", [P, KF, L])
        h = sb("h", [P, TT, D])
        tb = sb("tb", [P, TT, D])
        s = tb
        pair_sum = [sb(f"pair_sum{i}", [P, L]) for i in range(SUMS)]
        gT_flat = gT[:, :, :].rearrange("p a b -> p (a b)")
        part = TT * D
        q = gT_flat[:, 0:part].rearrange("p (t d) -> p t d", t=TT)
        li = gT_flat[:, part:2 * part].rearrange("p (t d) -> p t d", t=TT)
        kT = gT_flat[:, 2 * part:3 * part].rearrange("p (k l) -> p k l", k=KD)
        ksq = gT_flat[:, 3 * part:4 * part].rearrange("p (k l) -> p k l", k=KD)
        proj_g = F[:, :, 0:D]
        junk_act = li
        junk_dve = gT_flat[:, 3 * part:4 * part].rearrange("p (t d) -> p t d", t=TT)
        stat = sb("stat", [P, TT, 6])
        mv = sb("mv", [P, TT, 2])
        r = sb("r", [P, TT])
        shift = sb("shift", [P, TT])
        ssq = sb("ssq", [P, TT])
        rq = sb("rq", [P, TT])
        ssk = sb("ssk", [P, TT])
        rk = sb("rk", [P, TT])
        qw = sb("qw", [P, TT])
        qw2 = sb("qw2", [P, TT])
        ssg = sb("ssg", [P, 1])
        rg = sb("rg", [P, 1])
        gcol = sb("gcol", [P, KD])
        dots = sb("dots", [P, TT, NE])
        top = sb("top", [P, TT, 8])
        top_i = sb("top_i", [P, TT, 8], U32)
        top_f = sb("top_f", [P, TT, 2])
        dv = sb("dv", [P, TT])
        e2 = sb("e2", [P, TT])
        den = sb("den", [P, TT])
        wts = sb("wts", [P, TT, 2])
        pos2 = sb("pos2", [P, TT])
        oh = [sb(f"oh{i}", [P, TT, NE]) for i in range(2)]
        asg = sb("asg", [P, TT, NE], BF16)
        cum = sb("cum", [P, TT, NE])
        keep = sb("keep", [P, TT, NE])
        pick = [sb(f"pick{i}", [P, TT, NE]) for i in range(2)]
        slot_f = sb("slot_f", [P, TT, 2])
        idx = sb("idx", [P, TT, 2], U32)
        run = sb("run", [P, NE])

        pre_weights_in = sem("pre_weights_in")
        post_weights_in = sem("post_weights_in")
        consts = sem("consts")
        setup_dve = sem("setup_dve")
        setup_act = sem("setup_act")
        x_loaded = sem("x_loaded")
        xd_stored = sem("xd_stored")
        bc_loaded = [[sem(f"{n}_loaded{i}") for i in range(2)] for n in "BC"]
        xr_loaded = sem("xr_loaded")
        xn_stored = sem("xn_stored")
        xn_loaded = sem("xn_loaded")
        x1_stored = sem("x1_stored")
        scattered = sem("scattered")
        carried_pool = sem("carried_pool")
        carried_sp = sem("carried_sp")
        carried_dve = sem("carried_dve")
        zero_tile = sem("zero_tile")
        zeroed = sem("zeroed")

        pre_dve = Steps(sem("pre_dve"), ["x_stats", "x_aggr"]
                        + [f"conv{c}_{j}" for c in range(KI) for j in range(3)]
                        + ["w0", "w2", "delta0", "delta2"])
        pre_act = Steps(sem("pre_act"), ["x_normed", "xT"] + [f"tap{c}" for c in range(KI)] + ["u"]
                        + [f"g{c}" for c in range(KI)] + ["xd"] + [f"z{c}" for c in range(KI)] + ["z_abs", "sp_exp0", "sp_exp2", "sp_ln0", "sp_ln2"])
        pre_pe = Steps(sem("pre_pe"), ["xT"] + [f"u{c}" for c in range(KI)] + [f"g{c}" for c in range(KI)]
                       + ["xd"] + [f"dt{c}" for c in range(KI)])
        pre_pool = Steps(sem("pre_pool"), ["x_m", "x_v", "x_r", "x_shift", "rest0", "log1p0", "rest2", "log1p2", "du0", "du2"])
        scan_exp = Steps(sem("scan_exp"), range(NU))
        scan_in = Steps(sem("scan_in"), range(NU))
        scan_h = Steps(sem("scan_h"), range(NU))
        scan_hc = Steps(sem("scan_hc"), range(NU))
        scan_sum = Steps(sem("scan_sum"), range(NU))
        scan_add = Steps(sem("scan_add"), range(NU))
        post_pe = Steps(sem("post_pe"), ["m0", "m1", "hT", "q", "k", "ssk", "G", "hs", "tT", "fl", "sT"]
                        + [f"d1_{j}" for j in range(KF)])
        late_pe = Steps(sem("late_pe"), [f"d2_{tile}" for tile in range(TT)] + ["nT", "dots", "cum"])
        post_act = Steps(sem("post_act"), ["h_normed", "hT", "q_sq", "kT", "k_sq", "q_gelu", "tT", "s_normed", "sT"]
                         + [f"gelu{j}" for j in range(KF)])
        late_act = Steps(sem("late_act"), ["o_normed", "n_normed", "nT", "e2"])
        post_dve = Steps(sem("post_dve"), [f"y_{a}{c}" for a in "ab" for c in (0, 1)]
                         + [f"y_{a}{c}" for a in "ab" for c in (2, 3)]
                         + ["h_sum", "h_stats", "h_aggr", "q_sum"]
                         + ["hi_stats", "hi_aggr", "li_g", "li", "qw", "qw2", "ssk", "ssg", "G", "proj_g", "t",
                            "s_sum", "s_stats", "s_aggr"])
        late_dve = Steps(sem("late_dve"), ["f_sum0", "f_sum1", "f_stats", "f_aggr",
                            "f_g", "f_normed", "o_stats", "o_aggr",
                                            "n_stats", "n_aggr", "dots", "top", "top_i", "dv", "top_f", "den", "w1", "w2", "pos2", "oh0", "oh1",
                            "oh1_pos", "asg", "w_all", "cum", "keep", "run", "slotv", "slotk", "pick0", "pick1",
                            "slot0", "slot1", "idx", "idx_all"])
        post_pool = Steps(sem("post_pool"), ["h_m", "h_v", "h_r", "h_shift", "h_g", "h_b", "q_v", "q_r", "hi_v", "hi_r",
                                             "G_v", "G_r", "k_v", "k_r", "h_fl", "t_li", "s_m", "s_v", "s_r", "s_shift"])
        late_pool = Steps(sem("late_pool"), ["s_g", "s_b", "f_v", "f_r", "o_m", "o_v", "o_r", "o_shift", "x1", "n_m", "n_v", "n_r", "n_shift"])
        sp_sent = Steps(sem("sp_sent"), ["sent"])

        def matrix(name):
            return t[name].rearrange("(k p) n -> p k n", p=P)

        def vectors(pairs):
            return [(dst[:, :], t[name].rearrange("(k p) -> p k", p=P)) for dst, name in pairs]

        PRE_IN = [(in_w[:, :, :], matrix("in_w")), (conv_w[:, :, :], matrix("conv_w")),
                  (a_neg[:, :, :], matrix("A_log")), (xp_w[:, :, :], matrix("xp_w")), (dt_w[:, :], t["dt_w"])]
        PRE_IN += vectors(((conv_b, "conv_b"), (dt_b, "dt_b")))
        POST_IN = [(dst[:, :, :], matrix(name)) for dst, name in
                   ((out_w, "out_w"), (q_w, "q_w"), (k_w, "k_w"), (pr_w, "pr_w"), (fl_w, "fl_w"), (d1_w, "d1_w"),
                    (d2_w, "d2_w"), (emb, "emb"))]
        POST_IN += vectors(((d_skip, "D_skip"), (k_b, "k_b"), (g0f, "ln0_g"), (b0f, "ln0_b"), (g1f, "ln1_g"),
                            (b1f, "ln1_b"), (d1_b, "d1_b")))
        POST_IN += [(rows[n][:, :], t[n].partition_broadcast(P)) for n in rows]
        POST_IN += [(d2_row[:, :], t["d2_b"].partition_broadcast(P)), (s[:, 0, :], t["ln1_b"].partition_broadcast(P))]

        SLOTS = 3

        def run_slots(stages, parts=None):
            stages = [Stage(stage) for stage in stages]
            for slot in range(SLOTS * NU):
                if parts is not None:
                    parts[slot % SLOTS](slot // SLOTS)
                for stage in stages:
                    stage.run_to(slot)

        def nothing(k):
            pass

        def all_sequences(engine, pre, scan, post, late):
            run_slots([pre(0, 0)])
            scan(0, 0, pre(1, 1))
            scan(1, 1, post(0, 0, True), pre(2, 0))
            with engine.Fori(0, (S - 4) // 2) as i:
                for par in range(2):
                    b = 2 * i + (2 + par)
                    scan(b, par, late(b - 2), post(b - 1, 1 - par, True), pre(b + 1, 1 - par))
            scan(S - 2, 0, late(S - 4), post(S - 3, 1, True), pre(S - 1, 1))
            scan(S - 1, 1, late(S - 3), post(S - 2, 0, False))
            run_slots([late(S - 2), post(S - 1, 1, False)])
            run_slots([late(S - 1)])

        block = ctx.enter_context(nc.Block())

        @block.sync
        def _(sp):
            sp.sem_inc(x1_stored, 16)
            sp_sent.credit(sp)
            for dst, src in PRE_IN:
                with nc.allow_non_contiguous_dma(reason="small per-channel vectors, once"):
                    sp.dma_start(dst, src).then_inc(pre_weights_in, 16)

            def load_rows(half, b, par, pair):
                src = bc_dram[par].rearrange("(s n) l -> s n l", s=2)[half, 2 * pair:2 * pair + 2, :]
                sp.dma_start(bc[half][pair % 2][:, :, :], src.partition_broadcast(P))\
                    .then_inc(bc_loaded[half][pair % 2], 16)

            def load_bc(b, par, pair):
                for half, used in ((0, scan_in), (1, scan_hc)):
                    k = (pair - 2) * KI + KI - 1
                    sp.wait_ge(*(used.at(k, b) if pair >= 2 else used.at(NU + k, b - 1)))
                    sp.sem_inc(carried_sp, 1)
                    load_rows(half, b, par, pair)

            def pre(b, par):
                yield 10
                if not isinstance(b, int) or b > 0:
                    sp.wait_ge(*pre_pe.at("xT", b - 1))
                    sp.sem_inc(carried_sp, 1)
                    sp.wait_ge(xn_stored, 16 * b)
                    sp.sem_inc(carried_sp, 1)
                sp.dma_start(xin[:, :, :], x_v[b]).then_inc(x_loaded, 16)
                yield 24
                sp.wait_ge(*pre_act.at("x_normed", b))
                sp.sem_inc(carried_sp, 1)
                sp.wait_ge(*post_dve.at("h_sum", b - 2))
                sp.sem_inc(carried_sp, 1)
                sp.dma_start(xn_v[par], xin[:, :, :]).then_inc(xn_stored, 16)
                yield 50
                sp.wait_ge(*pre_act.at("xd", b))
                sp.dma_start(bc_dram[par], xd[R:NX, :]).then_inc(xd_stored, 16)
                yield 94
                sp.wait_ge(xd_stored, 16 * (b + 1))
                sp.sem_inc(carried_sp, 1)
                load_bc(b, par, 0)

            def scan(b, par, *stages):
                def rows(k):
                    if k % KI == 0 and k // KI + 1 < NP2:
                        load_bc(b, par, k // KI + 1)
                run_slots(stages, (rows, nothing, nothing))

            def post(b, par, more):
                yield 7
                sp.wait_ge(*post_dve.at("s_sum", b - 1))
                sp.sem_inc(carried_sp, 1)
                sp.wait_ge(xn_stored, 16 * (b + 1))
                sp.sem_inc(carried_sp, 1)
                sp.dma_start(h[:, :, :], xn_v[par]).then_inc(xn_loaded, 16)
                yield 56
                sp.wait_ge(x1_stored, 16 * (b + 1))
                sp.sem_inc(carried_sp, 1)
                sp.wait_ge(*late_act.at("n_normed", b - 1))
                sp.sem_inc(carried_sp, 1)
                sp.dma_start(x_res[:, :, :], x_v[b]).then_inc(xr_loaded, 16)

            def late(b):
                yield 29
                sp.wait_ge(*late_pool.at("x1", b))
                sp.sem_inc(carried_sp, 1)
                sp.dma_start(x1_v[b], x_res[:, :, :]).then_inc(x1_stored, 16)
                yield 55
                sp.wait_ge(scattered, 16 * 2 * TT * (b + 1))
                sp.sem_inc(sp_sent.did("sent"), 1)

            all_sequences(sp, pre, scan, post, late)
            sp.wait_ge(x1_stored, 16 * (S + 1))

        @block.gpsimd
        def _(pool):
            pool.memset(ident[:, :], 0.0).then_inc(consts, 1)
            pool.memset(ones[:, :], 1.0).then_inc(consts, 1)
            pool.memset(ones_bf[:, :], 1.0).then_inc(consts, 1)
            pool.memset(tri[:, :], 1.0).then_inc(consts, 1)
            pool.memset(eps5[:, :], LN_EPS).then_inc(consts, 1)
            pool.memset(run[:, :], 0.0).then_inc(consts, 1)
            pool.memset(minus_half[:, :], -0.5).then_inc(consts, 1)
            for i in range(2):
                pool.memset(dA[i][:, :, 0:1], 0.0).then_inc(consts, 1)
            pool.iota(iota8[:, :], pattern=[[1, NE]], base=0, channel_multiplier=0,
                      allow_small_or_imprecise_dtypes=True).then_inc(consts, 1)
            pool.iota(slot0[:, :], pattern=[[CAP, NE]], base=-1 - int(FAR), channel_multiplier=0,
                      allow_small_or_imprecise_dtypes=True).then_inc(consts, 1)
            pool.wait_ge(consts, 11)
            pool.affine_select(out=ident[:, :], in_=ident[:, :], compare_op=ALU.not_equal, fill=1.0, base=0,
                               pattern=[[-1, P]], channel_multiplier=1).then_inc(consts, 1)
            pool.affine_select(out=tri[:, :], in_=tri[:, :], compare_op=ALU.is_ge, fill=0.0, base=0,
                               pattern=[[1, P]], channel_multiplier=-1).then_inc(consts, 1)
            for steps in (pre_pool, scan_hc, post_pool, late_pool):
                steps.credit(pool)

            def power(steps, name, out, value, least, op, b):
                pool.sem_inc(carried_pool, 1)
                pool.tensor_scalar(out[:, :], value, least, None, op).then_inc(steps.did(f"{name}_v"), 1)
                pool.wait_ge(*steps.at(f"{name}_v", b))
                pool.tensor_tensor(out[:, :], out[:, :], minus_half[:, 0:out.shape[1]], ALU.pow)\
                    .then_inc(steps.did(f"{name}_r"), 1)

            def scale_and_shift(steps, name, out, shifted, mv_t, eps, b):
                pool.sem_inc(carried_pool, 1)
                pool.tensor_scalar(shifted[:, :], mv_t[:, :, 0], -1.0, None, ALU.mult)\
                    .then_inc(steps.did(f"{name}_m"), 1)
                power(steps, name, out, mv_t[:, :, 1], eps, ALU.add, b)
                pool.wait_ge(*steps.at(f"{name}_r", b))
                pool.tensor_tensor(shifted[:, :], shifted[:, :], out[:, :], ALU.mult)\
                    .then_inc(steps.did(f"{name}_shift"), 1)

            def pre(b, par):
                yield 20
                pool.wait_ge(*pre_dve.at("x_aggr", b))
                scale_and_shift(pre_pool, "x", r_pre, shift_pre, mv_pre, LN_EPS, b)
                for c, slot in ((0, 61), (2, 69)):
                    yield slot
                    two = du[par][:, c:c + 2, :]
                    pool.wait_ge(*pre_dve.at(f"w{c}", b))
                    pool.tensor_tensor(rest[:, :, :], two, rest[:, :, :], ALU.subtract)\
                        .then_inc(pre_pool.did(f"rest{c}"), 1)
                    yield slot + 4
                    pool.wait_ge(*pre_act.at(f"sp_ln{c}", b))
                    pool.wait_ge(*pre_pool.at(f"rest{c}", b))
                    pool.tensor_tensor(two, two, rest[:, :, :], ALU.add).then_inc(pre_pool.did(f"log1p{c}"), 1)
                for c, slot in ((0, 82), (2, 88)):
                    yield slot
                    pool.wait_ge(*pre_dve.at(f"delta{c}", b))
                    pool.tensor_tensor(du[par][:, c:c + 2, :], delta[par][:, c:c + 2, :], u[par][:, c:c + 2, :],
                                       ALU.mult).then_inc(pre_pool.did(f"du{c}"), 1)

            def scan(b, par, *stages):
                def times_c(k):
                    pair, c = k // KI, k % KI
                    tile = st[k % RING]
                    if c == 0:
                        pool.wait_ge(bc_loaded[1][pair % 2], 16 * (NP2 // 2) * b + 16 * (pair // 2 + 1))
                    pool.wait_ge(*scan_h.at(k, b))
                    pool.tensor_tensor(tile[:, :, :], tile[:, :, :], bc[1][pair % 2][:, :, :], ALU.mult)\
                        .then_inc(scan_hc.did(k), 1)

                def behind(k):
                    if k >= 1:
                        times_c(k - 1)
                run_slots(stages, (nothing, behind, nothing))
                times_c(NU - 1)
                if isinstance(b, int) and b == 0:
                    pool.wait_ge(setup_dve, 2)
                    pool.wait_ge(zeroed, 16 * xe_zero_v.shape[0])

            def times(name, dst, row, steps=post_pool):
                pool.tensor_tensor(dst[:, :, :], dst[:, :, :], row[:, :].unsqueeze(1).to_broadcast([P, TT, D]),
                                   ALU.mult).then_inc(steps.did(name), 1)

            def plus(name, dst, row, steps=post_pool):
                pool.tensor_tensor(dst[:, :, :], dst[:, :, :], row[:, :].unsqueeze(1).to_broadcast([P, TT, D]),
                                   ALU.add).then_inc(steps.did(name), 1)

            def post(b, par, more):
                yield 19
                pool.wait_ge(*post_dve.at("h_aggr", b))
                scale_and_shift(post_pool, "h", r, shift, mv, EPS, b)
                yield 24
                pool.wait_ge(*post_pe.at("hT", b))
                times("h_g", h, rows["ln0_g"])
                yield 27
                pool.wait_ge(*post_pool.at("h_g", b))
                plus("h_b", h, rows["ln0_b"])
                yield 33
                pool.wait_ge(*post_act.at("q_sq", b))
                power(post_pool, "q", rq, ssq[:, :], EPS * EPS, ALU.max, b)
                pool.wait_ge(*post_dve.at("hi_aggr", b))
                power(post_pool, "hi", r, mv[:, :, 1], EPS, ALU.add, b)
                yield 49
                pool.wait_ge(*post_dve.at("ssg", b))
                power(post_pool, "G", rg, ssg[:, :], EPS * EPS, ALU.max, b)
                power(post_pool, "k", rk, ssk[:, :], EPS * EPS, ALU.max, b)
                yield 53
                plus("h_fl", h, rows["fl_b"])
                yield 60
                pool.wait_ge(*post_dve.at("t", b))
                pool.tensor_tensor(tb[:, :, :], tb[:, :, :], li, ALU.mult).then_inc(post_pool.did("t_li"), 1)
                yield 71
                pool.wait_ge(*post_dve.at("s_aggr", b))
                scale_and_shift(post_pool, "s", r, shift, mv, EPS, b)

            def late(b):
                yield 1
                pool.wait_ge(*post_pe.at("sT", b))
                times("s_g", s, rows["ln1_g"], late_pool)
                yield 4
                pool.wait_ge(*late_pool.at("s_g", b))
                plus("s_b", s, d2_row, late_pool)
                yield 20
                pool.wait_ge(*late_dve.at("f_aggr", b))
                power(late_pool, "f", r_late, mv_late[:, :, 1], EPS, ALU.add, b)
                yield 25
                pool.wait_ge(*late_dve.at("o_aggr", b))
                scale_and_shift(late_pool, "o", r_late, shift_late, mv_late, LN_EPS, b)
                yield 28
                pool.wait_ge(*late_act.at("o_normed", b))
                pool.wait_ge(xr_loaded, 16 * (b + 1))
                pool.tensor_tensor(x_res[:, :, :], x_res[:, :, :], s[:, :, :], ALU.add).then_inc(late_pool.did("x1"), 1)
                yield 31
                pool.wait_ge(*late_dve.at("n_aggr", b))
                scale_and_shift(late_pool, "n", r_late, shift_late, mv_late, LN_EPS, b)
                for n in range(2 * TT):
                    yield 44 + n + (2 if n >= 4 else 0)
                    if n == 0:
                        pool.wait_ge(*late_dve.at("idx", b))
                        pool.sem_inc(carried_pool, 1)
                    tile, choice = divmod(n, 2)
                    pool.indirect_dma_start(
                        out=xe_dram, out_offset=bass.IndirectOffsetOnAxis(ap=idx[:, tile, choice:choice + 1], axis=0),
                        in_=tb[:, tile, :], in_offset=None, bounds_check=NSLOT - 1, oob_is_err=False)\
                        .then_inc(scattered, 16)

            all_sequences(pool, pre, scan, post, late)

        @block.scalar
        def _(act):
            for steps in (pre_act, scan_exp, post_act, late_act):
                steps.credit(act)
            for dst, src in POST_IN:
                with nc.allow_non_contiguous_dma(reason="small per-channel vectors, once"):
                    act.dma_start(dst, src).then_inc(post_weights_in, 16)
            act.wait_ge(zero_tile, 1)
            for a in range(xe_zero_v.shape[0]):
                act.dma_start(xe_zero_v[a], gT_flat).then_inc(zeroed, 16)
            act.wait_ge(consts, 13)
            act.wait_ge(pre_weights_in, 16 * len(PRE_IN))
            act.activation(a_neg[:, :, :], a_neg[:, :, :], ACT.Exp).then_inc(setup_act, 1)
            act.wait_ge(setup_dve, 1)

            def normalise(dst, src, r_t, shift_t):
                for tile in range(TT):
                    last = act.activation(dst[:, tile, :], src[:, tile, :], ACT.Identity,
                                          bias=shift_t[:, tile:tile + 1], scale=r_t[:, tile:tile + 1])
                return last

            def pre(b, par):
                yield 22
                act.wait_ge(*pre_pool.at("x_shift", b))
                normalise(xin, xin, r_pre, shift_pre).then_inc(pre_act.did("x_normed"), 1)
                yield 26
                act.wait_ge(*pre_pe.at("xT", b))
                act.copy(xT[par][:, 0, :], RB[0][:, :])
                act.copy(xT[par][:, 1, :], RB[1][:, :]).then_inc(pre_act.did("xT"), 1)
                for c in range(KI):
                    yield (29, 31, 34, 36)[c]
                    act.wait_ge(*pre_pe.at(f"u{c}", b))
                    if c == 0:
                        act.wait_ge(*post_pe.at("m1", b - 2))
                    act.activation(u[par][:, c, :], RB[c % 2][:, :], ACT.Identity, bias=conv_b[:, c:c + 1],
                                   scale=conv_w[:, c, 3:4]).then_inc(pre_act.did(f"tap{c}"), 1)
                yield 41
                act.wait_ge(*pre_dve.at("conv3_2", b))
                act.activation(u[par][:, :, :], u[par][:, :, :], ACT.Silu).then_inc(pre_act.did("u"), 1)
                for c in range(KI):
                    if c == 2:
                        yield 46
                    act.wait_ge(*pre_pe.at(f"g{c}", b))
                    act.activation(g[par][:, c, :], RB[c % 2][:, :], ACT.Silu).then_inc(pre_act.did(f"g{c}"), 1)
                yield 49
                act.wait_ge(*pre_pe.at("xd", b))
                act.wait_ge(xd_stored, 16 * b)
                act.copy(xd[:, :], RB[0][0:NX, :]).then_inc(pre_act.did("xd"), 1)
                for c in range(KI):
                    yield 52 + c
                    act.wait_ge(*pre_pe.at(f"dt{c}", b))
                    act.activation(delta[par][:, c, :], RB[(c + 1) % 2][:, :], ACT.Identity, bias=dt_b[:, c:c + 1])\
                        .then_inc(pre_act.did(f"z{c}"), 1)
                yield 57
                act.wait_ge(*pre_act.at("z3", b))
                act.activation(du[par][:, :, :], delta[par][:, :, :], ACT.Abs).then_inc(pre_act.did("z_abs"), 1)
                for c, slot in ((0, 58), (2, 60)):
                    yield slot
                    act.wait_ge(*pre_act.at("z_abs", b))
                    act.activation(du[par][:, c:c + 2, :], du[par][:, c:c + 2, :], ACT.Exp, scale=-1.0)\
                        .then_inc(pre_act.did(f"sp_exp{c}"), 1)
                for c, slot in ((0, 63), (2, 71)):
                    yield slot
                    act.wait_ge(*pre_pool.at(f"rest{c}", b))
                    act.activation(du[par][:, c:c + 2, :], du[par][:, c:c + 2, :], ACT.Ln, bias=ones[:, 0:1])\
                        .then_inc(pre_act.did(f"sp_ln{c}"), 1)
                yield 95
                decay(b, par, 0, 0)
                decay(b, par, 0, 1).then_inc(scan_exp.did(0), 1)

            def decay(b, par, k, j):
                pair, c = k // KI, k % KI
                if j == 0:
                    if k == 0:
                        act.wait_ge(*pre_dve.at("delta2", b))
                    act.wait_ge(*(scan_h.at(NU - 2 + k, b - 1) if k < 2 else scan_h.at(k - 2, b)))
                return act.activation(dA[k % 2][:, j, 1:L], delta[par][:, c, 1:L], ACT.Exp,
                                      scale=a_neg[:, c, 2 * pair + j:2 * pair + j + 1])

            def scan(b, par, *stages):
                def first_half(k):
                    if k + 1 < NU:
                        decay(b, par, k + 1, 0)

                def second_half(k):
                    if k + 1 < NU:
                        decay(b, par, k + 1, 1).then_inc(scan_exp.did(k + 1), 1)
                run_slots(stages, (first_half, second_half, nothing))
                if isinstance(b, int) and b == 0:
                    act.wait_ge(post_weights_in, 16 * len(POST_IN))

            def post(b, par, more):
                yield 21
                act.wait_ge(*post_pool.at("h_shift", b))
                normalise(h, h, r, shift).then_inc(post_act.did("h_normed"), 1)
                yield 25
                act.wait_ge(*post_pe.at("hT", b))
                for c in range(KD):
                    last = act.activation(F[:, c, :], PB[c][:, :], ACT.Identity, bias=b0f[:, c:c + 1],
                                          scale=g0f[:, c:c + 1])
                last.then_inc(post_act.did("hT"), 1)
                yield 30
                act.wait_ge(*post_dve.at("q_sum", b))
                for tile in range(TT):
                    last = act.activation(junk_act[:, tile, :], q[:, tile, :], ACT.Square, accum_out=ssq[:, tile:tile + 1])
                last.then_inc(post_act.did("q_sq"), 1)
                yield 33
                act.wait_ge(*post_pe.at("k", b))
                for c in range(KD):
                    last = act.activation(kT[:, c, :], PB[c][:, :], ACT.Identity, bias=k_b[:, c:c + 1])
                last.then_inc(post_act.did("kT"), 1)
                yield 34
                act.wait_ge(*post_act.at("kT", b))
                act.activation(ksq, kT, ACT.Square).then_inc(post_act.did("k_sq"), 1)
                yield 37
                act.wait_ge(*post_pool.at("q_r", b))
                for tile in range(TT):
                    last = act.activation(q[:, tile, :], q[:, tile, :], ACT.Gelu, scale=rq[:, tile:tile + 1])
                last.then_inc(post_act.did("q_gelu"), 1)
                yield 63
                act.wait_ge(*post_pe.at("tT", b))
                act.copy(F[:, 0, :], PB[0][:, :])
                act.copy(F[:, 1, :], PB[1][:, :]).then_inc(post_act.did("tT"), 1)
                yield 73
                act.wait_ge(*post_pool.at("s_shift", b))
                normalise(s, s, r, shift).then_inc(post_act.did("s_normed"), 1)
                yield 77
                act.wait_ge(*post_pe.at("sT", b))
                for c in range(KD):
                    last = act.activation(F[:, c, :], PB[c][:, :], ACT.Identity, bias=b1f[:, c:c + 1],
                                          scale=g1f[:, c:c + 1])
                last.then_inc(post_act.did("sT"), 1)
                for j in range(KF):
                    if j % 4 == 0:
                        yield 84 + 7 * (j // 4)
                    act.wait_ge(*post_pe.at(f"d1_{j}", b))
                    act.activation(gT[:, j, :], FB[j % 4][:, :], ACT.Gelu, bias=d1_b[:, j:j + 1])\
                        .then_inc(post_act.did(f"gelu{j}"), 1)

            def late(b):
                yield 26
                act.wait_ge(*late_pool.at("o_shift", b))
                normalise(s, s, r_late, shift_late).then_inc(late_act.did("o_normed"), 1)
                yield 33
                act.wait_ge(*late_pool.at("n_shift", b))
                normalise(tb, x_res, r_late, shift_late).then_inc(late_act.did("n_normed"), 1)
                yield 36
                act.wait_ge(*late_pe.at("nT", b))
                act.copy(F[:, 0, :], PB[0][:, :])
                act.copy(F[:, 1, :], PB[1][:, :]).then_inc(late_act.did("nT"), 1)
                yield 40
                act.wait_ge(*late_dve.at("dv", b))
                act.activation(e2[:, :], dv[:, :], ACT.Exp).then_inc(late_act.did("e2"), 1)

            all_sequences(act, pre, scan, post, late)

        @block.tensor
        def _(pe):
            for steps in (pre_pe, scan_sum, post_pe, late_pe):
                steps.credit(pe)
            pe.wait_ge(consts, 13)
            pe.wait_ge(pre_weights_in, 16 * len(PRE_IN))

            def turn(src, banks):
                for c in range(KD):
                    for tile in range(TT):
                        last = pe.transpose(banks[c][:, tile * P:(tile + 1) * P], src[:, tile, c * P:(c + 1) * P],
                                            ident[:, :])
                return last

            def token_major(srcT, w, K, tiles=range(TT), banks=PB):
                for tile in tiles:
                    for c in range(K):
                        last = pe.matmul(banks[tile // 2][:, (tile % 2) * D:(tile % 2 + 1) * D],
                                         srcT[:, c, tile * P:(tile + 1) * P], w[:, c, :], start=c == 0, stop=c == K - 1)
                return last

            def pre(b, par):
                yield 24
                pe.wait_ge(*pre_act.at("x_normed", b))
                if not isinstance(b, int) or b >= 2:
                    pe.wait_ge(*post_act.at(f"gelu{KF - 1}", b - 3))
                turn(xin, RB).then_inc(pre_pe.did("xT"), 1)
                for m in range(2 * KI):
                    name = f"u{m}" if m < KI else f"g{m - KI}"
                    yield (27, 29, 32, 34, 37, 39, 42, 44)[m]
                    if m == 0:
                        pe.wait_ge(*pre_act.at("xT", b))
                    elif 2 <= m < KI + 2:
                        pe.wait_ge(*pre_dve.at(f"conv{m - 2}_2", b))
                    elif m >= KI + 2:
                        pe.wait_ge(*pre_act.at(f"g{m - KI - 2}", b))
                    for c in range(KD):
                        last = pe.matmul(RB[m % 2][:, :], in_w[:, c, m * P:(m + 1) * P], xT[par][:, c, :],
                                         start=c == 0, stop=c == KD - 1)
                    last.then_inc(pre_pe.did(name), 1)
                yield 47
                pe.wait_ge(*pre_act.at("g2", b))
                for c in range(KI):
                    last = pe.matmul(RB[0][0:NX, :], xp_w[:, c, :], u[par][:, c, :], start=c == 0, stop=c == KI - 1)
                last.then_inc(pre_pe.did("xd"), 1)
                for c in range(KI):
                    yield 50 + c
                    if c == 0:
                        pe.wait_ge(*pre_act.at("g3", b))
                        pe.wait_ge(*pre_act.at("xd", b))
                    elif c >= 2:
                        pe.wait_ge(*pre_act.at(f"z{c - 2}", b))
                    pe.matmul(RB[(c + 1) % 2][:, :], dt_w[:, c * P:(c + 1) * P], xd[0:R, :], start=True, stop=True)\
                        .then_inc(pre_pe.did(f"dt{c}"), 1)

            def scan(b, par, *stages):
                def add(k):
                    pair, c = k // KI, k % KI
                    if pair == 0:
                        pe.wait_ge(*post_dve.at(f"y_a{c}", b - 1))
                    pe.wait_ge(*scan_add.at(k, b))
                    pe.matmul(Y[c][:, :], ident[:, :], pair_sum[k % SUMS][:, :], start=pair == 0,
                              stop=pair == NP2 - 1).then_inc(scan_sum.did(k), 1)

                run_slots(stages, (nothing, nothing, lambda k: add(k - 3) if k >= 3 else None))
                for k in range(NU - 3, NU):
                    add(k)
                if isinstance(b, int) and b == 0:
                    pe.wait_ge(post_weights_in, 16 * len(POST_IN))

            def post(b, par, more):
                for half in range(2):
                    yield 8 + 2 * half
                    if half == 0:
                        pe.wait_ge(*post_dve.at("y_b3", b))
                        if isinstance(b, int) and b == 0:
                            pe.wait_ge(*pre_act.at("z3", 1))
                    token_major(u[par], out_w, KI, (2 * half, 2 * half + 1), RB).then_inc(post_pe.did(f"m{half}"), 1)
                yield 23
                pe.wait_ge(*post_act.at("h_normed", b))
                pe.wait_ge(*late_dve.at("f_sum1", b - 1))
                turn(h, PB).then_inc(post_pe.did("hT"), 1)
                yield 26
                pe.wait_ge(*post_act.at("hT", b))
                token_major(F, q_w, KD).then_inc(post_pe.did("q"), 1)
                yield 30
                pe.wait_ge(*post_dve.at("q_sum", b))
                for m in range(KD):
                    for c in range(KD):
                        last = pe.matmul(PB[m][:, :], k_w[:, c, m * P:(m + 1) * P], F[:, c, :],
                                         start=c == 0, stop=c == KD - 1)
                last.then_inc(post_pe.did("k"), 1)
                yield 40
                pe.wait_ge(*post_act.at("k_sq", b))
                pe.wait_ge(*late_dve.at("dots", b - 1))
                for tile in range(TT):
                    for c in range(KD):
                        last = pe.matmul(PB[0][:, tile:tile + 1], ksq[:, c, tile * P:(tile + 1) * P], ones[:, 0:1],
                                         start=c == 0, stop=c == KD - 1)
                last.then_inc(post_pe.did("ssk"), 1)
                yield 45
                pe.wait_ge(*post_dve.at("qw2", b))
                pe.wait_ge(*late_dve.at("run", b - 1))
                for c in range(KD):
                    for tile in range(TT):
                        pe.matmul(PB[1][:, c:c + 1], q[:, tile, c * P:(c + 1) * P], qw[:, tile:tile + 1],
                                  start=tile == 0, stop=tile == TT - 1)
                pe.matmul(PB[1][:, 8:8 + TT], ones[:, :], qw2[:, :], start=True, stop=True)\
                    .then_inc(post_pe.did("G"), 1)
                yield 54
                pe.wait_ge(*post_dve.at("proj_g", b))
                token_major(kT, proj_g, KD).then_inc(post_pe.did("hs"), 1)
                yield 61
                pe.wait_ge(*post_pool.at("t_li", b))
                turn(tb, PB).then_inc(post_pe.did("tT"), 1)
                yield 65
                pe.wait_ge(*post_act.at("tT", b))
                token_major(F, fl_w, KD).then_inc(post_pe.did("fl"), 1)
                yield 75
                pe.wait_ge(*post_act.at("s_normed", b))
                turn(s, PB).then_inc(post_pe.did("sT"), 1)
                for j in range(KF):
                    if j % 2 == 0:
                        yield (79, 81, 86, 88)[j // 2]
                    if j == 0:
                        pe.wait_ge(*post_act.at("sT", b))
                    elif j == 2 and more:
                        pe.wait_ge(*pre_act.at("z3", b + 2))
                    elif j >= 4:
                        pe.wait_ge(*post_act.at(f"gelu{j - 4}", b))
                    for c in range(KD):
                        last = pe.matmul(FB[j % 4][:, :], d1_w[:, c, j * P:(j + 1) * P], F[:, c, :],
                                         start=c == 0, stop=c == KD - 1)
                    last.then_inc(post_pe.did(f"d1_{j}"), 1)

            def late(b):
                for tile in range(TT):
                    yield (1, 3, 13, 15)[tile]
                    pe.wait_ge(*post_act.at(f"gelu{KF - 1}", b))
                    token_major(gT, d2_w, KF, (tile,)).then_inc(late_pe.did(f"d2_{tile}"), 1)
                yield 35
                pe.wait_ge(*late_act.at("n_normed", b))
                if not isinstance(b, int) or b < S - 1:
                    pe.wait_ge(*post_act.at("kT", b + 1))
                turn(tb, PB).then_inc(late_pe.did("nT"), 1)
                yield 37
                pe.wait_ge(*late_act.at("nT", b))
                for tile in range(TT):
                    for c in range(KD):
                        last = pe.matmul(PB[0][:, tile * NE:(tile + 1) * NE], F[:, c, tile * P:(tile + 1) * P],
                                         emb[:, c, :], start=c == 0, stop=c == KD - 1)
                last.then_inc(late_pe.did("dots"), 1)
                yield 42
                pe.wait_ge(*late_dve.at("asg", b))
                for tile in range(TT):
                    dst = PB[1][:, tile * NE:(tile + 1) * NE]
                    for before in range(tile):
                        pe.matmul(dst, ones_bf[:, :], asg[:, before, :], start=before == 0, stop=False)
                    pe.matmul(dst, tri[:, :], asg[:, tile, :], start=tile == 0, stop=True)
                for tile in range(TT):
                    last = pe.matmul(PB[1][:, TT * NE:(TT + 1) * NE], ones_bf[:, :], asg[:, tile, :],
                                     start=tile == 0, stop=tile == TT - 1)
                last.then_inc(late_pe.did("cum"), 1)

            all_sequences(pe, pre, scan, post, late)

        @block.vector
        def _(dve):
            dve.memset(gT_flat, 0.0).then_inc(zero_tile, 1)
            for steps in (pre_dve, scan_in, scan_h, scan_add, post_dve, late_dve):
                steps.credit(dve)
            dve.wait_ge(consts, 13)
            dve.wait_ge(pre_weights_in, 16 * len(PRE_IN))
            dve.wait_ge(setup_act, 1)
            dve.tensor_scalar(a_neg[:, :, :], a_neg[:, :, :], -1.0, None, ALU.mult).then_inc(setup_dve, 1)

            def stats(steps, name, src, stat_t, mv_t, b):
                for tile in range(TT):
                    last = dve.bn_stats(stat_t[:, tile, :], src[:, tile, :])
                last.then_inc(steps.did(f"{name}_stats"), 1)
                dve.wait_ge(*steps.at(f"{name}_stats", b))
                dve.sem_inc(carried_dve, 1)
                for tile in range(TT):
                    last = dve.bn_aggr(mv_t[:, tile, :], stat_t[:, tile, :])
                last.then_inc(steps.did(f"{name}_aggr"), 1)

            def pre(b, par):
                yield 19
                dve.wait_ge(x_loaded, 16 * (b + 1))
                stats(pre_dve, "x", xin, stat_pre, mv_pre, b)
                for c in range(KI):
                    yield (30, 32, 35, 37)[c]
                    for j in range(3):
                        if j == 0:
                            dve.wait_ge(*pre_act.at(f"tap{c}", b))
                        else:
                            dve.wait_ge(*pre_dve.at(f"conv{c}_{j - 1}", b))
                        late = u[par][:, c, j + 1:L]
                        dve.scalar_tensor_tensor(late, RB[c % 2][:, 0:L - 1 - j], conv_w[:, c, 2 - j:3 - j], late,
                                                 ALU.mult, ALU.add).then_inc(pre_dve.did(f"conv{c}_{j}"), 1)
                for c, slot in ((0, 60), (2, 68)):
                    yield slot
                    if c == 0:
                        dve.wait_ge(*pre_act.at("sp_exp0", b))
                    else:
                        dve.wait_ge(*pre_pool.at("log1p0", b))
                        dve.wait_ge(*pre_act.at("sp_exp2", b))
                    dve.tensor_scalar(rest[:, :, :], du[par][:, c:c + 2, :], 1.0, 1.0, ALU.add, ALU.subtract)\
                        .then_inc(pre_dve.did(f"w{c}"), 1)
                for c, slot in ((0, 67), (2, 76)):
                    yield slot
                    dve.wait_ge(*pre_pool.at(f"log1p{c}", b))
                    dve.scalar_tensor_tensor(delta[par][:, c:c + 2, :], delta[par][:, c:c + 2, :], 0.0,
                                             du[par][:, c:c + 2, :], ALU.max, ALU.add)\
                        .then_inc(pre_dve.did(f"delta{c}"), 1)
                yield 95
                drive(b, par, 0)

            def drive(b, par, k):
                pair, c = k // KI, k % KI
                if k == 0:
                    dve.wait_ge(*pre_pool.at("du2", b))
                if c == 0:
                    dve.wait_ge(bc_loaded[0][pair % 2], 16 * (NP2 // 2) * b + 16 * (pair // 2 + 1))
                dve.wait_ge(*(scan_add.at(NU - RING + k, b - 1) if k < RING else scan_add.at(k - RING, b)))
                dve.tensor_tensor(st[k % RING][:, :, :], du[par][:, c, :].unsqueeze(1).to_broadcast([P, 2, L]),
                                  bc[0][pair % 2][:, :, :], ALU.mult).then_inc(scan_in.did(k), 1)

            def scan(b, par, *stages):
                def ahead(k):
                    if k + 1 < NU:
                        drive(b, par, k + 1)

                def add_up(k):
                    dve.wait_ge(*scan_hc.at(k, b))
                    dve.wait_ge(*(scan_sum.at(k - SUMS, b) if k >= SUMS else scan_sum.at(NU + k - SUMS, b - 1)))
                    dve.tensor_tensor(pair_sum[k % SUMS][:, :], st[k % RING][:, 0, :], st[k % RING][:, 1, :],
                                      ALU.add).then_inc(scan_add.did(k), 1)

                def behind(k):
                    if k >= 3:
                        add_up(k - 3)

                def recur(k):
                    dve.wait_ge(*scan_exp.at(k, b))
                    dve.wait_ge(*scan_in.at(k, b))
                    flat = st[k % RING][:, :, :].rearrange("p a l -> p (a l)")
                    dve.tensor_tensor_scan(flat, dA[k % 2][:, :, :].rearrange("p a l -> p (a l)"), flat, 0.0,
                                           ALU.mult, ALU.add).then_inc(scan_h.did(k), 1)
                run_slots(stages, (behind, recur, ahead))
                for k in range(NU - 3, NU):
                    add_up(k)
                if isinstance(b, int) and b == 0:
                    dve.wait_ge(post_weights_in, 16 * len(POST_IN))
                    dve.wait_ge(zeroed, 16 * xe_zero_v.shape[0])
                    dve.tensor_tensor(d2_row[:, :], d2_row[:, :], s[:, 0, :], ALU.add).then_inc(setup_dve, 1)

            def own(name, b):
                return post_dve.at(name, b)

            def affine(steps, first, second, dst, src, mv_t, r_t, g_row, b_row, b):
                for tile in range(TT):
                    last = dve.scalar_tensor_tensor(dst[:, tile, :], src[:, tile, :], mv_t[:, tile, 0:1], g_row[:, :],
                                                    ALU.subtract, ALU.mult)
                last.then_inc(steps.did(first), 1)
                dve.wait_ge(*steps.at(first, b))
                for tile in range(TT):
                    last = dve.scalar_tensor_tensor(dst[:, tile, :], dst[:, tile, :], r_t[:, tile:tile + 1], b_row[:, :],
                                                    ALU.mult, ALU.add)
                last.then_inc(steps.did(second), 1)

            def post(b, par, more):
                for c0 in (0, 2):
                    yield 3 + c0
                    for c in (c0, c0 + 1):
                        dve.wait_ge(*scan_sum.at(NU - KI + c, b))
                        dve.scalar_tensor_tensor(u[par][:, c, :], u[par][:, c, :], d_skip[:, c:c + 1], Y[c][:, :],
                                                 ALU.mult, ALU.add).then_inc(post_dve.did(f"y_a{c}"), 1)
                    for c in (c0, c0 + 1):
                        dve.wait_ge(*own(f"y_a{c}", b))
                        dve.tensor_tensor(u[par][:, c, :], u[par][:, c, :], g[par][:, c, :], ALU.mult)\
                            .then_inc(post_dve.did(f"y_b{c}"), 1)
                yield 16
                dve.wait_ge(*post_pe.at("m1", b))
                dve.wait_ge(xn_loaded, 16 * (b + 1))
                for i in range(2):
                    last = dve.tensor_tensor(h[:, 2 * i:2 * i + 2, :], RB[i][:, :].rearrange("p (a d) -> p a d", a=2),
                                             h[:, 2 * i:2 * i + 2, :], ALU.add)
                last.then_inc(post_dve.did("h_sum"), 1)
                yield 17
                dve.wait_ge(*own("h_sum", b))
                stats(post_dve, "h", h, stat, mv, b)
                yield 29
                dve.wait_ge(*post_pe.at("q", b))
                for i in range(2):
                    last = dve.tensor_tensor(q[:, 2 * i:2 * i + 2, :], PB[i][:, :].rearrange("p (a d) -> p a d", a=2),
                                             rows["q_b"][:, :].unsqueeze(1).to_broadcast([P, 2, D]), ALU.add)
                last.then_inc(post_dve.did("q_sum"), 1)
                yield 31
                dve.wait_ge(*post_pool.at("h_b", b))
                stats(post_dve, "hi", h, stat, mv, b)
                yield 35
                dve.wait_ge(*post_pool.at("hi_r", b))
                affine(post_dve, "li_g", "li", li, h, mv, r, rows["lni_g"], rows["lni_b"], b)
                yield 41
                dve.wait_ge(*post_act.at("q_gelu", b))
                dve.wait_ge(*post_pe.at("ssk", b))
                for tile in range(TT):
                    last = dve.tensor_tensor_reduce(out=junk_dve[:, tile, :], in0=q[:, tile, :], in1=rows["w_g"][:, :],
                                                    scale=D ** -0.5, scalar=0.0, op0=ALU.mult, op1=ALU.add,
                                                    accum_out=qw[:, tile:tile + 1])
                last.then_inc(post_dve.did("qw"), 1)
                dve.wait_ge(*own("qw", b))
                dve.tensor_tensor(qw2[:, :], qw[:, :], qw[:, :], ALU.mult).then_inc(post_dve.did("qw2"), 1)
                dve.tensor_copy(ssk[:, :], PB[0][:, 0:TT]).then_inc(post_dve.did("ssk"), 1)
                yield 47
                dve.wait_ge(*post_pe.at("G", b))
                dve.tensor_reduce(ssg[:, :], PB[1][:, 8:8 + TT], AX_X, ALU.add).then_inc(post_dve.did("ssg"), 1)
                yield 52
                dve.wait_ge(*post_pool.at("G_r", b))
                dve.tensor_scalar(gcol[:, :], PB[1][:, 0:KD], rg[:, 0:1], None, ALU.mult)\
                    .then_inc(post_dve.did("G"), 1)
                dve.wait_ge(*own("G", b))
                for c in range(KD):
                    last = dve.tensor_scalar(proj_g[:, c, :], pr_w[:, c, :], gcol[:, c:c + 1], None, ALU.mult)
                last.then_inc(post_dve.did("proj_g"), 1)
                yield 59
                dve.wait_ge(*post_pe.at("hs", b))
                dve.wait_ge(*post_pool.at("k_r", b))
                dve.wait_ge(*sp_sent.at("sent", b - 1))
                for tile in range(TT):
                    last = dve.scalar_tensor_tensor(tb[:, tile, :], PB[tile // 2][:, (tile % 2) * D:(tile % 2 + 1) * D],
                                                    rk[:, tile:tile + 1], rows["pr_b"][:, :], ALU.mult, ALU.add)
                last.then_inc(post_dve.did("t"), 1)
                yield 69
                dve.wait_ge(*post_pe.at("fl", b))
                dve.wait_ge(*post_pool.at("h_fl", b))
                for i in range(2):
                    last = dve.tensor_tensor(s[:, 2 * i:2 * i + 2, :], PB[i][:, :].rearrange("p (a d) -> p a d", a=2),
                                             h[:, 2 * i:2 * i + 2, :], ALU.add)
                last.then_inc(post_dve.did("s_sum"), 1)
                dve.wait_ge(*own("s_sum", b))
                stats(post_dve, "s", s, stat, mv, b)

            def late(b):
                for i in range(2):
                    yield 7 + 11 * i
                    dve.wait_ge(*late_pe.at(f"d2_{2 * i + 1}", b))
                    if i == 0:
                        dve.wait_ge(*late_pool.at("s_b", b))
                    part_s = s[:, 2 * i:2 * i + 2, :]
                    dve.tensor_tensor(part_s, PB[i][:, :].rearrange("p (a d) -> p a d", a=2), part_s, ALU.add)\
                        .then_inc(late_dve.did(f"f_sum{i}"), 1)
                dve.wait_ge(*late_dve.at("f_sum1", b))
                stats(late_dve, "f", s, stat_late, mv_late, b)
                yield 21
                dve.wait_ge(*late_pool.at("f_r", b))
                affine(late_dve, "f_g", "f_normed", s, s, mv_late, r_late, rows["ln2_g"], rows["ln2_b"], b)
                yield 23
                dve.wait_ge(*late_dve.at("f_normed", b))
                stats(late_dve, "o", s, stat_late, mv_late, b)
                yield 30
                dve.wait_ge(*late_pool.at("x1", b))
                stats(late_dve, "n", x_res, stat_late, mv_late, b)
                yield 39
                dve.wait_ge(*late_pe.at("dots", b))
                dve.tensor_copy(dots[:, :, :], PB[0][:, 0:TT * NE].rearrange("p (t e) -> p t e", t=TT))\
                    .then_inc(late_dve.did("dots"), 1)
                dve.wait_ge(*late_dve.at("dots", b))
                dve.sem_inc(carried_dve, 1)
                for tile in range(TT):
                    last = dve.max(top[:, tile, :], dots[:, tile, :])
                last.then_inc(late_dve.did("top"), 1)
                dve.wait_ge(*late_dve.at("top", b))
                dve.sem_inc(carried_dve, 1)
                for tile in range(TT):
                    last = dve.max_index(top_i[:, tile, :], top[:, tile, :], dots[:, tile, :])
                last.then_inc(late_dve.did("top_i"), 1)
                dve.tensor_tensor(dv[:, :], top[:, :, 1], top[:, :, 0], ALU.subtract).then_inc(late_dve.did("dv"), 1)
                dve.wait_ge(*late_dve.at("top_i", b))
                dve.tensor_copy(top_f[:, :, :], top_i[:, :, 0:2]).then_inc(late_dve.did("top_f"), 1)
                yield 41
                dve.wait_ge(*late_act.at("e2", b))
                dve.tensor_scalar(den[:, :], e2[:, :], 1.0, None, ALU.add).then_inc(late_dve.did("den"), 1)
                dve.wait_ge(*late_dve.at("den", b))
                dve.reciprocal(wts[:, :, 0], den[:, :]).then_inc(late_dve.did("w1"), 1)
                dve.wait_ge(*late_dve.at("w1", b))
                dve.tensor_tensor(wts[:, :, 1], e2[:, :], wts[:, :, 0], ALU.mult).then_inc(late_dve.did("w2"), 1)
                dve.wait_ge(*late_dve.at("w2", b))
                dve.tensor_scalar(pos2[:, :], wts[:, :, 1], 0.0, None, ALU.is_gt).then_inc(late_dve.did("pos2"), 1)
                for i in range(2):
                    dve.tensor_tensor(oh[i][:, :, :], iota8[:, :].unsqueeze(1).to_broadcast([P, TT, NE]),
                                      top_f[:, :, i:i + 1].to_broadcast([P, TT, NE]), ALU.is_equal)\
                        .then_inc(late_dve.did(f"oh{i}"), 1)
                dve.wait_ge(*late_dve.at("oh1", b))
                dve.tensor_tensor(oh[1][:, :, :], oh[1][:, :, :], pos2[:, :].unsqueeze(2).to_broadcast([P, TT, NE]),
                                  ALU.mult).then_inc(late_dve.did("oh1_pos"), 1)
                dve.wait_ge(*late_dve.at("oh1_pos", b))
                dve.tensor_tensor(asg[:, :, :], oh[0][:, :, :], oh[1][:, :, :], ALU.add)\
                    .then_inc(late_dve.did("asg"), 1)
                dve.tensor_copy(w_all[:, bass.ds(b * TT, TT), :], wts[:, :, :]).then_inc(late_dve.did("w_all"), 1)
                yield 44
                dve.wait_ge(*late_pe.at("cum", b))
                dve.tensor_tensor(cum[:, :, :], PB[1][:, 0:TT * NE].rearrange("p (t e) -> p t e", t=TT),
                                  run[:, :].unsqueeze(1).to_broadcast([P, TT, NE]), ALU.add)\
                    .then_inc(late_dve.did("cum"), 1)
                dve.wait_ge(*late_dve.at("cum", b))
                dve.tensor_scalar(keep[:, :, :], cum[:, :, :], float(CAP), None, ALU.is_le)\
                    .then_inc(late_dve.did("keep"), 1)
                dve.tensor_tensor(run[:, :], PB[1][:, TT * NE:(TT + 1) * NE], run[:, :], ALU.add)\
                    .then_inc(late_dve.did("run"), 1)
                dve.tensor_tensor(cum[:, :, :], cum[:, :, :], slot0[:, :].unsqueeze(1).to_broadcast([P, TT, NE]),
                                  ALU.add).then_inc(late_dve.did("slotv"), 1)
                dve.wait_ge(*late_dve.at("slotv", b))
                dve.tensor_tensor(cum[:, :, :], cum[:, :, :], keep[:, :, :], ALU.mult)\
                    .then_inc(late_dve.did("slotk"), 1)
                dve.wait_ge(*late_dve.at("slotk", b))
                for i in range(2):
                    dve.tensor_tensor(pick[i][:, :, :], cum[:, :, :], oh[i][:, :, :], ALU.mult)\
                        .then_inc(late_dve.did(f"pick{i}"), 1)
                for i in range(2):
                    dve.wait_ge(*late_dve.at(f"pick{i}", b))
                    dve.tensor_reduce(slot_f[:, :, i], pick[i][:, :, :], AX_X, ALU.add)\
                        .then_inc(late_dve.did(f"slot{i}"), 1)
                dve.wait_ge(*late_dve.at("slot1", b))
                dve.tensor_scalar(idx[:, :, :], slot_f[:, :, :], FAR, None, ALU.add).then_inc(late_dve.did("idx"), 1)
                dve.wait_ge(*late_dve.at("idx", b))
                dve.tensor_copy(idx_all[:, bass.ds(b * TT, TT), :], idx[:, :, :]).then_inc(late_dve.did("idx_all"), 1)

            all_sequences(dve, pre, scan, post, late)


def expert_phase(nc, t, env, sem):
    D, NE, EI, KD, KE, CAP, TB, QB, BLK = (env[k] for k in ("D", "NE", "EI", "KD", "KE", "CAP", "TB", "QB", "BLK"))
    ident, bank, xe_v, ye_v = (env[k] for k in ("ident", "bank", "xe_v", "ye_v"))
    NB = 2 * QB
    with ExitStack() as ctx:
        def sb(name, shape, dt=F32):
            return ctx.enter_context(nc.sbuf_tensor(name, shape, dt))

        w1 = [sb(f"w1_{i}", [P, KD, EI]) for i in range(2)]
        w2 = [sb(f"w2_{i}", [P, KE, D]) for i in range(2)]
        X = [sb(f"X{i}", [P, TB, D]) for i in range(2)]
        XT = [sb(f"XT{i}", [P, KD, BLK]) for i in range(2)]
        I = [sb(f"I{i}", [P, KE, BLK]) for i in range(2)]
        O = [sb(f"O{i}", [P, TB, D]) for i in range(2)]
        XB, MB, OB = bank[0:2], bank[2:6], bank[6:8]

        carried_sp_e = sem("carried_sp_e")
        w_loaded = [sem(f"w_loaded{i}") for i in range(2)]
        slots_loaded = [sem(f"slots_loaded{i}") for i in range(2)]
        stored = [sem(f"stored{i}") for i in range(2)]
        e_turn = Steps(sem("e_turn"), range(NB))
        e_turned = Steps(sem("e_turned"), range(NB))
        e_mm1 = Steps(sem("e_mm1"), range(NB * KE))
        e_relu_act = Steps(sem("e_relu_act"), range(NB * KE // 2))
        e_relu_dve = Steps(sem("e_relu_dve"), range(NB * KE // 2))
        e_mm2 = Steps(sem("e_mm2"), range(NB))
        e_out = Steps(sem("e_out"), range(NB))

        def before(steps, n, back, i):
            return steps.at(n - back, i) if n >= back else steps.at(len(steps.names) + n - back, i - 1)

        block = ctx.enter_context(nc.Block())

        @block.sync
        def _(sp):
            with sp.Fori(0, NE // 2) as i:
                for n in range(NB):
                    e, q = divmod(n, QB)
                    if q == 0:
                        sp.wait_ge(*e_mm2.at(n + QB - 1, i - 1))
                        sp.sem_inc(carried_sp_e, 1)
                        sp.dma_start(w1[e][:, :, :], t["e1_w"][2 * i + e].rearrange("(k p) n -> p k n", p=P))\
                            .then_inc(w_loaded[e], 16)
                        sp.dma_start(w2[e][:, :, :], t["e2_w"][2 * i + e].rearrange("(k p) n -> p k n", p=P))\
                            .then_inc(w_loaded[e], 16)
                    sp.wait_ge(*before(e_turn, n, 2, i))
                    sp.sem_inc(carried_sp_e, 1)
                    sp.dma_start(X[n % 2][:, :, :], xe_v[i * NB + n]).then_inc(slots_loaded[n % 2], 16)

        @block.tensor
        def _(pe):
            for steps in (e_turn, e_mm1, e_mm2):
                steps.credit(pe)

            def turn(n, i):
                pe.wait_ge(slots_loaded[n % 2], 16 * (NB // 2) * i + 16 * (n // 2 + 1))
                pe.wait_ge(*before(e_turned, n, 1, i))
                for c in range(KD):
                    for tile in range(TB):
                        last = pe.transpose(XB[c][:, tile * P:(tile + 1) * P], X[n % 2][:, tile, c * P:(c + 1) * P],
                                            ident[:, :])
                last.then_inc(e_turn.did(n), 1)

            with pe.Fori(0, NE // 2) as i:
                turn(0, i)
                for n in range(NB):
                    e = n // QB
                    if n % QB == 0:
                        pe.wait_ge(w_loaded[e], 32 * (i + 1))
                    pe.wait_ge(*e_turned.at(n, i))
                    for m in range(KE):
                        relu = e_relu_act if m % 2 == 0 else e_relu_dve
                        pe.wait_ge(*before(relu, n * KE // 2 + m // 2, KE // 2, i))
                        for c in range(KD):
                            last = pe.matmul(MB[m][:, 0:BLK], w1[e][:, c, m * P:(m + 1) * P], XT[n % 2][:, c, :],
                                             start=c == 0, stop=c == KD - 1)
                        last.then_inc(e_mm1.did(n * KE + m), 1)
                    if n + 1 < NB:
                        turn(n + 1, i)
                    pe.wait_ge(*e_relu_act.at(n * KE // 2 + KE // 2 - 1, i))
                    pe.wait_ge(*e_relu_dve.at(n * KE // 2 + KE // 2 - 1, i))
                    pe.wait_ge(*before(e_out, n, 1, i))
                    for tile in range(TB):
                        for c in range(KE):
                            last = pe.matmul(OB[tile // 2][:, (tile % 2) * D:(tile % 2 + 1) * D],
                                             I[n % 2][:, c, tile * P:(tile + 1) * P], w2[e][:, c, :],
                                             start=c == 0, stop=c == KE - 1)
                    last.then_inc(e_mm2.did(n), 1)

        @block.scalar
        def _(act):
            for steps in (e_turned, e_relu_act):
                steps.credit(act)
            for half in range(2):
                act.sem_inc(stored[half], 16)
            with act.Fori(0, NE // 2) as i:
                def copy_turned(n):
                    act.wait_ge(*e_turn.at(n, i))
                    act.wait_ge(*before(e_mm1, n * KE + KE - 1, 2 * KE, i))
                    for c in range(KD):
                        last = act.copy(XT[n % 2][:, c, :], XB[c][:, 0:BLK])
                    last.then_inc(e_turned.did(n), 1)

                copy_turned(0)
                for n in range(NB):
                    act.wait_ge(*before(e_mm2, n, 2, i))
                    for m in range(0, KE, 2):
                        act.wait_ge(*e_mm1.at(n * KE + m, i))
                        act.activation(I[n % 2][:, m, :], MB[m][:, 0:BLK], ACT.Relu)\
                            .then_inc(e_relu_act.did(n * KE // 2 + m // 2), 1)
                    if n + 1 < NB:
                        copy_turned(n + 1)
                    act.wait_ge(*e_out.at(n, i))
                    act.dma_start(ye_v[i * NB + n], O[n % 2][:, :, :]).then_inc(stored[n % 2], 16)
            for half in range(2):
                act.wait_ge(stored[half], 16 * (NE // 2) * (NB // 2) + 16)

        @block.vector
        def _(dve):
            for steps in (e_relu_dve, e_out):
                steps.credit(dve)
            with dve.Fori(0, NE // 2) as i:
                for n in range(NB):
                    dve.wait_ge(*before(e_mm2, n, 2, i))
                    for m in range(1, KE, 2):
                        dve.wait_ge(*e_mm1.at(n * KE + m, i))
                        dve.tensor_scalar(I[n % 2][:, m, :], MB[m][:, 0:BLK], 0.0, None, ALU.max)\
                            .then_inc(e_relu_dve.did(n * KE // 2 + m // 2), 1)
                    dve.wait_ge(*e_mm2.at(n, i))
                    dve.wait_ge(stored[n % 2], 16 * (NB // 2) * i + 16 * (n // 2 + 1))
                    for tile in range(0, TB, 2):
                        last = dve.tensor_copy(O[n % 2][:, tile:tile + 2, :],
                                               OB[tile // 2][:, :].rearrange("p (a d) -> p a d", a=2))
                    last.then_inc(e_out.did(n), 1)


def combine_phase(nc, t, env, sem):
    S, D, TT, NSLOT = (env[k] for k in ("S", "D", "TT", "NSLOT"))
    idx_all, w_all, eps5, ye_dram, x1_v, out_v = (
        env[k] for k in ("idx_all", "w_all", "eps5", "ye_dram", "x1_v", "out_v"))
    with ExitStack() as ctx:
        def sb(name, shape, dt=F32):
            return ctx.enter_context(nc.sbuf_tensor(name, shape, dt))

        G = 4
        rows = [[sb(f"rows{i}_{c}", [P, TT, D]) for c in range(2)] for i in range(G)]
        idx_c = [sb(f"idx_c{i}", [P, TT, 2], U32) for i in range(G)]
        w_c = [sb(f"w_c{i}", [P, TT, 2]) for i in range(G)]
        x1 = [sb(f"x1_{i}", [P, TT, D]) for i in range(G)]
        stat = [sb(f"c_stat{i}", [P, TT, 6]) for i in range(G)]
        mv = [sb(f"c_mv{i}", [P, TT, 2]) for i in range(G)]
        r = [sb(f"c_r{i}", [P, TT]) for i in range(G)]
        shift = [sb(f"c_shift{i}", [P, TT]) for i in range(G)]

        gathered = [sem(f"gathered{n}") for n in range(G)]
        gathers_begun = sem("gathers_begun")
        carried = sem("carried")
        carried_sp_c = sem("carried_sp_c")
        x1_loaded = [sem(f"x1_loaded{n}") for n in range(G)]
        out_stored = [sem(f"out_stored{n}") for n in range(G)]
        ready = Steps(sem("c_ready"), range(G))
        c_sum = Steps(sem("c_sum"), [f"{name}{n}" for n in range(G) for name in ("sum", "stats", "aggr")])
        c_shift = Steps(sem("c_shift"), range(G))
        c_out = Steps(sem("c_out"), range(G))
        c_scaled = Steps(sem("c_scaled"), range(G))
        c_r = Steps(sem("c_r"), [f"{name}{n}" for n in range(G) for name in ("ln", "r")])
        c_normed = Steps(sem("c_normed"), range(G))

        def turns(engine, parts):
            for n in range(G):
                for back, part in parts:
                    if n >= back:
                        part(n - back, 0)
            with engine.Fori(0, S // G - 1) as j:
                for n in range(G):
                    for back, part in parts:
                        part((n - back) % G, j + 1 if n >= back else j)
            for n in range(G, G + max(back for back, _ in parts)):
                for back, part in parts:
                    if 0 <= n - back < G:
                        part(n - back, S // G - 1)

        block = ctx.enter_context(nc.Block())

        @block.sync
        def _(sp):
            for n in range(G):
                sp.sem_inc(out_stored[n], 16)

            def load(n, i):
                sp.wait_ge(out_stored[n], 16 * (i + 1))
                sp.sem_inc(carried_sp_c, 1)
                sp.dma_start(x1[n][:, :, :], x1_v[G * i + n]).then_inc(x1_loaded[n], 16)

            def store(n, i):
                sp.wait_ge(*c_out.at(n, i))
                sp.sem_inc(carried_sp_c, 1)
                sp.dma_start(out_v[G * i + n], x1[n][:, :, :]).then_inc(out_stored[n], 16)

            turns(sp, ((3, store), (0, load)))
            for n in range(G):
                sp.wait_ge(out_stored[n], 16 * (S // G + 1))

        @block.gpsimd
        def _(pool):
            with pool.Fori(0, S // G) as i:
                for n in range(G):
                    pool.wait_ge(*ready.at(n, i))
                    pool.sem_inc(gathers_begun, 1)
                    for tile in range(TT):
                        for c in range(2):
                            pool.indirect_dma_start(
                                out=rows[n][c][:, tile, :], out_offset=None, in_=ye_dram,
                                in_offset=bass.IndirectOffsetOnAxis(ap=idx_c[n][:, tile, c:c + 1], axis=0),
                                bounds_check=NSLOT - 1, oob_is_err=False).then_inc(gathered[n], 16)

        @block.scalar
        def _(act):
            for steps in (c_scaled, c_r, c_normed):
                steps.credit(act)

            def scaled(n, i):
                act.wait_ge(gathered[n], 16 * 2 * TT * (i + 1))
                act.wait_ge(*ready.at(n, i))
                for tile in range(TT):
                    last = act.activation(rows[n][0][:, tile, :], rows[n][0][:, tile, :], ACT.Copy,
                                          scale=w_c[n][:, tile, 0:1])
                last.then_inc(c_scaled.did(n), 1)

            def power(n, i):
                act.wait_ge(*c_sum.at(f"aggr{n}", i))
                act.activation(r[n][:, :], mv[n][:, :, 1], ACT.Ln, bias=eps5[:, 0:1]).then_inc(c_r.did(f"ln{n}"), 1)
                act.wait_ge(*c_r.at(f"ln{n}", i))
                act.activation(r[n][:, :], r[n][:, :], ACT.Exp, scale=-0.5).then_inc(c_r.did(f"r{n}"), 1)

            def normalise(n, i):
                act.wait_ge(*c_shift.at(n, i))
                for tile in range(TT):
                    last = act.activation(rows[n][0][:, tile, :], rows[n][0][:, tile, :], ACT.Identity,
                                          bias=shift[n][:, tile:tile + 1], scale=r[n][:, tile:tile + 1])
                last.then_inc(c_normed.did(n), 1)

            turns(act, ((2, normalise), (0, scaled), (1, power)))

        @block.vector
        def _(dve):
            for steps in (ready, c_sum, c_shift, c_out):
                steps.credit(dve)

            def prepare(n, i):
                dve.wait_ge(*c_out.at(n, i - 1))
                for c in range(2):
                    dve.memset(rows[n][c][:, :, :], 0.0)
                dve.tensor_copy(w_c[n][:, :, :], w_all[:, bass.ds((G * i + n) * TT, TT), :])
                dve.tensor_copy(idx_c[n][:, :, :], idx_all[:, bass.ds((G * i + n) * TT, TT), :])\
                    .then_inc(ready.did(n), 1)

            def both(n, i):
                a, b = rows[n]
                dve.wait_ge(*c_scaled.at(n, i))
                dve.wait_ge(gathered[n], 16 * 2 * TT * (i + 1))
                for tile in range(TT):
                    last = dve.scalar_tensor_tensor(a[:, tile, :], b[:, tile, :], w_c[n][:, tile, 1:2],
                                                    a[:, tile, :], ALU.mult, ALU.add)
                last.then_inc(c_sum.did(f"sum{n}"), 1)
                dve.wait_ge(*c_sum.at(f"sum{n}", i))
                for tile in range(TT):
                    last = dve.bn_stats(stat[n][:, tile, :], a[:, tile, :])
                last.then_inc(c_sum.did(f"stats{n}"), 1)
                dve.wait_ge(*c_sum.at(f"stats{n}", i))
                dve.sem_inc(carried, 1)
                for tile in range(TT):
                    last = dve.bn_aggr(mv[n][:, tile, :], stat[n][:, tile, :])
                last.then_inc(c_sum.did(f"aggr{n}"), 1)

            def shifted(n, i):
                dve.wait_ge(*c_r.at(f"r{n}", i))
                dve.scalar_tensor_tensor(shift[n][:, :], mv[n][:, :, 0], -1.0, r[n][:, :], ALU.mult, ALU.mult)\
                    .then_inc(c_shift.did(n), 1)

            def add(n, i):
                dve.wait_ge(*c_normed.at(n, i))
                dve.wait_ge(x1_loaded[n], 16 * (i + 1))
                dve.tensor_tensor(x1[n][:, :, :], x1[n][:, :, :], rows[n][0][:, :, :], ALU.add)\
                    .then_inc(c_out.did(n), 1)

            turns(dve, ((4, add), (0, prepare), (2, both), (3, shifted)))


def kernel(**inputs):
    import numpy as _np
    import concourse.bacc as _bacc
    from concourse import mybir as _mybir
    from concourse.bass_utils import run_bass_kernel_spmd as _run

    def a(name):
        return _np.asarray(inputs[f"L0_attn_{name}"])

    def f(name):
        return _np.asarray(inputs[f"L0_ffn_{name}"])

    host = {"x": a("input_tensor"), "in_w": a("in_proj_w").T, "conv_w": a("conv_w"), "conv_b": a("conv_b"),
            "xp_w": a("x_proj_w").T, "dt_w": a("dt_proj_w").T, "dt_b": a("dt_proj_b"), "A_log": a("A_log"),
            "D_skip": a("D_skip"), "out_w": a("out_proj_w").T, "ln0_g": a("ln0_g"), "ln0_b": a("ln0_b"),
            "q_w": a("q_w").T, "q_b": a("q_b"), "k_w": a("k_w").T, "k_b": a("k_b"), "w_g": a("w_g").reshape(-1),
            "pr_w": a("proj_w").T, "pr_b": a("proj_b"), "fl_w": a("fl_w").T, "fl_b": a("fl_b"),
            "lni_g": a("lni_g"), "lni_b": a("lni_b"), "ln1_g": a("ln1_g"), "ln1_b": a("ln1_b"),
            "d1_w": a("d1_w").T, "d1_b": a("d1_b"), "d2_w": a("d2_w").T, "d2_b": a("d2_b"),
            "ln2_g": a("ln2_g"), "ln2_b": a("ln2_b"), "emb": f("expert_embeddings").T,
            "e1_w": f("first_linear").transpose(0, 2, 1), "e2_w": f("second_linear").transpose(0, 2, 1)}
    nc = _bacc.Bacc("TRN2", target_bir_lowering=False, num_devices=1)
    arrays, t = {}, {}
    for name, value in host.items():
        value = _np.ascontiguousarray(value)
        arrays[f"in_{name}"] = value
        t[name] = nc.dram_tensor(f"in_{name}", value.shape, _mybir.dt.from_np(value.dtype), kind="ExternalInput").ap()
    t["out"] = nc.dram_tensor("out_0", host["x"].shape, _mybir.dt.float32, kind="ExternalOutput").ap()
    build(nc, t)
    result = _run(nc, [arrays], core_ids=[0])
    return result.results[0]["out_0"]
```
